# Optimizing a Trainium2 kernel written in Bass

```python
import numpy as np
import jax
import jax.numpy as jnp

def _softmax(x, axis=-1):
    return jax.nn.softmax(x, axis=axis)

def _gelu(x):
    return jax.nn.gelu(x, approximate=True)

def _silu(x):
    return jax.nn.silu(x)

def _sigmoid(x):
    return jax.nn.sigmoid(x)

def _layernorm(x, axis=-1, eps=1e-05):
    m = jnp.mean(x, axis=axis, keepdims=True)
    v = jnp.var(x, axis=axis, keepdims=True)
    return (x - m) / jnp.sqrt(v + eps)

def _scatter_add(tgt, idx, src, axis=0):
    return tgt.at[idx].add(src)

def _segment_sum(src, seg, n):
    return jax.ops.segment_sum(src, seg, n)
kernel_name = 'mk_decoder_preln_d1_seqx_r4_2c1977'

def setup_inputs(seed: int=0):
    np.random.seed(seed)
    _w = jnp.asarray

    def _rec_inputs():
        import jax
        import jax.numpy as jnp
        _rk = jax.random.key(seed)
        x = -0.0002928 + 1 * jax.random.normal(jax.random.fold_in(_rk, 1), (4, 1024, 256), jnp.float32)
        _lenS = 1024 - jax.random.randint(jax.random.fold_in(_rk, 7), (4,), 0, max(1, 1024 // 4) + 1, jnp.int32)
        _lenS2 = 64 - jax.random.randint(jax.random.fold_in(_rk, 8), (4,), 0, max(1, 64 // 4) + 1, jnp.int32)
        _ctx_1024P = jax.random.normal(jax.random.fold_in(_rk, 11), (4, 16, 256), jnp.float32)
        _ctx_1024c = jax.random.dirichlet(jax.random.fold_in(_rk, 511), 0.3 * jnp.ones((16,), jnp.float32), (4, 64))
        _ctx_1024t = jnp.einsum('bsk,bkd->bsd', _ctx_1024c, _ctx_1024P)
        _ctx_1024t = _ctx_1024t * jax.lax.rsqrt(jnp.mean(jnp.square(_ctx_1024t)) + 1e-12) * 0.953939
        ctx_1024 = -1.39393e-06 + 0.999914 * (_ctx_1024t + 0.3 * jax.random.normal(jax.random.fold_in(_rk, 611), (4, 64, 256), jnp.float32))
        _validS = jnp.arange(1024)[None, :] < _lenS[:, None]
        _validS2 = jnp.arange(64)[None, :] < _lenS2[:, None]
        _causal = jnp.tril(jnp.ones((1024, 1024), dtype=bool))
        mask_Bx1x1xS2_ik0 = jnp.where(jnp.broadcast_to(_validS2[:, None, None, :], (4, 1, 1, 64)), 0, 1).astype(jnp.int32)
        mask_1x1xSxS2_ik0 = jnp.where(jnp.broadcast_to(_validS2[0:1, None, None, :], (1, 1, 1024, 64)), 0, 1).astype(jnp.int32)
        return (x, ctx_1024, mask_Bx1x1xS2_ik0, mask_1x1xSxS2_ik0)
    x, ctx_1024, mask_Bx1x1xS2_ik0, mask_1x1xSxS2_ik0 = _rec_inputs()

    def _L0_attn_setup():
        import jax, jax.numpy as jnp
        import numpy as np
        import math
        B, L, D = (2, 1024, 256)
        H, DK, DV = (4, 64, 64)
        CS = 32
        CONV = 4
        FIR_S, FIR_L = (3, 31)
        GIN = D + 3 * DV
        GH = D * 2 // 2
        MIN_LOCAL = 0.05

        def dwconv(x, w):
            k = w.shape[-1]
            xf = jnp.pad(jnp.swapaxes(x, 1, 2), ((0, 0), (0, 0), (k - 1, 0)))
            y = jax.lax.conv_general_dilated(xf, w[:, None, :], (1,), 'VALID', dimension_numbers=('NCH', 'OIH', 'NCH'), feature_group_count=w.shape[0])
            return jnp.swapaxes(y, 1, 2)

        def l2n(x):
            return x * jax.lax.rsqrt(jnp.sum(x * x, -1, keepdims=True) + 1e-12)

        def delta_rule(q, k, v, beta):
            b, h, Lq, dk = q.shape
            dv = v.shape[-1]
            n = Lq // CS
            q, k = (l2n(q), l2n(k))
            v = v * beta[..., None]
            kb = k * beta[..., None]
            rs = lambda t: t.reshape(b, h, n, CS, t.shape[-1])
            q, k, v, kb = (rs(q), rs(k), rs(v), rs(kb))
            strict_lo = jnp.tril(jnp.ones((CS, CS), bool), -1)
            A = jnp.where(strict_lo, kb @ jnp.swapaxes(k, -1, -2), 0.0)
            eye = jnp.eye(CS, dtype=q.dtype)
            Tinv = jax.scipy.linalg.solve_triangular(eye + A, jnp.broadcast_to(eye, A.shape), lower=True, unit_diagonal=True)
            u = Tinv @ v
            w = Tinv @ kb
            strict_up = jnp.triu(jnp.ones((CS, CS), bool), 1)

            def step(S, xs):
                q_i, k_i, u_i, w_i = xs
                attn = jnp.where(strict_up, 0.0, q_i @ jnp.swapaxes(k_i, -1, -2))
                u_i = u_i - w_i @ S
                o_i = q_i @ S + attn @ u_i
                S = S + jnp.swapaxes(k_i, -1, -2) @ u_i
                return (S, o_i)
            mv = lambda t: jnp.moveaxis(t, 2, 0)
            S0 = jnp.zeros((b, h, dk, dv), q.dtype)
            _, out = jax.lax.scan(step, S0, (mv(q), mv(k), mv(u), mv(w)))
            return jnp.moveaxis(out, 0, 2).reshape(b, h, Lq, dv)

        def _forward(hidden_states, q_proj_w, k_proj_w, v_proj_w, b_proj_w, q_conv_w, k_conv_w, v_conv_w, fir_short_w, fir_long_w, fg_w1, fg_b1, fg_w2, fg_b2, logit_temp, o_norm_w, o_proj_w):
            b, l, _ = hidden_states.shape
            hs = hidden_states
            q = jax.nn.silu(dwconv(hs @ q_proj_w.T, q_conv_w)).reshape(b, l, H, DK)
            k = jax.nn.silu(dwconv(hs @ k_proj_w.T, k_conv_w)).reshape(b, l, H, DK)
            v = jax.nn.silu(dwconv(hs @ v_proj_w.T, v_conv_w)).reshape(b, l, H, DV)
            beta = jax.nn.sigmoid(hs @ b_proj_w.T)
            tr = lambda t: jnp.swapaxes(t, 1, 2)
            delta = tr(delta_rule(tr(q), tr(k), tr(v), jnp.swapaxes(beta, 1, 2)))
            fir = lambda x, w: dwconv(x.reshape(b, l, H * DV), w.reshape(H * DV, -1)).reshape(b, l, H, DV)
            short = fir(v, fir_short_w)
            long_ = fir(v, fir_long_w)
            gate_in = jnp.concatenate([hs, short.mean(2), long_.mean(2), delta.mean(2)], -1)
            logits = jax.nn.gelu(gate_in @ fg_w1.T + fg_b1, approximate=False) @ fg_w2.T + fg_b2
            temp = jax.nn.softplus(logit_temp) + 0.0001
            wgt = jax.nn.softmax(logits / temp, -1)[:, :, None, :]
            wgt = jnp.broadcast_to(wgt, (b, l, H, 4))
            floor = MIN_LOCAL * wgt[..., 3:4]
            wloc = jnp.maximum(wgt[..., :2], floor)
            wgt = jnp.concatenate([wloc, wgt[..., 2:]], -1)
            wgt = wgt / wgt.sum(-1, keepdims=True)
            o = wgt[..., 0:1] * short + wgt[..., 1:2] * long_ + wgt[..., 2:3] * delta + wgt[..., 3:4] * v
            o = o * jax.lax.rsqrt(jnp.mean(o * o, -1, keepdims=True) + 1e-05) * o_norm_w
            return o.reshape(b, l, H * DV) @ o_proj_w.T
        key = jax.random.key(seed)
        ks = jax.random.split(key, 12)
        s = 0.02
        return {'hidden_states': jax.random.normal(ks[0], (B, L, D), jnp.float32), 'q_proj_w': jax.random.normal(ks[1], (H * DK, D), jnp.float32) * s, 'k_proj_w': jax.random.normal(ks[2], (H * DK, D), jnp.float32) * s, 'v_proj_w': jax.random.normal(ks[3], (H * DV, D), jnp.float32) * s, 'b_proj_w': jax.random.normal(ks[4], (H, D), jnp.float32) * s, 'q_conv_w': jax.random.normal(ks[5], (H * DK, CONV), jnp.float32) * s, 'k_conv_w': jax.random.normal(ks[6], (H * DK, CONV), jnp.float32) * s, 'v_conv_w': jax.random.normal(ks[7], (H * DV, CONV), jnp.float32) * s, 'fir_short_w': jnp.zeros((H, DV, FIR_S), jnp.float32).at[..., -1].set(1.0), 'fir_long_w': jnp.zeros((H, DV, FIR_L), jnp.float32).at[..., -1].set(1.0), 'fg_w1': jax.random.normal(ks[8], (GH, GIN), jnp.float32) * s, 'fg_b1': jnp.zeros((GH,), jnp.float32), 'fg_w2': jax.random.normal(ks[9], (4, GH), jnp.float32) * s, 'fg_b2': jnp.array([-0.2, -0.2, 1.0, 3.0], jnp.float32), 'logit_temp': jnp.full((1,), math.log(math.expm1(0.7)), jnp.float32), 'o_norm_w': jnp.ones((DV,), jnp.float32), 'o_proj_w': jax.random.normal(ks[10], (D, H * DV), jnp.float32) * s}
    _L0_attn_all = _L0_attn_setup()
    _L0_attn_in = {k: v for k, v in _L0_attn_all.items() if k in ('q_proj_w', 'k_proj_w', 'v_proj_w', 'b_proj_w', 'q_conv_w', 'k_conv_w', 'v_conv_w', 'fir_short_w', 'fir_long_w', 'fg_w1', 'fg_b1', 'fg_w2', 'fg_b2', 'logit_temp', 'o_norm_w', 'o_proj_w')}
    del _L0_attn_all

    def _L0_xattn_setup():
        import jax, jax.numpy as jnp
        import numpy as np
        E, H = (256, 16)
        N, S, T = (2, 512, 512)
        key = jax.random.key(seed)
        ks = jax.random.split(key, 8)
        scale = 1.0 / np.sqrt(E)
        q = jax.random.normal(ks[0], (N, S, E), dtype=jnp.float32)
        k = jax.random.normal(ks[1], (N, T, E), dtype=jnp.float32)
        v = jax.random.normal(ks[2], (N, T, E), dtype=jnp.float32)
        pad_mask = jax.random.randint(ks[3], (N, 1, 1, T), 0, 2, dtype=jnp.int32)
        subsq_mask = jnp.tril(jnp.ones((S, T), dtype=jnp.int32))[None, None]
        Wq = jax.random.normal(ks[4], (E, E), dtype=jnp.float32) * scale
        Wk = jax.random.normal(ks[5], (E, E), dtype=jnp.float32) * scale
        Wv = jax.random.normal(ks[6], (E, E), dtype=jnp.float32) * scale
        bq = jnp.zeros((E,), dtype=jnp.float32)
        bk = jnp.zeros((E,), dtype=jnp.float32)
        bv = jnp.zeros((E,), dtype=jnp.float32)
        return {'query': q, 'key': k, 'value': v, 'pad_mask': pad_mask, 'subsq_mask': subsq_mask, 'Wq': Wq, 'bq': bq, 'Wk': Wk, 'bk': bk, 'Wv': Wv, 'bv': bv}
    _L0_xattn_all = _L0_xattn_setup()
    _L0_xattn_in = {k: v for k, v in _L0_xattn_all.items() if k in ('Wq', 'bq', 'Wk', 'bk', 'Wv', 'bv')}
    del _L0_xattn_all

    def _L0_ffn_setup():
        import jax, jax.numpy as jnp
        import numpy as np
        H = 256
        I = 128
        E = 8
        K = 2
        SI = I * 2
        B, S = (2, 256)

        def _mlp(x, gw, uw, dw):
            return jax.nn.silu(x @ gw.T) * (x @ uw.T) @ dw.T
        key = jax.random.key(seed)
        ks = jax.random.split(key, 9)
        s = 0.02
        return {'x': jax.random.normal(ks[0], (B, S, H), jnp.float32), 'gate_w': jax.random.normal(ks[1], (E, H), jnp.float32) * s, 'lb_bias': jnp.zeros((E,), jnp.float32), 'expert_gate_w': jax.random.normal(ks[2], (E, I, H), jnp.float32) * s, 'expert_up_w': jax.random.normal(ks[3], (E, I, H), jnp.float32) * s, 'expert_down_w': jax.random.normal(ks[4], (E, H, I), jnp.float32) * s, 'shared_gate_w': jax.random.normal(ks[5], (SI, H), jnp.float32) * s, 'shared_up_w': jax.random.normal(ks[6], (SI, H), jnp.float32) * s, 'shared_down_w': jax.random.normal(ks[7], (H, SI), jnp.float32) * s}
    _L0_ffn_all = _L0_ffn_setup()
    _L0_ffn_in = {k: v for k, v in _L0_ffn_all.items() if k in ('gate_w', 'lb_bias', 'expert_gate_w', 'expert_up_w', 'expert_down_w', 'shared_gate_w', 'shared_up_w', 'shared_down_w')}
    del _L0_ffn_all
    return {'x': x, 'ctx_1024': ctx_1024, 'mask_Bx1x1xS2_ik0': mask_Bx1x1xS2_ik0, 'mask_1x1xSxS2_ik0': mask_1x1xSxS2_ik0, 'L0_attn_q_proj_w': _L0_attn_in['q_proj_w'], 'L0_attn_k_proj_w': _L0_attn_in['k_proj_w'], 'L0_attn_v_proj_w': _L0_attn_in['v_proj_w'], 'L0_attn_b_proj_w': _L0_attn_in['b_proj_w'], 'L0_attn_q_conv_w': _L0_attn_in['q_conv_w'], 'L0_attn_k_conv_w': _L0_attn_in['k_conv_w'], 'L0_attn_v_conv_w': _L0_attn_in['v_conv_w'], 'L0_attn_fir_short_w': _L0_attn_in['fir_short_w'], 'L0_attn_fir_long_w': _L0_attn_in['fir_long_w'], 'L0_attn_fg_w1': _L0_attn_in['fg_w1'], 'L0_attn_fg_b1': _L0_attn_in['fg_b1'], 'L0_attn_fg_w2': _L0_attn_in['fg_w2'], 'L0_attn_fg_b2': _L0_attn_in['fg_b2'], 'L0_attn_logit_temp': _L0_attn_in['logit_temp'], 'L0_attn_o_norm_w': _L0_attn_in['o_norm_w'], 'L0_attn_o_proj_w': _L0_attn_in['o_proj_w'], 'L0_xattn_Wq': _L0_xattn_in['Wq'], 'L0_xattn_bq': _L0_xattn_in['bq'], 'L0_xattn_Wk': _L0_xattn_in['Wk'], 'L0_xattn_bk': _L0_xattn_in['bk'], 'L0_xattn_Wv': _L0_xattn_in['Wv'], 'L0_xattn_bv': _L0_xattn_in['bv'], 'L0_ffn_gate_w': _L0_ffn_in['gate_w'], 'L0_ffn_lb_bias': _L0_ffn_in['lb_bias'], 'L0_ffn_expert_gate_w': _L0_ffn_in['expert_gate_w'], 'L0_ffn_expert_up_w': _L0_ffn_in['expert_up_w'], 'L0_ffn_expert_down_w': _L0_ffn_in['expert_down_w'], 'L0_ffn_shared_gate_w': _L0_ffn_in['shared_gate_w'], 'L0_ffn_shared_up_w': _L0_ffn_in['shared_up_w'], 'L0_ffn_shared_down_w': _L0_ffn_in['shared_down_w']}

def reference(x, ctx_1024, mask_Bx1x1xS2_ik0, mask_1x1xSxS2_ik0, L0_attn_q_proj_w, L0_attn_k_proj_w, L0_attn_v_proj_w, L0_attn_b_proj_w, L0_attn_q_conv_w, L0_attn_k_conv_w, L0_attn_v_conv_w, L0_attn_fir_short_w, L0_attn_fir_long_w, L0_attn_fg_w1, L0_attn_fg_b1, L0_attn_fg_w2, L0_attn_fg_b2, L0_attn_logit_temp, L0_attn_o_norm_w, L0_attn_o_proj_w, L0_xattn_Wq, L0_xattn_bq, L0_xattn_Wk, L0_xattn_bk, L0_xattn_Wv, L0_xattn_bv, L0_ffn_gate_w, L0_ffn_lb_bias, L0_ffn_expert_gate_w, L0_ffn_expert_up_w, L0_ffn_expert_down_w, L0_ffn_shared_gate_w, L0_ffn_shared_up_w, L0_ffn_shared_down_w):
    import jax
    import jax.numpy as jnp

    def _L0_attn_ref(hidden_states, q_proj_w, k_proj_w, v_proj_w, b_proj_w, q_conv_w, k_conv_w, v_conv_w, fir_short_w, fir_long_w, fg_w1, fg_b1, fg_w2, fg_b2, logit_temp, o_norm_w, o_proj_w):
        import jax, jax.numpy as jnp
        import numpy as np
        import math
        B, L, D = (2, 1024, 256)
        H, DK, DV = (4, 64, 64)
        CS = 32
        CONV = 4
        FIR_S, FIR_L = (3, 31)
        GIN = D + 3 * DV
        GH = D * 2 // 2
        MIN_LOCAL = 0.05

        def dwconv(x, w):
            k = w.shape[-1]
            xf = jnp.pad(jnp.swapaxes(x, 1, 2), ((0, 0), (0, 0), (k - 1, 0)))
            y = jax.lax.conv_general_dilated(xf, w[:, None, :], (1,), 'VALID', dimension_numbers=('NCH', 'OIH', 'NCH'), feature_group_count=w.shape[0])
            return jnp.swapaxes(y, 1, 2)

        def l2n(x):
            return x * jax.lax.rsqrt(jnp.sum(x * x, -1, keepdims=True) + 1e-12)

        def delta_rule(q, k, v, beta):
            b, h, Lq, dk = q.shape
            dv = v.shape[-1]
            n = Lq // CS
            q, k = (l2n(q), l2n(k))
            v = v * beta[..., None]
            kb = k * beta[..., None]
            rs = lambda t: t.reshape(b, h, n, CS, t.shape[-1])
            q, k, v, kb = (rs(q), rs(k), rs(v), rs(kb))
            strict_lo = jnp.tril(jnp.ones((CS, CS), bool), -1)
            A = jnp.where(strict_lo, kb @ jnp.swapaxes(k, -1, -2), 0.0)
            eye = jnp.eye(CS, dtype=q.dtype)
            Tinv = jax.scipy.linalg.solve_triangular(eye + A, jnp.broadcast_to(eye, A.shape), lower=True, unit_diagonal=True)
            u = Tinv @ v
            w = Tinv @ kb
            strict_up = jnp.triu(jnp.ones((CS, CS), bool), 1)

            def step(S, xs):
                q_i, k_i, u_i, w_i = xs
                attn = jnp.where(strict_up, 0.0, q_i @ jnp.swapaxes(k_i, -1, -2))
                u_i = u_i - w_i @ S
                o_i = q_i @ S + attn @ u_i
                S = S + jnp.swapaxes(k_i, -1, -2) @ u_i
                return (S, o_i)
            mv = lambda t: jnp.moveaxis(t, 2, 0)
            S0 = jnp.zeros((b, h, dk, dv), q.dtype)
            _, out = jax.lax.scan(step, S0, (mv(q), mv(k), mv(u), mv(w)))
            return jnp.moveaxis(out, 0, 2).reshape(b, h, Lq, dv)

        def _forward(hidden_states, q_proj_w, k_proj_w, v_proj_w, b_proj_w, q_conv_w, k_conv_w, v_conv_w, fir_short_w, fir_long_w, fg_w1, fg_b1, fg_w2, fg_b2, logit_temp, o_norm_w, o_proj_w):
            b, l, _ = hidden_states.shape
            hs = hidden_states
            q = jax.nn.silu(dwconv(hs @ q_proj_w.T, q_conv_w)).reshape(b, l, H, DK)
            k = jax.nn.silu(dwconv(hs @ k_proj_w.T, k_conv_w)).reshape(b, l, H, DK)
            v = jax.nn.silu(dwconv(hs @ v_proj_w.T, v_conv_w)).reshape(b, l, H, DV)
            beta = jax.nn.sigmoid(hs @ b_proj_w.T)
            tr = lambda t: jnp.swapaxes(t, 1, 2)
            delta = tr(delta_rule(tr(q), tr(k), tr(v), jnp.swapaxes(beta, 1, 2)))
            fir = lambda x, w: dwconv(x.reshape(b, l, H * DV), w.reshape(H * DV, -1)).reshape(b, l, H, DV)
            short = fir(v, fir_short_w)
            long_ = fir(v, fir_long_w)
            gate_in = jnp.concatenate([hs, short.mean(2), long_.mean(2), delta.mean(2)], -1)
            logits = jax.nn.gelu(gate_in @ fg_w1.T + fg_b1, approximate=False) @ fg_w2.T + fg_b2
            temp = jax.nn.softplus(logit_temp) + 0.0001
            wgt = jax.nn.softmax(logits / temp, -1)[:, :, None, :]
            wgt = jnp.broadcast_to(wgt, (b, l, H, 4))
            floor = MIN_LOCAL * wgt[..., 3:4]
            wloc = jnp.maximum(wgt[..., :2], floor)
            wgt = jnp.concatenate([wloc, wgt[..., 2:]], -1)
            wgt = wgt / wgt.sum(-1, keepdims=True)
            o = wgt[..., 0:1] * short + wgt[..., 1:2] * long_ + wgt[..., 2:3] * delta + wgt[..., 3:4] * v
            o = o * jax.lax.rsqrt(jnp.mean(o * o, -1, keepdims=True) + 1e-05) * o_norm_w
            return o.reshape(b, l, H * DV) @ o_proj_w.T
        return _forward(hidden_states, q_proj_w, k_proj_w, v_proj_w, b_proj_w, q_conv_w, k_conv_w, v_conv_w, fir_short_w, fir_long_w, fg_w1, fg_b1, fg_w2, fg_b2, logit_temp, o_norm_w, o_proj_w)

    def _L0_xattn_ref(query, key, value, pad_mask, subsq_mask, Wq, bq, Wk, bk, Wv, bv):
        import jax, jax.numpy as jnp
        import numpy as np
        E, H = (256, 16)
        N, S, T = (2, 512, 512)
        n, s, e = query.shape
        t = value.shape[1]
        d = e // H
        q = (query @ Wq.T + bq).reshape(n, s, H, d).transpose(0, 2, 1, 3)
        k = (key @ Wk.T + bk).reshape(n, t, H, d).transpose(0, 2, 1, 3)
        v = (value @ Wv.T + bv).reshape(n, t, H, d).transpose(0, 2, 1, 3)
        att = jnp.einsum('bhsd,bhtd->bhst', q, k) / jnp.sqrt(jnp.float32(d))
        att = jnp.where(pad_mask == 0, jnp.float32(-1000000000.0), att)
        att = jnp.where(subsq_mask == 0, jnp.float32(-1000000000.0), att)
        prob = jax.nn.softmax(att, axis=-1)
        out = jnp.einsum('bhst,bhtd->bhsd', prob, v)
        return out.transpose(0, 2, 1, 3).reshape(n, s, e)

    def _L0_ffn_ref(x, gate_w, lb_bias, expert_gate_w, expert_up_w, expert_down_w, shared_gate_w, shared_up_w, shared_down_w):
        import jax, jax.numpy as jnp
        import numpy as np
        H = 256
        I = 128
        E = 8
        K = 2
        SI = I * 2
        B, S = (2, 256)

        def _mlp(x, gw, uw, dw):
            return jax.nn.silu(x @ gw.T) * (x @ uw.T) @ dw.T
        b, s, h = x.shape
        xf = x.reshape(-1, h)
        logits = xf @ gate_w.T + lb_bias
        scores = jax.nn.sigmoid(logits.astype(jnp.float32))
        topw, topi = jax.lax.top_k(scores, K)
        topw = (topw / (topw.sum(-1, keepdims=True) + 1e-08)).astype(x.dtype)
        out = jnp.zeros_like(xf)
        for e in range(E):
            m = topi == e
            sel = m.any(axis=-1)
            cnt = m.sum()
            wmean = (topw * m).sum() / jnp.maximum(cnt, 1).astype(topw.dtype)
            y = _mlp(xf, expert_gate_w[e], expert_up_w[e], expert_down_w[e])
            out = out + jnp.where(sel[:, None], y * wmean, jnp.zeros((), x.dtype))
        out = out.reshape(b, s, h)
        out = out + _mlp(x, shared_gate_w, shared_up_w, shared_down_w)
        return out
    x = x + _L0_attn_ref(_layernorm(x, axis=-1), L0_attn_q_proj_w, L0_attn_k_proj_w, L0_attn_v_proj_w, L0_attn_b_proj_w, L0_attn_q_conv_w, L0_attn_k_conv_w, L0_attn_v_conv_w, L0_attn_fir_short_w, L0_attn_fir_long_w, L0_attn_fg_w1, L0_attn_fg_b1, L0_attn_fg_w2, L0_attn_fg_b2, L0_attn_logit_temp, L0_attn_o_norm_w, L0_attn_o_proj_w)
    x = x + _L0_xattn_ref(_layernorm(x, axis=-1), ctx_1024, ctx_1024, mask_Bx1x1xS2_ik0, mask_1x1xSxS2_ik0, L0_xattn_Wq, L0_xattn_bq, L0_xattn_Wk, L0_xattn_bk, L0_xattn_Wv, L0_xattn_bv)
    x = x + _L0_ffn_ref(_layernorm(x, axis=-1), L0_ffn_gate_w, L0_ffn_lb_bias, L0_ffn_expert_gate_w, L0_ffn_expert_up_w, L0_ffn_expert_down_w, L0_ffn_shared_gate_w, L0_ffn_shared_up_w, L0_ffn_shared_down_w)
    return x

_drawn_inputs = setup_inputs


def setup_inputs(seed=0):
    import zlib

    import numpy as np

    out = dict(_drawn_inputs(seed))
    spreads = {'L0_attn_fg_b1': (0.0, 2.0),
     'L0_attn_o_norm_w': (1.0, 0.2),
     'L0_xattn_bq': (0.0, 0.287),
     'L0_xattn_bk': (0.0, 2.0),
     'L0_xattn_bv': (0.0, 0.1),
     'L0_ffn_lb_bias': (0.0, 0.8)}
    factors = {'L0_attn_q_proj_w': 22.765,
     'L0_attn_k_proj_w': 22.061,
     'L0_attn_b_proj_w': 42.526,
     'L0_attn_q_conv_w': 21.021,
     'L0_attn_k_conv_w': 23.047,
     'L0_attn_fir_short_w': 6.59,
     'L0_attn_fir_long_w': 6.563,
     'L0_attn_fg_w1': 8.0,
     'L0_attn_fg_w2': 8.0,
     'L0_attn_fg_b2': 8.0,
     'L0_ffn_gate_w': 8.0,
     'L0_ffn_expert_gate_w': 8.0,
     'L0_ffn_expert_up_w': 8.0,
     'L0_ffn_expert_down_w': 8.0,
     'L0_ffn_shared_gate_w': 4.188,
     'L0_ffn_shared_up_w': 4.102,
     'L0_ffn_shared_down_w': 4.133}
    for name, (base, spread) in spreads.items():
        noise = np.random.default_rng([zlib.crc32(name.encode()), seed]).standard_normal(out[name].shape)
        drawn = base * np.exp(spread * noise) if base else spread * noise
        out[name] = jnp.asarray(drawn.astype(out[name].dtype))
    for name, factor in factors.items():
        out[name] = (out[name] * factor).astype(out[name].dtype)
    return out
```

```python
from contextlib import ExitStack

import numpy as np

import concourse.bass as bass
from concourse import mybir

ALU = mybir.AluOpType
ACT = mybir.ActivationFunctionType
AX = mybir.AxisListType
F32 = mybir.dt.float32
BF16 = mybir.dt.bfloat16
I32 = mybir.dt.int32

P = 128
B, L, D = 4, 1024, 256
G = 2
GT = L // G
T = GT // P
H, DH = 4, 64
HT = T * H
CK = D // P
CONV, FS, FL = 4, 3, 31
HALO = FL - 1
XH, XD, S2 = 16, 16, 64
NPAIR = XH // 2
E, EI = 8, 128
ES = 10
NEG = -1.0e9
MIN_LOCAL = 0.05
LEVELS = (1, 2, 4, 8, 16, 32, 64)


def columns(spec):
    at, out = 0, {}
    for name, width in spec:
        out[name] = (at, at + width)
        at += width
    return out, at


CONST, NCONST = columns([("ident", P), ("lower", P), ("upper", P)] + [(f"level{s}", P) for s in LEVELS]
                        + [("eye64", DH), ("headsel", 2), ("mean_s", P), ("mean_l", P), ("ones", P),
                           ("head16", 8), ("eye32", 32), ("before", E * E)])
PARAM, NPARAM = columns([("conv", 6 * CONV), ("fir_s", CK * FS), ("fir_l", CK * FL), ("fg_b1", CK),
                         ("bq", CK), ("bk", CK), ("bv", D), ("fg_b2", 4), ("lb", E), ("temp", 1), ("onorm", 1)])
WEIGHT, NWEIGHT = columns([("k", CK * D), ("q", CK * D), ("v", CK * D), ("beta", CK * H), ("fg1", 4 * D),
                           ("fg2", CK * 4), ("o", CK * D), ("xq", CK * D), ("xk", CK * D), ("xv", CK * D),
                           ("route", CK * E)])


def psum_plan():
    plan = []

    def ring(names, banks=range(8)):
        for i, n in enumerate(names):
            plan.append((n, banks[i % len(banks)]))

    for g in range(G):
        names = ["hsT0", "hsT1"] + [f"proj{j}" for j in range(6)] + ["stat"]
        names += [f"kv{t}" for t in range(T)]
        ring([f"{n}.{g}" for n in names])
        ring([f"gram{t}{i}.{g}" for t in range(T) for i in range(2)])
        names = ["P1"]
        for s in LEVELS[1:5]:
            names += [f"P{s}", f"D{s}"]
        names += ["P32a", "P32b", "R32a", "R32b", "T32a", "T32b", "P64a", "P64b", "R64a", "R64b"]
        names += [f"uw{t}" for t in range(T)] + [f"wa{t}" for t in range(T)]
        for t in range(T):
            names += [f"state{t}", f"out{t}0", f"out{t}1"]
        names += ["gm", "dmT", "h1a", "h1b", "logit"] + [f"sl{t}" for t in range(T)]
        names += ["oT0", "oT1", "oproj0", "oproj1"]
        if g == 0:
            names += ["kx", "vx"]
        names += ["any", "x1T0", "x1T1", "qx0", "qx1"]
        names += [f"sx{t}{c}" for t in range(T) for c in range(CK)]
        names += ["mxT"]
        ring([f"{n}.{g}" for n in names])
        ring([f"sT{j}.{g}" for j in range(NPAIR)], range(4))
        ring([f"pv{t}.{g}" for t in range(T)], range(4, 8))
        ring([f"{n}.{g}" for n in ("x2T0", "x2T1", "route")])
    bank = dict(plan)
    seen = [0] * 8
    index = {}
    for n, k in plan:
        index[n] = seen[k]
        seen[k] += 1
    return bank, index, seen


SIGNALS = {
    "x_loaded": 32, "ctx_loaded": 16 * 3, "stats_ready": 6 * 1, "rstd_ready": 6 * 1, "xn_ready": 6 * 1,
    "conv_ready": 12, "act_ready": 12, "squares_ready": 2, "rnorm_ready": 2, "scale_ready": 2,
    "fir_done": 4, "level_ready": 14, "level_used": 14, "rows_ready": 16, "compact_ready": 10,
    "blocks_ready": 10, "blocks_cleared": 4, "delta_ready": 8, "exp_ready": 2, "gate_ready": 4, "mix_ready": 2,
    "osq_ready": 2, "oms_ready": 2, "orms_ready": 2, "on_ready": 2, "mask_ready": 2, "kblk_ready": 1,
    "nmx_ready": 2, "pv_used": 14, "x2_ready": 2, "x2_stored": 64,
}


def decoder(nc, x, ctxT, pad_row, pad_col, sub, subT, const_d, param_d, weight_d, ffn_d, out, x2_d, xnT_d):
    bank_of, fill_index, fills_per_batch = psum_plan()
    es = ExitStack()
    with es:
        def sb(name, shape, dt=F32):
            return es.enter_context(nc.sbuf_tensor(name, shape, dt))

        sems = {}

        def sem(name):
            if name not in sems:
                sems[name] = es.enter_context(nc.semaphore(name))
            return sems[name]

        banks = [es.enter_context(nc.psum_tensor(f"bank{i}", [P, 512], F32)) for i in range(8)]
        filled = [sem(f"bank{i}_filled") for i in range(8)]
        drained = [sem(f"bank{i}_drained") for i in range(8)]

        const = sb("const", [P, NCONST])
        param = sb("param", [P, NPARAM])
        wt = sb("wt", [P, NWEIGHT])

        def cst(n, rows=slice(0, P)):
            return const[rows, CONST[n][0]:CONST[n][1]]

        def prm(n, i=0, w=None):
            a = PARAM[n][0] + i
            return param[:, a:(a + w) if w else PARAM[n][1]]

        def wgt(n, c, width):
            a = WEIGHT[n][0] + c * width
            return wt[:, a:a + width]

        ident_b = sb("ident_b", [P, P], BF16)
        ones_b = sb("ones_b", [P, P], BF16)
        aug_lhs = sb("aug_lhs", [P, NPAIR, P], BF16)
        minus_half = sb("minus_half", [P, 16])
        eps = sb("eps", [P, 2, 8])
        rtemp = sb("rtemp", [P, 8])
        wo_n = sb("wo_n", [P, CK, D])

        xt = sb("xt", [P, T, D])
        xn = sb("xn", [P, T, D])
        stats = sb("stats", [P, T, 6])
        spare = sb("spare", [P, 1])
        mv = sb("mv", [P, T, 2])
        rstd = sb("rstd", [P, T])
        hsT = sb("hsT", [P, CK, GT])
        pre = sb("pre", [P, 6, CONV - 1 + GT])
        cv = sb("cv", [P, 2, GT])
        kq = sb("kq", [P, 2, 2, GT])
        vT = sb("vT", [P, CK, HALO + GT])
        lng = sb("lng", [P, CK, GT])
        sht = sb("sht", [P, CK, GT])
        st = sb("st", [P, T, 12])
        rn = sb("rn", [P, T, 8])
        beta = sb("beta", [P, T, H])
        rb = sb("rb", [P, T, H])
        sc = sb("sc", [P, T, H])
        kvt = sb("kvt", [P, T, 512])
        Y = sb("Y", [P, HT, P])
        A = sb("A", [P, HT, P])
        attnT = sb("attnT", [P, HT, P])
        Bl = sb("Bl", [P, 2, HT, P])
        sq = Bl[:, 1, :, :].rearrange("p (a c) d -> p a (c d)", a=4)
        Tf = sb("Tf", [P, HT, P])
        Rf = sb("Rf", [P, HT, P])
        Rc = sb("Rc", [P, HT, 32])
        Tc = sb("Tc", [P, HT, 32])
        Pc = sb("Pc", [P, HT, 32])
        UW = sb("UW", [P, HT, P])
        Pf = UW
        QeT = sb("QeT", [P, T, 2, P])
        MT = sb("MT", [P, T, 2, DH])
        S = sb("S", [P, 2, 2, DH])
        delta = sb("delta", [P, T, D])
        gmT = sb("gmT", [P, GT])
        dm = sb("dm", [P, T, DH])
        dmT = sb("dmT", [DH, GT])
        h1T = sb("h1T", [P, CK, GT])
        gw = sb("gw", [P, 8, T, 4])
        gs = sb("gs", [P, 4, T])
        om = sb("om", [P, T, D])
        oss = sb("oss", [P, HT])
        orn = sb("orn", [P, HT])
        osq = cv[:, :, :].rearrange("p a b -> p (a b)").rearrange("p (t d) -> p t d", t=T)
        xnT = A[:, 0:8, :].rearrange("p (c a) b -> p c (a b)", c=CK)
        qx = A[:, 8:16, :].rearrange("p (c a) b -> p c (a b)", c=CK)
        PT = attnT[:, :, :].rearrange("p (s a) b -> p s (a b)", s=4)
        abc = h1T[:, 0, :]
        Kblk = sb("Kblk", [P, CK, 8, S2])
        kxT = sb("kxT", [P, CK, S2])
        Va = sb("Va", [P, NPAIR, 34])
        ctx = sb("ctx", [P, CK, P])
        padr = sb("padr", [P, S2], I32)
        padc = sb("padc", [S2, 1], I32)
        subi = sb("subi", [P, L // P, S2], I32)
        subTi = sb("subTi", [S2, L], I32)
        sub01 = sb("sub01", [P, L // P, S2], BF16)
        subT01 = sb("subT01", [S2, L], BF16)
        pr01 = sb("pr01", [P, S2])
        pc01 = sb("pc01", [S2, 1])
        mbf = sb("mbf", [P, L // P, S2], BF16)
        mb = sb("mb", [P, L // P, S2], BF16)
        mT = sb("mT", [S2, GT], BF16)
        aug = sb("aug", [P, GT], BF16)
        nmx = sb("nmx", [P, 2, T, XH])
        nmb = sb("nmb", [P, T, 3 * XH], BF16)
        rden = sb("rden", [P, T, NPAIR, 2])
        xo = sb("xo", [P, D])
        route = sb("route", [P, B * G * T, E])

        plus = (lambda b, per, k: b * per + k)
        PRIMED = {"kblk_ready": 1, "blocks_cleared": 1, "x2_stored": 16}
        counted = {}

        class Signals:

            def __init__(self, eng, b):
                self.eng, self.b = eng, b

            def wait(self, name, k, before=0):
                self.eng.wait_ge(sem(name), plus(self.b, SIGNALS[name], k + PRIMED.get(name, 0)))

            def filled(self, name):
                k = bank_of[name]
                self.eng.wait_ge(filled[k], plus(self.b, fills_per_batch[k], fill_index[name] + 1))
                return banks[k]

            def drained(self, name):
                k = bank_of[name]
                self.eng.wait_ge(drained[k], plus(self.b, fills_per_batch[k], fill_index[name] + 1 + 1))

            def bank_free(self, name):
                k = bank_of[name]
                self.eng.wait_ge(drained[k], plus(self.b, fills_per_batch[k], fill_index[name] + 1))
                return banks[k]

        def full(ins, name):
            ins.then_inc(filled[bank_of[name]], 1)

        def free(ins, name):
            ins.then_inc(drained[bank_of[name]], 1)

        def done(ins, name, n=1):
            counted[name] = counted.get(name, 0) + n
            ins.then_inc(sem(name), n)

        NDMA_W = 6
        w_loaded = sem("weights_loaded")
        setup_dve = sem("setup_dve")
        setup_pool = sem("setup_pool")
        ffn_loaded = sem("ffn_weights_loaded")
        dve_step = sem("dve_step")
        pool_step = sem("pool_step")
        N_DVE_SETUP, N_POOL_SETUP = 12, 12
        block = es.enter_context(nc.Block())

        ffw = [Bl[:, 0, :, :], Bl[:, 1, :, :], Tf[:, :, :], Rf[:, :, :]]
        ffw = [a.rearrange("p a b -> p (a b)") for a in ffw]

        def expert(e):
            k, i = divmod(e, 2)
            if k < 4:
                base = ffw[k][:, i * 768:(i + 1) * 768]
            else:
                base = UW[:, :, :].rearrange("p a b -> p (a b)")[:, i * 768:(i + 1) * 768]
            return (base[:, 0:256].rearrange("p (c n) -> p c n", c=2),
                    base[:, 256:512].rearrange("p (c n) -> p c n", c=2), base[:, 512:768])

        fx = [Y[:, 0:8, :].rearrange("p (c a) b -> p c (a b)", c=CK),
              Y[:, 8:16, :].rearrange("p (c a) b -> p c (a b)", c=CK)]
        facc = [xt, xn]
        fg = [kvt[:, i, :] for i in range(2)]
        fh = [kvt[:, 2 + i, :] for i in range(2)]
        coef = sb("coef", [P, B * G * T, E])

        @block.sync
        def _(sp):
            sp.dma_start(const[:, :], const_d).then_inc(w_loaded, 16)
            sp.dma_start(param[:, :], param_d).then_inc(w_loaded, 16)
            sp.dma_start(wt[:, :], weight_d).then_inc(w_loaded, 16)
            sp.dma_start(subi[:, :, :], sub.rearrange("(t p) k -> p t k", p=P)).then_inc(w_loaded, 16)
            sp.dma_start(subTi[:, :], subT).then_inc(w_loaded, 16)
            with sp.Fori(0, B) as b:
                s = Signals(sp, b)
                s.wait("kblk_ready", 0)
                done(sp.dma_start(ctx[:, :, :], ctxT[b, :, :, :]), "ctx_loaded", 16)
                done(sp.dma_start(padr[:, :], pad_row[b, :, :]), "ctx_loaded", 16)
                done(sp.dma_start(padc[:, :], pad_col[b, :, :]), "ctx_loaded", 16)
                for g in range(G):
                    s.wait("x2_stored", 32 * g)
                    done(sp.dma_start(xt[:, :, :], x[b, g * GT:(g + 1) * GT, :]
                                      .rearrange("(t p) d -> p t d", p=P)), "x_loaded", 16)
                    s.wait("x2_ready", g + 1)
                    done(sp.dma_start(x2_d[b, g, :, :, :], xt[:, :, :]), "x2_stored", 16)
                    s.drained(f"x2T0.{g}")
                    s.drained(f"x2T1.{g}")
                    done(sp.dma_start(xnT_d[b, g, :, :, :], xnT), "x2_stored", 16)
            sp.wait_ge(sem("x2_stored"), B * SIGNALS["x2_stored"] + 16)
            for e in range(ES):
                gt_, up_, dn_ = expert(e)
                k, i = divmod(e, 2)
                flat = (ffw[k] if k < 4 else UW[:, :, :].rearrange("p a b -> p (a b)"))[:, i * 768:(i + 1) * 768]
                sp.dma_start(flat, ffn_d[:, e, :]).then_inc(ffn_loaded, 16)
            with sp.Fori(0, B) as b:
                for g in range(G):
                    sp.wait_ge(sem("y_stored"), b * 32 + 16 * g + 16)
                    sp.dma_start(fx[g], xnT_d[b, g, :, :, :]).then_inc(sem("fx_loaded"), 16)
                    sp.dma_start(facc[g][:, :, :], x2_d[b, g, :, :, :]).then_inc(sem("fx_loaded"), 16)
                    sp.wait_ge(sem("ff_y_used"), b * (G * 9) + g * 9 + 9 + 1)
                    sp.dma_start(out[b, g * GT:(g + 1) * GT, :].rearrange("(t p) d -> p t d", p=P),
                                 facc[g][:, :, :]).then_inc(sem("y_stored"), 16)
            sp.wait_ge(sem("y_stored"), B * G * 16 + 16)

        @block.tensor
        def _(pe):
            mm, tr = pe.matmul, pe.transpose
            ident = cst("ident")
            pe.wait_ge(w_loaded, 16 * 5)
            pe.wait_ge(setup_dve, N_DVE_SETUP)
            pe.wait_ge(setup_pool, N_POOL_SETUP)
            with pe.Fori(0, B) as b:
                s = Signals(pe, b)

                def transpose_rows(src, names):
                    for c in range(CK):
                        o = s.bank_free(names[c])
                        for t in range(T):
                            last = tr(o[:, t * P:(t + 1) * P], src[:, t, c * P:(c + 1) * P], ident)
                        full(last, names[c])

                for g in range(G):
                    s.wait("xn_ready", 3 * g + 1)
                    transpose_rows(xn, [f"hsT0.{g}", f"hsT1.{g}"])
                    s.drained(f"hsT0.{g}")
                    s.drained(f"hsT1.{g}")
                    for j, w in enumerate(("k", "k", "q", "q", "v", "v")):
                        n = f"proj{j}.{g}"
                        o = s.bank_free(n)
                        for c in range(CK):
                            last = mm(o[:, :], wgt(w, c, D)[:, (j % 2) * P:(j % 2 + 1) * P], hsT[:, c, :],
                                      start=c == 0, stop=c == CK - 1)
                        full(last, n)
                    n = f"stat.{g}"
                    o = s.bank_free(n)
                    s.wait("squares_ready", g + 1)
                    for t in range(T):
                        tt = slice(t * P, (t + 1) * P)
                        for c in range(CK):
                            mm(o[:, t * 12 + 8:t * 12 + 12], hsT[:, c, tt], wgt("beta", c, H),
                               start=c == 0, stop=c == CK - 1)
                        for i in range(4):
                            a = 2 * (i % 2) + (1 - i // 2)
                            last = mm(o[:, t * 12 + 2 * i:t * 12 + 2 * i + 2], sq[:, a, tt], cst("headsel"),
                                      start=True, stop=True)
                    full(last, n)
                    for t in range(T):
                        n = f"kv{t}.{g}"
                        o = s.bank_free(n)
                        tt = slice(t * P, (t + 1) * P)
                        for c in range(CK):
                            tr(o[:, c * P:(c + 1) * P], kq[:, c, 0, tt], ident)
                        s.wait("act_ready", 6 * g + 6)
                        for c in range(CK):
                            last = tr(o[:, (2 + c) * P:(3 + c) * P],
                                      vT[:, c, HALO + t * P:HALO + (t + 1) * P], ident)
                        full(last, n)
                    for t in range(T):
                        for r in range(2):
                            n = f"gram{t}{r}.{g}"
                            o = s.bank_free(n)
                            for i in range(2):
                                rr = slice(DH * r, DH * r + DH)
                                last = mm(o[:, i * 2 * P:(i + 1) * 2 * P], kq[rr, i, 0, t * P:(t + 1) * P],
                                          kq[rr, i, :, t * P:(t + 1) * P], start=True, stop=True)
                            full(last, n)
                    lv = 7 * g
                    n = f"P1.{g}"
                    o = s.bank_free(n)
                    s.wait("level_ready", lv + 1)
                    for h in range(HT):
                        last = mm(o[:, h * 32:(h + 1) * 32], Bl[:, 0, h, :], cst("eye32"), start=True, stop=True)
                    full(last, n)
                    for i, size in enumerate(LEVELS[1:5]):
                        n = f"P{size}.{g}"
                        o = s.bank_free(n)
                        s.wait("level_ready", lv + 2 + i)
                        if i == 0:
                            s.drained(f"P1.{g}")
                        else:
                            s.drained(f"D{LEVELS[i]}.{g}")
                        for h in range(HT):
                            last = mm(o[:, h * 32:(h + 1) * 32], Bl[:, (i + 1) % 2, h, :], Rc[:, h, :],
                                      start=True, stop=True)
                        full(last, n)
                        s.drained(n)
                        s.wait("blocks_ready", 5 * g + i + 1)
                        s.wait("blocks_cleared", 2 * g)
                        n = f"D{size}.{g}"
                        o = s.bank_free(n)
                        for h in range(HT):
                            last = mm(o[:, h * 32:(h + 1) * 32], Tf[:, h, :], Pc[:, h, :], start=True, stop=True)
                        full(last, n)
                    s.wait("blocks_ready", 5 * g + 5)
                    halves = [("a", 0), ("b", 8)]
                    s.wait("level_ready", lv + 6)
                    odd = lambda M, h: M[:, h, :].rearrange("p (a c) -> p a c", a=2)[:, :, 32:64]
                    even = lambda M, h: M[:, h, :].rearrange("p (a c) -> p a c", a=2)[:, :, 0:32]
                    for x_, h0 in halves:
                        n = f"P32{x_}.{g}"
                        o = s.bank_free(n)
                        for h in range(8):
                            last = mm(o[:, h * 64:(h + 1) * 64], Bl[:, 1, h0 + h, :], odd(Rf, h0 + h),
                                      start=True, stop=True)
                        full(last, n)
                    for x_, h0 in halves:
                        s.drained(f"P32{x_}.{g}")
                        n = f"R32{x_}.{g}"
                        o = s.bank_free(n)
                        for h in range(8):
                            last = mm(o[:, h * 64:(h + 1) * 64], Tf[:, h0 + h, :], odd(Pf, h0 + h),
                                      start=True, stop=True)
                        full(last, n)
                    for x_, h0 in halves:
                        n = f"T32{x_}.{g}"
                        o = s.bank_free(n)
                        for h in range(8):
                            last = mm(o[:, h * 64:(h + 1) * 64], Pf[:, h0 + h, :], even(Tf, h0 + h),
                                      start=True, stop=True)
                        full(last, n)
                    s.wait("level_ready", lv + 7)
                    for x_, h0 in halves:
                        s.drained(f"R32{x_}.{g}")
                        n = f"P64{x_}.{g}"
                        o = s.bank_free(n)
                        for h in range(8):
                            last = mm(o[:, h * 64:(h + 1) * 64], Bl[:, 0, h0 + h, :], Rf[:, h0 + h, 64:128],
                                      start=True, stop=True)
                        full(last, n)
                    for x_, h0 in halves:
                        s.drained(f"P64{x_}.{g}")
                        s.drained(f"T32{x_}.{g}")
                        n = f"R64{x_}.{g}"
                        o = s.bank_free(n)
                        for h in range(8):
                            last = mm(o[:, h * 64:(h + 1) * 64], Tf[:, h0 + h, :], Pf[:, h0 + h, 64:128],
                                      start=True, stop=True)
                        full(last, n)
                    s.wait("rows_ready", 8 * g + 8)
                    for t in range(T):
                        if t % 2 == 0:
                            s.drained(f"R64{'ab'[t // 2]}.{g}")
                        n = f"uw{t}.{g}"
                        o = s.bank_free(n)
                        for h in range(H):
                            last = mm(o[:, h * P:(h + 1) * P], Rf[:, t * H + h, :], Y[:, t * H + h, :],
                                      start=True, stop=True)
                        full(last, n)
                    for t in range(T):
                        s.drained(f"uw{t}.{g}")
                        n = f"wa{t}.{g}"
                        o = s.bank_free(n)
                        for h in range(H):
                            r, i = h % 2, h // 2
                            w_ = UW[:, t * H + h, 64:128]
                            mm(o[DH * r:DH * r + DH, i * P:(i + 1) * P], w_, attnT[:, t * H + h, :],
                               start=True, stop=True)
                            last = mm(o[DH * r:DH * r + DH, 256 + i * DH:256 + (i + 1) * DH], w_,
                                      kvt[:, t, h * DH:(h + 1) * DH], start=True, stop=True)
                        full(last, n)
                    for t in range(T):
                        s.drained(f"wa{t}.{g}")
                        if t > 0:
                            s.drained(f"state{t - 1}.{g}")
                        first = t == 0 and g == 0
                        n = f"state{t}.{g}"
                        o = s.bank_free(n)
                        for h in range(H):
                            rr, i = slice(DH * (h % 2), DH * (h % 2) + DH), h // 2
                            cc = slice(i * DH, (i + 1) * DH)
                            last = mm(o[rr, cc], kvt[:, t, h * DH:(h + 1) * DH], UW[:, t * H + h, 0:64],
                                      start=True, stop=first)
                            if not first:
                                last = mm(o[rr, cc], MT[rr, t, i, :], S[rr, t % 2, i, :], start=False, stop=True)
                        full(last, n)
                        for r in range(2):
                            n = f"out{t}{r}.{g}"
                            o = s.bank_free(n)
                            rr = slice(DH * r, DH * r + DH)
                            for i in range(2):
                                h = 2 * i + r
                                cc = slice(i * DH, (i + 1) * DH)
                                last = mm(o[:, cc], attnT[:, t * H + h, :], UW[:, t * H + h, 0:64],
                                          start=True, stop=first)
                                if not first:
                                    last = mm(o[:, cc], QeT[rr, t, i, :], S[rr, t % 2, i, :],
                                              start=False, stop=True)
                            full(last, n)
                    n = f"gm.{g}"
                    o = s.bank_free(n)
                    s.wait("fir_done", 2 * g + 2)
                    for i in range(4):
                        src = (sht, lng)[i // 2]
                        last = mm(o[:, :], cst(("mean_s", "mean_l")[i // 2]), src[:, i % 2, :],
                                  start=i == 0, stop=i == 3)
                    full(last, n)
                    n = f"dmT.{g}"
                    o = s.bank_free(n)
                    s.wait("delta_ready", 4 * g + 4)
                    for t in range(T):
                        last = mm(o[0:DH, t * P:(t + 1) * P], dm[:, t, :], ident, start=True, stop=True)
                    full(last, n)
                    s.drained(f"gm.{g}")
                    s.drained(f"dmT.{g}")
                    for m in range(CK):
                        n = f"h1{'ab'[m]}.{g}"
                        o = s.bank_free(n)
                        for i in range(4):
                            rhs = (hsT[:, 0, :], hsT[:, 1, :], gmT[:, :], dmT[:, :])[i]
                            k_ = DH if i == 3 else P
                            last = mm(o[:, :], wgt("fg1", i, D)[0:k_, m * P:(m + 1) * P], rhs,
                                      start=i == 0, stop=i == 3)
                        full(last, n)
                    s.drained(f"h1a.{g}")
                    s.drained(f"h1b.{g}")
                    n = f"logit.{g}"
                    o = s.bank_free(n)
                    for t in range(T):
                        for c in range(CK):
                            last = mm(o[:, t * 4:(t + 1) * 4], h1T[:, c, t * P:(t + 1) * P], wgt("fg2", c, 4),
                                      start=c == 0, stop=c == CK - 1)
                    full(last, n)
                    for t in range(T):
                        n = f"sl{t}.{g}"
                        o = s.bank_free(n)
                        for i in range(4):
                            last = tr(o[:, i * P:(i + 1) * P], (sht, lng)[i // 2][:, i % 2, t * P:(t + 1) * P], ident)
                        full(last, n)
                    s.wait("on_ready", g + 1)
                    transpose_rows(om, [f"oT0.{g}", f"oT1.{g}"])
                    s.drained(f"oT0.{g}")
                    s.drained(f"oT1.{g}")
                    for i in range(2):
                        n = f"oproj{i}.{g}"
                        o = s.bank_free(n)
                        for j in range(2):
                            t = 2 * i + j
                            for c in range(CK):
                                last = mm(o[:, j * D:(j + 1) * D], h1T[:, c, t * P:(t + 1) * P], wo_n[:, c, :],
                                          start=c == 0, stop=c == CK - 1)
                        full(last, n)
                    if g == 0:
                        s.wait("ctx_loaded", 48)
                        n = f"kx.{g}"
                        o = s.bank_free(n)
                        for m in range(CK):
                            for c in range(CK):
                                last = mm(o[:, m * S2:(m + 1) * S2], wgt("xk", c, D)[:, m * P:(m + 1) * P],
                                          ctx[:, c, 0:S2], start=c == 0, stop=c == CK - 1)
                        full(last, n)
                        n = f"vx.{g}"
                        o = s.bank_free(n)
                        for c in range(CK):
                            last = mm(o[:, 0:D], ctx[:, c, :], wgt("xv", c, D), start=c == 0, stop=c == CK - 1)
                        full(last, n)
                    n = f"any.{g}"
                    o = s.bank_free(n)
                    s.wait("mask_ready", g + 1)
                    full(mm(o[:, :], ones_b[0:S2, :], mT[:, :], start=True, stop=True), n)
                    s.wait("xn_ready", 3 * g + 2)
                    transpose_rows(xn, [f"x1T0.{g}", f"x1T1.{g}"])
                    s.drained(f"x1T0.{g}")
                    s.drained(f"x1T1.{g}")
                    for m in range(CK):
                        n = f"qx{m}.{g}"
                        o = s.bank_free(n)
                        for c in range(CK):
                            last = mm(o[:, :], wgt("xq", c, D)[:, m * P:(m + 1) * P], xnT[:, c, :],
                                      start=c == 0, stop=c == CK - 1)
                        full(last, n)
                    s.drained(f"qx0.{g}")
                    s.drained(f"qx1.{g}")
                    s.wait("kblk_ready", 1)
                    for t in range(T):
                        for c in range(CK):
                            n = f"sx{t}{c}.{g}"
                            o = s.bank_free(n)
                            ov = o[:, :].rearrange("p (h k) -> p h k", h=8)
                            mm(ov, qx[:, c, t * P:(t + 1) * P], Kblk[:, c, :, :], start=True, stop=False)
                            full(mm(ov, ident_b[:, :], mb[:, g * T + t, :].unsqueeze(1).broadcast_to([P, 8, S2]),
                                    start=False, stop=True), n)
                    n = f"mxT.{g}"
                    o = s.bank_free(n)
                    s.wait("nmx_ready", g + 1)
                    for t in range(T):
                        last = mm(o[64:112, t * P:(t + 1) * P], nmb[:, t, :], ident_b[:, :], start=True, stop=True)
                    full(last, n)
                    s.drained(n)
                    pvb = [s.bank_free(f"pv{t}.{g}") for t in range(T)]
                    s.drained("vx.0")

                    def scores(j):
                        n = f"sT{j}.{g}"
                        o = s.bank_free(n)
                        c, i = divmod(j, 4)
                        lhs = Kblk[:, c, 2 * i:2 * i + 2, :].rearrange("p a b -> p (a b)")
                        mm(o[:, :], lhs, qx[:, c, :], start=True, stop=False)
                        full(mm(o[:, :], aug_lhs[0:112, j, :], aug[0:112, :], start=False, stop=True), n)

                    def values(j):
                        s.drained(f"sT{j}.{g}")
                        for t in range(T):
                            last = mm(pvb[t][:, j * 34:(j + 1) * 34], PT[:, j % 4, t * P:(t + 1) * P], Va[:, j, :],
                                      start=True, stop=True)
                            if j == NPAIR - 1:
                                full(last, f"pv{t}.{g}")
                        if j < NPAIR - 1:
                            done(last, "pv_used")

                    scores(0)
                    scores(1)
                    for j in range(NPAIR):
                        if j + 2 < NPAIR:
                            scores(j + 2)
                        values(j)
                    s.wait("xn_ready", 3 * g + 3)
                    transpose_rows(xn, [f"x2T0.{g}", f"x2T1.{g}"])
                    s.drained(f"x2T0.{g}")
                    s.drained(f"x2T1.{g}")
                    n = f"route.{g}"
                    o = s.bank_free(n)
                    for t in range(T):
                        for c in range(CK):
                            last = mm(o[:, t * E:(t + 1) * E], xnT[:, c, t * P:(t + 1) * P], wgt("route", c, E),
                                      start=c == 0, stop=c == CK - 1)
                    full(last, n)
            pe.wait_ge(sem("route_sums"), 1)
            mm(banks[0][:, 0:2 * E], cst("ones"), gw[:, 0, :, :].rearrange("p t k -> p (t k)"),
               start=True, stop=True).then_inc(sem("route_total"), 1)
            pe.wait_ge(ffn_loaded, 16 * ES)
            pe.wait_ge(sem("coef_ready"), 1)
            with pe.Fori(0, B) as b:
                for g in range(G):
                    pe.wait_ge(sem("fx_loaded"), b * 64 + 32 * g + 32)

                    def hidden(e):
                        k = b * (G * ES) + g * ES + e
                        wg_, wu_, _ = expert(e)
                        pe.wait_ge(sem("ff_h_ready"), k if (g or e > 1) else b * (G * ES) + 1)
                        for c in range(CK):
                            last = mm(banks[e % 2][:, :], wg_[:, c, :], fx[g][:, c, :], start=c == 0, stop=c == CK - 1)
                        last.then_inc(sem("ff_gate"), 1)
                        for c in range(CK):
                            last = mm(banks[2 + e % 2][:, :], wu_[:, c, :], fx[g][:, c, :],
                                      start=c == 0, stop=c == CK - 1)
                        last.then_inc(sem("ff_up"), 1)

                    def down(e, srcs, slot):
                        pe.wait_ge(sem("ff_h_ready"), b * (G * ES) + g * ES + e + 2)
                        k = b * (G * 9) + g * 9 + slot
                        pe.wait_ge(sem("ff_y_used"), k if (g or slot > 1) else b * (G * 9) + 1)
                        for i in range(2):
                            o = banks[4 + 2 * ((g * 9 + slot) % 2) + i]
                            for j in range(2):
                                t = 2 * i + j
                                for q_, e_ in enumerate(srcs):
                                    last = mm(o[:, j * D:(j + 1) * D], fh[e_ % 2][:, t * P:(t + 1) * P], expert(e_)[2],
                                              start=q_ == 0, stop=q_ == len(srcs) - 1)
                        last.then_inc(sem("ff_y"), 1)

                    hidden(0)
                    for e in range(1, ES):
                        hidden(e)
                        if e < ES - 1 or True:
                            if e - 1 < E:
                                down(e - 1, [e - 1], e - 1)
                    down(ES - 1, [ES - 2, ES - 1], E)

        @block.scalar
        def _(act):
            act.wait_ge(w_loaded, 16 * 5)
            act.wait_ge(setup_dve, N_DVE_SETUP)
            act.wait_ge(setup_pool, N_POOL_SETUP)
            act.activation(rtemp[:, 1:2], rtemp[:, 0:1], ACT.Exp, scale=-1.0).then_inc(sem("temp_exp"), 1)
            act.wait_ge(sem("temp_exp"), 1)
            act.activation(rtemp[:, 2:3], rtemp[:, 1:2], ACT.Ln, bias=cst("ones")[:, 0:1]).then_inc(sem("temp_ln"), 1)
            with act.Fori(0, B) as b:
                s = Signals(act, b)

                def evac(out_, in_, name, func=ACT.Copy, **kw):
                    free(act.activation(out_, in_, func, **kw), name)

                for g in range(G):
                    for c in range(CK):
                        n = f"hsT{c}.{g}"
                        o = s.filled(n)
                        evac(hsT[:, c, :], o[:, :], n)
                    for j in range(6):
                        n = f"proj{j}.{g}"
                        o = s.filled(n)
                        if j == 0:
                            s.wait("rstd_ready", 3 * g + 1)
                        evac(pre[:, j, CONV - 1:], o[:, :], n)
                    for j in range(6):
                        s.wait("conv_ready", 6 * g + j + 1)
                        dst = kq[:, j % 2, j // 2, :] if j < 4 else vT[:, j % 2, HALO:]
                        done(act.activation(dst, cv[:, j % 2, :], ACT.Silu), "act_ready")
                    n = f"stat.{g}"
                    o = s.filled(n)
                    ov = o[:, 0:T * 12].rearrange("p (t k) -> p t k", t=T)
                    act.activation(st[:, :, 0:8], ov[:, :, 0:8], ACT.Copy)
                    evac(st[:, :, 8:12], ov[:, :, 8:12], n, ACT.Tanh, scale=0.5)
                    for t in range(T):
                        n = f"kv{t}.{g}"
                        o = s.filled(n)
                        evac(kvt[:, t, :], o[:, :], n)

                    def spread(dst, src, n):
                        for r in range(4):
                            rr = slice(32 * r, 32 * r + 32)
                            last = act.activation(dst[rr, :, rr], src[rr, :, :], ACT.Copy)
                        done(last, n)

                    for i, size in enumerate(LEVELS[1:5]):
                        s.wait("compact_ready", 5 * g + i + 1)
                        spread(Tf, Tc, "blocks_ready")
                        n = f"P{size}.{g}"
                        o = s.filled(n)
                        evac(Pc[:, :, :], o[:, :].rearrange("p (h k) -> p h k", k=32), n)
                    s.drained(f"D16.{g}")
                    for r in range(4):
                        rr = slice(32 * r, 32 * r + 32)
                        act.activation(Rf[rr, :, rr], Rc[rr, :, :], ACT.Copy)
                    s.wait("compact_ready", 5 * g + 5)
                    spread(Tf, Tc, "blocks_ready")
                    view = lambda M, h0: M[:, h0:h0 + 8, :].rearrange("p h (a c) -> p h a c", a=2)
                    for x_, h0 in (("a", 0), ("b", 8)):
                        n = f"P32{x_}.{g}"
                        o = s.filled(n)
                        evac(view(Pf, h0)[:, :, :, 32:64],
                             o[:, :].rearrange("p (h a c) -> p h a c", h=8, a=2), n)
                    for x_, h0 in (("a", 0), ("b", 8)):
                        n = f"P64{x_}.{g}"
                        o = s.filled(n)
                        s.filled(f"T32{x_}.{g}")
                        evac(Pf[:, h0:h0 + 8, 64:128], o[:, :].rearrange("p (h c) -> p h c", h=8), n)
                    for t in range(T):
                        n = f"uw{t}.{g}"
                        o = s.filled(n)
                        if t == 0:
                            s.filled(f"R64a.{g}")
                            s.filled(f"R64b.{g}")
                        evac(UW[:, t * H:(t + 1) * H, :], o[:, :].rearrange("p (h c) -> p h c", h=H), n)
                    for t in range(T):
                        n = f"state{t}.{g}"
                        o = s.filled(n)
                        if t > 0:
                            s.filled(f"out{t - 1}1.{g}")
                        evac(S[:, (t + 1) % 2, :, :], o[:, 0:P].rearrange("p (i c) -> p i c", i=2), n)
                    n = f"gm.{g}"
                    o = s.filled(n)
                    evac(gmT[:, :], o[:, :], n)
                    n = f"dmT.{g}"
                    o = s.filled(n)
                    evac(dmT[:, :], o[0:DH, :], n, scale=1.0 / H)
                    for m in range(CK):
                        n = f"h1{'ab'[m]}.{g}"
                        o = s.filled(n)
                        evac(h1T[:, m, :], o[:, :], n, ACT.Gelu, bias=prm("fg_b1", m, 1))
                    s.drained(f"logit.{g}")
                    s.wait("gate_ready", 2 * g + 1)
                    done(act.activation(gw[:, 1, :, :], gw[:, 0, :, :], ACT.Exp), "exp_ready")
                    for c in range(CK):
                        n = f"oT{c}.{g}"
                        o = s.filled(n)
                        evac(h1T[:, c, :], o[:, :], n)
                    if g == 0:
                        n = f"kx.{g}"
                        o = s.filled(n)
                        for m in range(CK):
                            last = act.activation(kxT[:, m, :], o[:, m * S2:(m + 1) * S2], ACT.Identity,
                                                  bias=prm("bk", m, 1))
                        free(last, n)
                    for c in range(CK):
                        n = f"x1T{c}.{g}"
                        o = s.filled(n)
                        evac(xnT[:, c, :], o[:, :], n)
                    for j in range(NPAIR):
                        n = f"sT{j}.{g}"
                        o = s.filled(n)
                        if j >= 4:
                            s.wait("pv_used", 7 * g + j - 3)
                        evac(PT[:, j % 4, :], o[:, :], n, ACT.Exp)
                    for c in range(CK):
                        n = f"x2T{c}.{g}"
                        o = s.filled(n)
                        evac(xnT[:, c, :], o[:, :], n)
            act.wait_ge(drained[bank_of["route.1"]], B * fills_per_batch[bank_of["route.1"]] + 1)
            act.activation(coef[:, :, :], route[:, :, :], ACT.Sigmoid).then_inc(sem("route_scores"), 1)
            with act.Fori(0, B) as b:
                for g in range(G):
                    for e in range(ES):
                        k = b * (G * ES) + g * ES + e
                        act.wait_ge(sem("ff_gate"), k + 1)
                        act.wait_ge(sem("ff_h_ready"), k if (g or e > 1) else b * (G * ES) + 1)
                        act.activation(fg[e % 2], banks[e % 2][:, :], ACT.Silu).then_inc(sem("ff_silu"), 1)

        @block.gpsimd
        def _(pool):
            n_setup = [0]

            def once(ins):
                n_setup[0] += 1
                ins.then_inc(setup_pool, 1)
                pool.wait_ge(setup_pool, n_setup[0])

            once(pool.memset(minus_half[:, :], -0.5))
            once(pool.memset(eps[:, 0, :], 1e-5))
            once(pool.memset(eps[:, 1, :], 1e-12))
            once(pool.memset(Tf[:, :, :], 0.0))
            once(pool.memset(Rf[:, :, :], 0.0))
            once(pool.memset(pre[:, :, :], 0.0))
            once(pool.memset(vT[:, :, :], 0.0))
            once(pool.memset(Va[:, :, :], 0.0))
            once(pool.memset(UW[:, :, :], 0.0))
            once(pool.memset(Va[0:64, :, 32:33], 1.0))
            once(pool.memset(Va[64:128, :, 33:34], 1.0))
            once(pool.memset(aug[:, :], 0.0))
            assert n_setup[0] == N_POOL_SETUP
            for k in range(8):
                pool.sem_inc(drained[k], 1)
            for n in ("ff_h_ready", "ff_y", "ff_y_used"):
                pool.sem_inc(sem(n), 1)
            for n in ("kblk_ready", "blocks_cleared", "x2_stored"):
                pool.sem_inc(sem(n), PRIMED[n])
            pool.sem_inc(sem("y_stored"), 16)
            pool.wait_ge(setup_dve, N_DVE_SETUP)
            steps = [0]
            with pool.Fori(0, B) as b:
                s = Signals(pool, b)
                POOL_STEPS = 8

                def link(ins):
                    steps[0] += 1
                    ins.then_inc(pool_step, 1)
                    pool.wait_ge(pool_step, plus(b, POOL_STEPS, steps[0]))

                def norm_scale(k, g):
                    s.wait("stats_ready", 3 * g + k)
                    link(pool.tensor_tensor(rstd[:, :], mv[:, :, 1], eps[:, 0, 0:T], ALU.add))
                    done(pool.tensor_tensor(rstd[:, :], rstd[:, :], minus_half[:, 0:T], ALU.pow), "rstd_ready")

                for g in range(G):
                    norm_scale(1, g)
                    s.wait("act_ready", 6 * g + 4)
                    done(pool.tensor_tensor(sq, kq[:, :, :, :].rearrange("p a b c -> p (a b) c"),
                                            kq[:, :, :, :].rearrange("p a b c -> p (a b) c"), ALU.mult),
                         "squares_ready")
                    s.drained(f"stat.{g}")
                    link(pool.tensor_tensor(rn[:, :, :], st[:, :, 0:8],
                                            eps[:, 1, 0:8].unsqueeze(1).broadcast_to([P, T, 8]), ALU.add))
                    done(pool.tensor_tensor(rn[:, :, :], rn[:, :, :],
                                            minus_half[:, 0:8].unsqueeze(1).broadcast_to([P, T, 8]), ALU.pow),
                         "rnorm_ready")
                    for i, size in enumerate(LEVELS):
                        s.wait("rows_ready", 8 * g + 4)
                        if i >= 2:
                            s.filled(f"P{LEVELS[i - 2]}{'b' if LEVELS[i - 2] > 16 else ''}.{g}")
                        done(pool.tensor_tensor(Bl[:, i % 2, :, :], A[:, :, :],
                                                cst(f"level{size}").unsqueeze(1).broadcast_to([P, HT, P]),
                                                ALU.mult), "level_ready")
                    s.drained(f"uw0.{g}")
                    for a in range(2):
                        rr, cc = slice(64 * a + 32, 64 * a + 64), slice(64 * a, 64 * a + 32)
                        zero = cst("upper", rr)[:, cc].unsqueeze(1).broadcast_to([32, HT, 32])
                        done(pool.tensor_tensor(Tf[rr, :, cc], zero, zero, ALU.mult), "blocks_cleared")
                        s.wait("blocks_cleared", 2 * g + a + 1)
                    s.wait("mix_ready", g + 1)
                    done(pool.tensor_tensor(osq, om[:, :, :], om[:, :, :], ALU.mult), "osq_ready")
                    s.wait("oms_ready", g + 1)
                    done(pool.tensor_tensor(orn[:, :], oss[:, :], minus_half[:, 0:HT], ALU.pow), "orms_ready")
                    norm_scale(2, g)
                    norm_scale(3, g)
                assert steps[0] == POOL_STEPS, steps

        @block.vector
        def _(dve):
            V = dve
            dve.wait_ge(w_loaded, 16 * 5)
            n_setup = [0]

            def once(ins):
                n_setup[0] += 1
                ins.then_inc(setup_dve, 1)
                dve.wait_ge(setup_dve, n_setup[0])

            once(V.tensor_copy(ident_b[:, :], cst("ident")))
            once(V.tensor_copy(ones_b[:, :], cst("ones")))
            once(V.tensor_copy(aug_lhs[0:S2, :, :].rearrange("p j (a k) -> p (j a) k", a=2),
                               cst("eye64", slice(0, S2)).unsqueeze(1).broadcast_to([S2, XH, S2])))
            once(V.memset(aug_lhs[64:128, :, :], 0.0))
            once(V.tensor_copy(aug_lhs[64:112, :, :].rearrange("p j (a k) -> p (j a) k", a=2),
                               cst("eye64", slice(64, 112))[:, 0:XH].unsqueeze(2).broadcast_to([48, XH, S2])))
            for part in (1, 2):
                once(V.tensor_tensor(aug_lhs[64:112, :, :].rearrange("p j (a k) -> p (j a) k", a=2),
                                     aug_lhs[64:112, :, :].rearrange("p j (a k) -> p (j a) k", a=2),
                                     cst("eye64", slice(64, 112))[:, part * XH:(part + 1) * XH].unsqueeze(2)
                                     .broadcast_to([48, XH, S2]), ALU.add))
            once(V.scalar_tensor_tensor(rtemp[:, 0:1], prm("temp"), -1.0, prm("temp"), ALU.mult, ALU.max))
            for c in range(CK):
                n0 = WEIGHT["o"][0] + c * D
                once(V.tensor_scalar(wo_n[:, c, :], wt[:, n0:n0 + D], prm("onorm"), None, ALU.mult))
            once(V.tensor_scalar(sub01[:, :, :], subi[:, :, :], 0.0, None, ALU.not_equal))
            once(V.tensor_scalar(subT01[:, :], subTi[:, :], 0.0, None, ALU.not_equal))
            assert n_setup[0] == N_DVE_SETUP, n_setup
            steps = [0]
            DVE_HEAD = 3

            def hlink(ins, k):
                ins.then_inc(dve_step, 1)
                dve.wait_ge(dve_step, k)

            dve.wait_ge(sem("temp_ln"), 1)
            hlink(V.scalar_tensor_tensor(rtemp[:, 3:4], prm("temp"), 0.0, rtemp[:, 2:3], ALU.max, ALU.add), 1)
            hlink(V.tensor_scalar(rtemp[:, 4:5], rtemp[:, 3:4], 1e-4, None, ALU.add), 2)
            hlink(V.reciprocal(rtemp[:, 5:6], rtemp[:, 4:5]), 3)

            with dve.Fori(0, B) as b:
                s = Signals(dve, b)

                def step(ins):
                    steps[0] += 1
                    ins.then_inc(dve_step, 1)
                    return steps[0]

                def after(k):
                    dve.wait_ge(dve_step, plus(b, DVE_STEPS, k + DVE_HEAD))

                def link(ins):
                    after(step(ins))

                def norm_rows(k, g):
                    for t in range(T):
                        last = step(V.bn_stats(stats[:, t, :], xt[:, t, :]))
                    after(last)
                    V.memset(spare[:, :], 0.0)
                    for t in range(T):
                        last = V.bn_aggr(mv[:, t, :], stats[:, t, :])
                    done(last, "stats_ready")
                    s.wait("rstd_ready", 3 * g + k)
                    for t in range(T):
                        last = V.tensor_scalar(xn[:, t, :], xt[:, t, :], mv[:, t, 0:1], rstd[:, t:t + 1],
                                               ALU.subtract, ALU.mult)
                    done(last, "xn_ready")

                fir_k = {}

                def fir(g, lo, hi):
                    for j in range(lo, hi):
                        for c in range(CK):
                            w_ = param[:, PARAM["fir_l"][0] + c * FL + j:PARAM["fir_l"][0] + c * FL + j + 1]
                            src = vT[:, c, j:j + GT]
                            if j == 0:
                                k = step(V.tensor_scalar(lng[:, c, :], src, w_, None, ALU.mult))
                            else:
                                after(fir_k[c])
                                ins = V.scalar_tensor_tensor(lng[:, c, :], src, w_, lng[:, c, :], ALU.mult, ALU.add)
                                k = step(ins)
                            fir_k[c] = k

                def fir_short(g):
                    for j in range(FS):
                        for c in range(CK):
                            w_ = param[:, PARAM["fir_s"][0] + c * FS + j:PARAM["fir_s"][0] + c * FS + j + 1]
                            src = vT[:, c, FL - FS + j:FL - FS + j + GT]
                            if j == 0:
                                fir_k["s", c] = step(V.tensor_scalar(sht[:, c, :], src, w_, None, ALU.mult))
                            else:
                                after(fir_k["s", c])
                                ins = V.scalar_tensor_tensor(sht[:, c, :], src, w_, sht[:, c, :], ALU.mult, ALU.add)
                                if j < FS - 1:
                                    fir_k["s", c] = step(ins)
                                else:
                                    done(ins, "fir_done")

                for g in range(G):
                    s.wait("x_loaded", 16 * g + 16)
                    if g == 0:
                        s.wait("ctx_loaded", 48)
                        step(V.tensor_scalar(pr01[:, :], padr[:, :], 0.0, None, ALU.not_equal))
                        link(V.tensor_scalar(pc01[:, :], padc[:, :], 0.0, None, ALU.not_equal))
                        link(V.tensor_tensor(mbf[:, :, :], sub01[:, :, :],
                                             pr01[:, :].unsqueeze(1).broadcast_to([P, L // P, S2]), ALU.mult))
                        step(V.tensor_scalar(mb[:, :, :], mbf[:, :, :], -1.0, -NEG, ALU.add, ALU.mult))
                    norm_rows(1, g)
                    for j in range(6):
                        s.drained(f"proj{j}.{g}")
                        if j >= 2:
                            s.wait("act_ready", 6 * g + j - 1)
                        cw = lambda i: param[:, PARAM["conv"][0] + j * CONV + i:PARAM["conv"][0] + j * CONV + i + 1]
                        link(V.tensor_scalar(cv[:, j % 2, :], pre[:, j, 0:GT], cw(0), None, ALU.mult))
                        for i in range(1, CONV):
                            ins = V.scalar_tensor_tensor(cv[:, j % 2, :], pre[:, j, i:i + GT], cw(i),
                                                         cv[:, j % 2, :], ALU.mult, ALU.add)
                            if i < CONV - 1:
                                link(ins)
                        done(ins, "conv_ready")
                    s.wait("act_ready", 6 * g + 6)
                    fir(g, 0, 4)
                    s.drained(f"stat.{g}")
                    link(V.tensor_scalar(beta[:, :, :], st[:, :, 8:12], 1.0, 0.5, ALU.add, ALU.mult))
                    s.wait("rnorm_ready", g + 1)
                    link(V.tensor_tensor(rb[:, :, :], beta[:, :, :], rn[:, :, 4:8], ALU.mult))
                    link(V.tensor_tensor(sc[:, :, :], rb[:, :, :], rn[:, :, 4:8], ALU.mult))
                    for t in range(T):
                        for r in range(2):
                            n = f"gram{t}{r}.{g}"
                            o = s.filled(n)
                            ov = o[:, :].rearrange("p (i a c) -> p i a c", i=2, a=2)
                            for i in range(2):
                                h = t * H + 2 * i + r
                                V.scalar_tensor_tensor(A[:, h, :], ov[:, i, 0, :], sc[:, t, 2 * i + r:2 * i + r + 1],
                                                       cst("lower"), ALU.mult, ALU.mult)
                            free(V.tensor_tensor(attnT[:, t * H + r:(t + 1) * H:2, :], ov[:, :, 1, :],
                                                 cst("upper").unsqueeze(1).broadcast_to([P, 2, P]), ALU.mult), n)
                        if t == T - 1:
                            pass
                    for t in range(T):
                        s.drained(f"kv{t}.{g}")
                        hh = slice(t * H, (t + 1) * H)
                        ins = V.tensor_tensor(Y[:, hh, 0:64], kvt[:, t, 256:512].rearrange("p (h c) -> p h c", h=H),
                                              rb[:, t, :].unsqueeze(2).broadcast_to([P, H, DH]), ALU.mult)
                        done(ins, "rows_ready")
                        ins = V.tensor_tensor(Y[:, hh, 64:128], kvt[:, t, 0:256].rearrange("p (h c) -> p h c", h=H),
                                              sc[:, t, :].unsqueeze(2).broadcast_to([P, H, DH]), ALU.mult)
                        done(ins, "rows_ready")
                    n = f"P1.{g}"
                    o = s.filled(n)
                    free(V.tensor_tensor(Rc[:, :, :], cst("eye32").unsqueeze(1).broadcast_to([P, HT, 32]),
                                         o[:, :].rearrange("p (h k) -> p h k", k=32), ALU.subtract), n)
                    s.drained(n)
                    done(V.transpose(Tc[:, :, :].rearrange("p h k -> p (h k)"),
                                     Rc[:, :, :].rearrange("p h k -> p (h k)")), "compact_ready")
                    for i, size in enumerate(LEVELS[1:5]):
                        fir(g, 4 + 4 * i, 8 + 4 * i)
                        n = f"D{size}.{g}"
                        o = s.filled(n)
                        free(V.tensor_tensor(Rc[:, :, :], Rc[:, :, :],
                                             o[:, :].rearrange("p (h k) -> p h k", k=32), ALU.subtract), n)
                        s.drained(n)
                        s.wait("blocks_ready", 5 * g + i + 1)
                        done(V.transpose(Tc[:, :, :].rearrange("p h k -> p (h k)"),
                                         Rc[:, :, :].rearrange("p h k -> p (h k)")), "compact_ready")
                    fir(g, 20, 24)
                    view = lambda M, h0: M[:, h0:h0 + 8, :].rearrange("p h (a c) -> p h a c", a=2)
                    for x_, h0 in (("a", 0), ("b", 8)):
                        n = f"R32{x_}.{g}"
                        o = s.filled(n)
                        for a in range(2):
                            rr = slice(64 * a, 64 * a + 32)
                            last = V.tensor_scalar(Rf[rr, h0:h0 + 8, 64 * a + 32:64 * a + 64],
                                                   o[rr, :].rearrange("p (h a c) -> p h a c", h=8, a=2)[:, :, a, :],
                                                   -1.0, None, ALU.mult)
                        free(last, n)
                    for x_, h0 in (("a", 0), ("b", 8)):
                        n = f"T32{x_}.{g}"
                        o = s.filled(n)
                        for a in range(2):
                            rr = slice(64 * a + 32, 64 * a + 64)
                            last = V.tensor_scalar(Tf[rr, h0:h0 + 8, 64 * a:64 * a + 32],
                                                   o[rr, :].rearrange("p (h a c) -> p h a c", h=8, a=2)[:, :, a, :],
                                                   -1.0, None, ALU.mult)
                        free(last, n)
                    fir(g, 24, 28)
                    for x_, h0 in (("a", 0), ("b", 8)):
                        n = f"R64{x_}.{g}"
                        o = s.filled(n)
                        free(V.tensor_scalar(Rf[0:64, h0:h0 + 8, 64:128], o[0:64, :].rearrange("p (h c) -> p h c", h=8),
                                             -1.0, None, ALU.mult), n)
                    fir(g, 28, FL)
                    fir_short(g)
                    for t in range(T):
                        n = f"wa{t}.{g}"
                        o = s.filled(n)
                        V.tensor_tensor(QeT[:, t, :, :], kq[:, :, 1, t * P:(t + 1) * P],
                                        o[:, 0:256].rearrange("p (i c) -> p i c", i=2), ALU.subtract)
                        free(V.tensor_tensor(MT[:, t, :, :], cst("eye64").unsqueeze(1).broadcast_to([P, 2, DH]),
                                             o[:, 256:384].rearrange("p (i c) -> p i c", i=2), ALU.subtract), n)
                    for t in range(T):
                        for r in range(2):
                            n = f"out{t}{r}.{g}"
                            o = s.filled(n)
                            free(V.tensor_tensor(delta[:, t, :].rearrange("p (i r c) -> p i r c", i=2, r=2)[:, :, r, :],
                                                 o[:, 0:P].rearrange("p (i c) -> p i c", i=2),
                                                 rn[:, t, r:4:2].unsqueeze(2).broadcast_to([P, 2, DH]), ALU.mult), n)
                        s.drained(f"out{t}0.{g}")
                        s.drained(f"out{t}1.{g}")
                        done(V.tensor_reduce(dm[:, t, :], delta[:, t, :].rearrange("p (h c) -> p c h", h=H),
                                             AX.X, ALU.add), "delta_ready")
                    n = f"logit.{g}"
                    o = s.filled(n)
                    free(V.tensor_tensor(gw[:, 2, :, :], o[:, 0:T * 4].rearrange("p (t k) -> p t k", t=T),
                                         prm("fg_b2").unsqueeze(1).broadcast_to([P, T, 4]), ALU.add), n)
                    s.drained(n)
                    link(V.tensor_scalar(gw[:, 3, :, :], gw[:, 2, :, :], rtemp[:, 5:6], None, ALU.mult))
                    link(V.tensor_reduce(gs[:, 0, :], gw[:, 3, :, :], AX.X, ALU.max))
                    done(V.tensor_tensor(gw[:, 0, :, :], gw[:, 3, :, :],
                                         gs[:, 0, :].unsqueeze(2).broadcast_to([P, T, 4]), ALU.subtract), "gate_ready")
                    s.wait("exp_ready", g + 1)
                    link(V.tensor_reduce(gs[:, 1, :], gw[:, 1, :, :], AX.X, ALU.add))
                    link(V.reciprocal(gs[:, 2, :], gs[:, 1, :]))
                    link(V.tensor_tensor(gw[:, 4, :, :], gw[:, 1, :, :],
                                         gs[:, 2, :].unsqueeze(2).broadcast_to([P, T, 4]), ALU.mult))
                    link(V.tensor_scalar(gs[:, 3, :], gw[:, 4, :, 3], MIN_LOCAL, None, ALU.mult))
                    step(V.tensor_copy(gw[:, 5, :, 2:4], gw[:, 4, :, 2:4]))
                    link(V.tensor_tensor(gw[:, 5, :, 0:2], gw[:, 4, :, 0:2],
                                         gs[:, 3, :].unsqueeze(2).broadcast_to([P, T, 2]), ALU.max))
                    link(V.tensor_reduce(gs[:, 1, :], gw[:, 5, :, :], AX.X, ALU.add))
                    link(V.reciprocal(gs[:, 2, :], gs[:, 1, :]))
                    done(V.tensor_tensor(gw[:, 6, :, :], gw[:, 5, :, :],
                                         gs[:, 2, :].unsqueeze(2).broadcast_to([P, T, 4]), ALU.mult), "gate_ready")
                    s.wait("gate_ready", 2 * g + 2)
                    ks = []
                    for t in range(T):
                        n = f"sl{t}.{g}"
                        o = s.filled(n)
                        ks.append(step(V.tensor_scalar(om[:, t, :], o[:, 0:256], gw[:, 6, t, 0:1], None, ALU.mult)))
                    for t in range(T):
                        n = f"sl{t}.{g}"
                        after(ks[t])
                        o = banks[bank_of[n]]
                        free(V.scalar_tensor_tensor(om[:, t, :], o[:, 256:512], gw[:, 6, t, 1:2], om[:, t, :],
                                                    ALU.mult, ALU.add), n)
                    for t in range(T):
                        s.drained(f"sl{t}.{g}")
                        ks[t] = step(V.scalar_tensor_tensor(om[:, t, :], delta[:, t, :], gw[:, 6, t, 2:3],
                                                            om[:, t, :], ALU.mult, ALU.add))
                    for t in range(T):
                        after(ks[t])
                        last = V.scalar_tensor_tensor(om[:, t, :], kvt[:, t, 256:512], gw[:, 6, t, 3:4],
                                                      om[:, t, :], ALU.mult, ALU.add)
                    done(last, "mix_ready")
                    s.wait("osq_ready", g + 1)
                    link(V.tensor_reduce(gw[:, 7, :, :].rearrange("p a b -> p (a b)"),
                                         osq.rearrange("p t (h c) -> p (t h) c", h=H), AX.X, ALU.add))
                    done(V.tensor_scalar(oss[:, :], gw[:, 7, :, :].rearrange("p a b -> p (a b)"), 1.0 / DH, 1e-5,
                                         ALU.mult, ALU.add), "oms_ready")
                    s.wait("orms_ready", g + 1)
                    omv = om[:, :, :].rearrange("p t (h c) -> p (t h) c", h=H)
                    done(V.tensor_tensor(omv, omv, orn[:, :].unsqueeze(2).broadcast_to([P, HT, DH]), ALU.mult),
                         "on_ready")
                    for i in range(2):
                        n = f"oproj{i}.{g}"
                        o = s.filled(n)
                        dst = xt[:, 2 * i:2 * i + 2, :]
                        free(V.tensor_tensor(dst, dst, o[:, :].rearrange("p (t d) -> p t d", t=2), ALU.add), n)
                    s.drained(f"oproj0.{g}")
                    s.drained(f"oproj1.{g}")
                    if g == 0:
                        n = f"vx.{g}"
                        o = s.filled(n)
                        for r in range(2):
                            rr = slice(64 * r, 64 * r + 64)
                            vv = o[rr, 0:D].rearrange("p (j r c) -> p j r c", r=2, c=XD)[:, :, r, :]
                            bb = prm("bv")[rr, :].rearrange("p (j r c) -> p j r c", r=2, c=XD)[:, :, r, :]
                            last = V.tensor_tensor(Va[rr, :, XD * r:XD * (r + 1)], vv, bb, ALU.add)
                        free(last, n)
                        s.drained(f"kx.{g}")
                        for c in range(CK):
                            last = V.tensor_tensor(Kblk[:, c, :, :], kxT[:, c, :].unsqueeze(1).broadcast_to([P, 8, S2]),
                                                   cst("head16").unsqueeze(2).broadcast_to([P, 8, S2]), ALU.mult)
                        done(last, "kblk_ready")
                    link(V.tensor_scalar(mT[:, :], subT01[:, g * GT:(g + 1) * GT], pc01[:, 0:1], None, ALU.mult))
                    done(V.tensor_scalar(aug[0:S2, :], mT[:, :], -1.0, -NEG, ALU.add, ALU.mult), "mask_ready")
                    norm_rows(2, g)
                    n = f"any.{g}"
                    o = s.filled(n)
                    free(V.tensor_scalar(abc, o[:, :], 1.0, XD ** -0.5, ALU.min, ALU.mult), n)
                    s.drained(n)
                    for m in range(CK):
                        n = f"qx{m}.{g}"
                        o = s.filled(n)
                        free(V.scalar_tensor_tensor(qx[:, m, :], o[:, :], prm("bq", m, 1), abc, ALU.add, ALU.mult), n)
                    for t in range(T):
                        for c in range(CK):
                            n = f"sx{t}{c}.{g}"
                            o = s.filled(n)
                            free(V.tensor_reduce(nmx[:, 0, t, 8 * c:8 * c + 8], o[:, :].rearrange("p (h k) -> p h k", h=8),
                                                 AX.X, ALU.max, negate=True), n)
                    s.drained(f"sx30.{g}")
                    s.drained(f"sx31.{g}")
                    link(V.tensor_copy(nmb[:, :, 0:16], nmx[:, 0, :, :]))
                    link(V.tensor_tensor(nmx[:, 1, :, :], nmx[:, 0, :, :], nmb[:, :, 0:16], ALU.subtract))
                    link(V.tensor_copy(nmb[:, :, 16:32], nmx[:, 1, :, :]))
                    link(V.tensor_tensor(nmx[:, 0, :, :], nmx[:, 1, :, :], nmb[:, :, 16:32], ALU.subtract))
                    done(V.tensor_copy(nmb[:, :, 32:48], nmx[:, 0, :, :]), "nmx_ready")
                    n = f"mxT.{g}"
                    o = s.filled(n)
                    free(V.tensor_copy(aug[64:112, :], o[64:112, :]), n)
                    for t in range(T):
                        n = f"pv{t}.{g}"
                        o = s.filled(n)
                        ov = o[:, 0:NPAIR * 34].rearrange("p (j c) -> p j c", c=34)
                        link(V.reciprocal(rden[:, t, :, :], ov[:, :, 32:34]))
                        free(V.tensor_tensor(xo[:, :].rearrange("p (j r c) -> p j r c", r=2, c=XD),
                                             ov[:, :, 0:32].rearrange("p j (r c) -> p j r c", r=2),
                                             rden[:, t, :, :].unsqueeze(3).broadcast_to([P, NPAIR, 2, XD]), ALU.mult), n)
                        s.drained(n)
                        ins = V.tensor_tensor(xt[:, t, :], xt[:, t, :], xo[:, :], ALU.add)
                        if t < T - 1:
                            link(ins)
                        else:
                            done(ins, "x2_ready")
                    s.wait("x2_ready", g + 1)
                    norm_rows(3, g)
                    n = f"route.{g}"
                    o = s.filled(n)
                    rv = route[:, :, :].rearrange("p (b t) e -> p b t e", b=B)
                    free(V.tensor_tensor(rv[:, b, g * T:(g + 1) * T, :],
                                         o[:, 0:T * E].rearrange("p (t e) -> p t e", t=T),
                                         prm("lb").unsqueeze(1).broadcast_to([P, T, E]), ALU.add), n)
                    if g == 0:
                        link(V.tensor_copy(pre[:, :, 0:CONV - 1], pre[:, :, GT:GT + CONV - 1]))
                        link(V.tensor_copy(vT[:, :, 0:HALO], vT[:, :, GT:GT + HALO]))
                    else:
                        link(V.memset(pre[:, :, 0:CONV - 1], 0.0))
                        link(V.memset(vT[:, :, 0:HALO], 0.0))
                assert steps[0] == DVE_STEPS, steps
            NT = B * G * T
            base = B * DVE_STEPS + DVE_HEAD
            tail = [base]

            def tlink(ins):
                tail[0] += 1
                ins.then_inc(dve_step, 1)
                dve.wait_ge(dve_step, tail[0])

            dve.wait_ge(drained[bank_of["route.1"]], B * fills_per_batch[bank_of["route.1"]] + 1)
            dve.wait_ge(sem("route_scores"), 1)
            gt_ = hsT[:, 0:CK, :].rearrange("p c n -> p (c n)")[:, 0:NT // 2 * E * E // 1]
            big = [kq[:, :, :, :].rearrange("p a b c -> p (a b c)"), delta, None]
            cmp = big[0].rearrange("p (t e f) -> p t e f", t=NT, e=E)
            eqv = attnT[:, :, :].rearrange("p a b -> p (a b)").rearrange("p (t e f) -> p t e f", t=NT, e=E)
            ce = coef[:, :, :].unsqueeze(3).broadcast_to([P, NT, E, E])
            cf = coef[:, :, :].unsqueeze(2).broadcast_to([P, NT, E, E])
            tlink(V.tensor_tensor(cmp, cf, ce, ALU.is_gt))
            tlink(V.tensor_tensor(eqv, cf, ce, ALU.is_equal))
            tlink(V.tensor_tensor(eqv.rearrange("p t e f -> p t (e f)"), eqv.rearrange("p t e f -> p t (e f)"),
                                  cst("before").unsqueeze(1).broadcast_to([P, NT, E * E]), ALU.mult))
            tlink(V.tensor_tensor(cmp, cmp, eqv, ALU.add))
            rank = xo[:, :].rearrange("p (t e) -> p t e", t=NT)
            sel = delta[:, 0, :].rearrange("p (t e) -> p t e", t=NT)
            selw = delta[:, 1, :].rearrange("p (t e) -> p t e", t=NT)
            den = delta[:, 2, 0:NT]
            tlink(V.tensor_reduce(rank, cmp, AX.X, ALU.add))
            tlink(V.tensor_scalar(sel, rank, 2.0, None, ALU.is_lt))
            tlink(V.tensor_tensor(selw, sel, coef[:, :, :], ALU.mult))
            tlink(V.tensor_reduce(den, selw, AX.X, ALU.add))
            tlink(V.tensor_scalar(delta[:, 2, NT:2 * NT], den, 1e-8, None, ALU.add))
            tlink(V.reciprocal(delta[:, 2, 2 * NT:3 * NT], delta[:, 2, NT:2 * NT]))
            tlink(V.tensor_tensor(selw, selw, delta[:, 2, 2 * NT:3 * NT].unsqueeze(2).broadcast_to([P, NT, E]),
                                  ALU.mult))
            sums = gw[:, 0, :, :].rearrange("p t k -> p (t k)")
            tlink(V.tensor_reduce(sums[:, 0:E], selw.rearrange("p t e -> p e t"), AX.X, ALU.add))
            V.tensor_reduce(sums[:, E:2 * E], sel.rearrange("p t e -> p e t"), AX.X, ALU.add)\
                .then_inc(sem("route_sums"), 1)
            dve.wait_ge(sem("route_total"), 1)
            tot = gw[:, 1, :, :].rearrange("p t k -> p (t k)")
            tlink(V.tensor_scalar(tot[:, 0:E], banks[0][:, E:2 * E], 1.0, None, ALU.max))
            tlink(V.reciprocal(tot[:, E:2 * E], tot[:, 0:E]))
            wm = gw[:, 2, :, :].rearrange("p t k -> p (t k)")
            tlink(V.tensor_tensor(wm[:, 0:E], banks[0][:, 0:E], tot[:, E:2 * E], ALU.mult))
            V.tensor_tensor(coef[:, :, :], sel, wm[:, 0:E].unsqueeze(1).broadcast_to([P, NT, E]), ALU.mult)\
                .then_inc(sem("coef_ready"), 1)
            dve.wait_ge(sem("coef_ready"), 1)
            with dve.Fori(0, B) as b:
                cv_ = coef[:, :, :].rearrange("p (b t) e -> p b t e", b=B)
                for g in range(G):
                    acc = facc[g]
                    dve.wait_ge(sem("fx_loaded"), b * 64 + 32 * g + 32)

                    def product(e):
                        k = b * (G * ES) + g * ES + e
                        dve.wait_ge(sem("ff_silu"), k + 1)
                        dve.wait_ge(sem("ff_up"), k + 1)
                        kd = b * (G * 9) + g * 9
                        dve.wait_ge(sem("ff_y"), kd + (e if e >= 2 else 1))
                        V.tensor_tensor(fh[e % 2], banks[2 + e % 2][:, :], fg[e % 2], ALU.mult)\
                            .then_inc(sem("ff_h_ready"), 1)

                    def gather(slot):
                        k = b * (G * 9) + g * 9 + slot
                        dve.wait_ge(sem("ff_y"), k + 2)
                        if slot:
                            dve.wait_ge(sem("ff_y_used"), k + 1)
                        for i in range(2):
                            o = banks[4 + 2 * ((g * 9 + slot) % 2) + i]
                            if slot == E:
                                last = V.tensor_tensor(acc[:, 2 * i:2 * i + 2, :], acc[:, 2 * i:2 * i + 2, :],
                                                       o[:, :].rearrange("p (t d) -> p t d", t=2), ALU.add)
                            else:
                                for j in range(2):
                                    t = 2 * i + j
                                    last = V.scalar_tensor_tensor(acc[:, t, :], o[:, j * D:(j + 1) * D],
                                                                  cv_[:, b, g * T + t, slot:slot + 1], acc[:, t, :],
                                                                  ALU.mult, ALU.add)
                        last.then_inc(sem("ff_y_used"), 1)

                    product(0)
                    for e in range(1, ES):
                        product(e)
                        if e - 1 < E:
                            gather(e - 1)
                    gather(E)

        wrong = {n: (SIGNALS.get(n), c) for n, c in counted.items() if SIGNALS.get(n) != c and n != "route_logits"}
        assert not wrong, wrong


DVE_STEPS = 268


def constants():
    c = np.zeros((P, NCONST), np.float32)
    p, q = np.arange(P)[:, None], np.arange(P)[None, :]

    def put(name, v):
        a, z = CONST[name]
        c[:, a:z] = v

    put("ident", p == q)
    put("lower", q < p)
    put("upper", p <= q)
    for s in LEVELS:
        put(f"level{s}", (p // (2 * s) == q // (2 * s)) & (p // s % 2 == 1) & (q // s % 2 == 0))
    put("eye64", p % DH == q[:, :DH])
    put("headsel", p // DH == q[:, :2])
    put("mean_s", (p % DH == q) / H)
    put("mean_l", (p % DH == q - DH) / H)
    put("ones", 1.0)
    put("head16", p // XD == q[:, :8])
    put("eye32", p % 32 == q[:, :32])
    e, f = np.arange(E)[:, None], np.arange(E)[None, :]
    put("before", (f < e).reshape(1, -1))
    return c


def kernel(**inputs):
    import concourse.bacc as _bacc
    from concourse import mybir as _mybir
    from concourse.bass_utils import run_bass_kernel_spmd as _run

    a = {n: np.asarray(v) for n, v in inputs.items()}
    f = np.float32

    def rows(w):
        wt = np.ascontiguousarray(w.T)
        n = wt.shape[0] // P
        return wt.reshape(n, P, -1).transpose(1, 0, 2).reshape(P, -1)

    def cols(v):
        v = v.reshape(CK, P, -1)
        return v.transpose(1, 0, 2).reshape(P, -1)

    def spread(v):
        return np.broadcast_to(v.reshape(1, -1), (P, v.size))

    pre = "L0_attn_"
    conv = np.concatenate([cols(a[pre + n + "_conv_w"]) for n in ("k", "q", "v")], axis=1)
    param = np.concatenate([
        conv, cols(a[pre + "fir_short_w"].reshape(D, FS)), cols(a[pre + "fir_long_w"].reshape(D, FL)),
        cols(a[pre + "fg_b1"]), cols(a["L0_xattn_bq"]), cols(a["L0_xattn_bk"]), spread(a["L0_xattn_bv"]),
        spread(a[pre + "fg_b2"]), spread(a["L0_ffn_lb_bias"]), spread(a[pre + "logit_temp"]),
        np.concatenate([a[pre + "o_norm_w"]] * 2).reshape(P, 1)], axis=1)
    w1 = a[pre + "fg_w1"]
    w1p = np.concatenate([w1, np.zeros((D, DH), f)], axis=1)
    weight = np.concatenate([
        rows(a[pre + "k_proj_w"]), rows(a[pre + "q_proj_w"]), rows(a[pre + "v_proj_w"]), rows(a[pre + "b_proj_w"]),
        rows(w1p), rows(a[pre + "fg_w2"]), rows(a[pre + "o_proj_w"]), rows(a["L0_xattn_Wq"]),
        rows(a["L0_xattn_Wk"]), rows(a["L0_xattn_Wv"]), rows(a["L0_ffn_gate_w"])], axis=1)
    ff = "L0_ffn_"
    gates = list(a[ff + "expert_gate_w"]) + list(a[ff + "shared_gate_w"].reshape(2, EI, D))
    ups = list(a[ff + "expert_up_w"]) + list(a[ff + "shared_up_w"].reshape(2, EI, D))
    sd = a[ff + "shared_down_w"]
    downs = list(a[ff + "expert_down_w"]) + [sd[:, :EI], sd[:, EI:]]
    ffn = np.stack([np.concatenate([rows(g), rows(u), rows(d)], axis=1) for g, u, d in zip(gates, ups, downs)], axis=1)
    ctx = a["ctx_1024"].transpose(0, 2, 1).reshape(B, CK, P, S2).transpose(0, 2, 1, 3)
    ctx = np.concatenate([ctx, ctx], axis=3)
    pad = a["mask_Bx1x1xS2_ik0"].reshape(B, S2)
    sub = a["mask_1x1xSxS2_ik0"].reshape(L, S2)
    feeds = {
        "x": a["x"], "ctxT": ctx, "pad_row": np.broadcast_to(pad[:, None, :], (B, P, S2)),
        "pad_col": pad.reshape(B, S2, 1), "sub": sub, "subT": sub.T, "const": constants(),
        "param": param, "weight": weight, "ffn": ffn,
    }
    nc = _bacc.Bacc("TRN2", target_bir_lowering=False, num_devices=1)
    arrays, aps = {}, []
    for n, v in feeds.items():
        v = np.ascontiguousarray(v)
        arrays[n + "_in"] = v
        aps.append(nc.dram_tensor(n + "_in", v.shape, _mybir.dt.from_np(v.dtype), kind="ExternalInput").ap())
    out = nc.dram_tensor("y", (B, L, D), _mybir.dt.float32, kind="ExternalOutput").ap()
    x2 = nc.dram_tensor("x2", (B, G, P, T, D), _mybir.dt.float32, kind="Internal").ap()
    xnT = nc.dram_tensor("xnT", (B, G, P, CK, GT), _mybir.dt.float32, kind="Internal").ap()
    decoder(nc, *aps, out, x2, xnT)
    r = _run(nc, [arrays], core_ids=[0])
    return r.results[0]["y"]
```

```python
from contextlib import ExitStack

import numpy as np

import concourse.bass as bass
from concourse import mybir

ALU = mybir.AluOpType
ACT = mybir.ActivationFunctionType
AX = mybir.AxisListType
F32 = mybir.dt.float32
BF16 = mybir.dt.bfloat16
I32 = mybir.dt.int32

P = 128
B, L, D = 4, 1024, 256
G = 2
GT = L // G
T = GT // P
H, DH = 4, 64
HT = T * H
CK = D // P
CONV, FS, FL = 4, 3, 31
HALO = FL - 1
XH, XD, S2 = 16, 16, 64
NPAIR = XH // 2
E, EI = 8, 128
ES = 10
NEG = -1.0e9
MIN_LOCAL = 0.05
LEVELS = (1, 2, 4, 8, 16, 32, 64)


def columns(spec):
    at, out = 0, {}
    for name, width in spec:
        out[name] = (at, at + width)
        at += width
    return out, at


CONST, NCONST = columns([("ident", P), ("lower", P), ("upper", P)] + [(f"level{s}", P) for s in LEVELS]
                        + [("eye64", DH), ("headsel", 2), ("mean_s", P), ("mean_l", P), ("ones", P),
                           ("head16", 8), ("eye32", 32), ("before", E * E)])
PARAM, NPARAM = columns([("conv", 6 * CONV), ("fir_s", CK * FS), ("fir_l", CK * FL), ("fg_b1", CK),
                         ("bq", CK), ("bk", CK), ("bv", D), ("fg_b2", 4), ("lb", E), ("temp", 1), ("onorm", 1)])
WEIGHT, NWEIGHT = columns([("k", CK * D), ("q", CK * D), ("v", CK * D), ("beta", CK * H), ("fg1", 4 * D),
                           ("fg2", CK * 4), ("o", CK * D), ("route", CK * E), ("xq", CK * D), ("xk", CK * D),
                           ("xv", CK * D)])


DVE_MAIN = (112, 112)
DVE_CROSS = (24, 20)
MAIN_BANKS, CROSS_BANKS = (0, 1, 2, 3), (4, 5, 6, 7)


def psum_plan():
    plan = []

    def ring(names, banks):
        for i, n in enumerate(names):
            plan.append((n, banks[i % len(banks)]))

    for g in range(G):
        names = ["hsT0", "hsT1"] + [f"proj{j}" for j in range(6)] + ["stat"]
        names += [f"kv{t}" for t in range(T)]
        ring([f"{n}.{g}" for n in names], MAIN_BANKS)
        ring([f"gram{t}{i}.{g}" for t in range(T) for i in range(2)], MAIN_BANKS)
        names = ["P1"]
        for s in LEVELS[1:5]:
            names += [f"P{s}", f"D{s}"]
        names += ["P32a", "P32b", "R32a", "R32b", "T32a", "T32b", "P64a", "P64b", "R64a", "R64b"]
        names += [f"uw{t}" for t in range(T)] + [f"wa{t}" for t in range(T)]
        for t in range(T):
            names += [f"state{t}", f"out{t}0", f"out{t}1"]
        names += ["gm", "dmT", "h1a", "h1b", "logit"] + [f"sl{t}" for t in range(T)]
        names += ["oT0", "oT1", "oproj0", "oproj1"]
        ring([f"{n}.{g}" for n in names], MAIN_BANKS)
        names = ["kx", "vx"] if g == 0 else []
        names += ["any", "x1T0", "x1T1", "qx0", "qx1"]
        names += [f"sx{t}{c}" for t in range(T) for c in range(CK)]
        names += ["mxT"]
        ring([f"{n}.{g}" for n in names], CROSS_BANKS)
        for u in range(2):
            ring([f"sT{u}{j}.{g}" for j in range(NPAIR // 2)], CROSS_BANKS[0:2])
            ring([f"pv{2 * u + i}.{g}" for i in range(2)], CROSS_BANKS[2:4])
        ring([f"{n}.{g}" for n in ("x2T0", "x2T1", "route")], CROSS_BANKS)
    bank = dict(plan)
    seen = [0] * 8
    index = {}
    for n, k in plan:
        index[n] = seen[k]
        seen[k] += 1
    return bank, index, seen


SIGNALS = {
    "x0_loaded": 16, "x1_loaded": 16, "hs_stats_ready": 2, "hs_rstd_ready": 2, "hs_rows_ready": 2,
    "conv_ready": 12, "act_ready": 12, "squares_ready": 2, "rnorm_ready": 2,
    "fir_done": 4, "level_ready": 14, "rows_ready": 16, "compact_ready": 10,
    "blocks_ready": 10, "blocks_cleared": 4, "delta_ready": 8, "exp_ready": 2, "gate_ready": 4, "mix_ready": 2,
    "osq_ready": 2, "oms_ready": 2, "orms_ready": 2, "on_ready": 2,
    "ctx_loaded": 16 * 3, "x_stats_ready": 4, "x_rstd_ready": 4, "x_rows_ready": 4,
    "mask_ready": 2, "kblk_ready": 1, "nmx_ready": 2, "pv_used": 12, "x2_ready": 2, "x2_stored": 64,
}


def decoder(nc, x, ctxT, pad_row, pad_col, sub, subT, const_d, param_d, weight_d, ffn_d, out, x2_d, xnT_d):
    bank_of, fill_index, fills_per_batch = psum_plan()
    es = ExitStack()
    with es:
        def sb(name, shape, dt=F32):
            return es.enter_context(nc.sbuf_tensor(name, shape, dt))

        sems = {}

        def sem(name):
            if name not in sems:
                sems[name] = es.enter_context(nc.semaphore(name))
            return sems[name]

        banks = [es.enter_context(nc.psum_tensor(f"bank{i}", [P, 512], F32)) for i in range(8)]
        filled = [sem(f"bank{i}_filled") for i in range(8)]
        drained = [sem(f"bank{i}_drained") for i in range(8)]

        const = sb("const", [P, NCONST])
        param = sb("param", [P, NPARAM])
        wt = sb("wt", [P, NWEIGHT])

        def cst(n, rows=slice(0, P)):
            return const[rows, CONST[n][0]:CONST[n][1]]

        def prm(n, i=0, w=None):
            a = PARAM[n][0] + i
            return param[:, a:(a + w) if w else PARAM[n][1]]

        def wgt(n, c, width):
            a = WEIGHT[n][0] + c * width
            return wt[:, a:a + width]

        ident_b = sb("ident_b", [P, P], BF16)
        ones_b = sb("ones_b", [P, P], BF16)
        aug_lhs = sb("aug_lhs", [P, NPAIR, P], BF16)
        minus_half = sb("minus_half", [P, 16])
        eps = sb("eps", [P, 2, 8])
        rtemp = sb("rtemp", [P, 8])

        xt = sb("xt", [P, G, T, D])
        spare = sb("spare", [P, 1])
        xn, stats, mv, rstd = ([sb(f"{n}_{i}", [P, T] + w) for i in ("hs", "x")]
                               for n, w in (("xn", [D]), ("stats", [6]), ("mv", [2]), ("rstd", [])))
        hsT = sb("hsT", [P, CK, GT])
        pre = sb("pre", [P, 6, CONV - 1 + GT])
        cv = sb("cv", [P, 2, GT])
        kq = sb("kq", [P, 2, 2, GT])
        vT = sb("vT", [P, CK, HALO + GT])
        lng = sb("lng", [P, CK, GT])
        sht = sb("sht", [P, CK, GT])
        st = sb("st", [P, T, 12])
        rn = sb("rn", [P, T, 8])
        beta = sb("beta", [P, T, H])
        rb = sb("rb", [P, T, H])
        sc = sb("sc", [P, T, H])
        kvt = sb("kvt", [P, T, 512])
        Y = sb("Y", [P, HT, P])
        A = sb("A", [P, HT, P])
        attnT = sb("attnT", [P, HT, P])
        Bl = sb("Bl", [P, 2, HT, P])
        sq = Bl[:, 1, :, :].rearrange("p (a c) d -> p a (c d)", a=4)
        Tf = sb("Tf", [P, HT, P])
        Rf = sb("Rf", [P, HT, P])
        Rc = sb("Rc", [P, HT, 32])
        Tc = sb("Tc", [P, HT, 32])
        Pc = sb("Pc", [P, HT, 32])
        UW = sb("UW", [P, HT, P])
        Pf = UW
        QeT = kq[:, :, 1, :]
        MT = sb("MT", [P, T, 2, DH])
        S = sb("S", [P, 2, 2, DH])
        delta = sb("delta", [P, T, D])
        gmT = A[:, 0:4, :].rearrange("p a b -> p (a b)")
        dm = sb("dm", [P, T, DH])
        dmT = A[0:DH, 4:8, :].rearrange("p a b -> p (a b)")
        h1T = A[:, 8:16, :].rearrange("p (c a) b -> p c (a b)", c=CK)
        gw = sb("gw", [P, 8, T, 4])
        gs = sb("gs", [P, 4, T])
        om = attnT[:, 0:8, :].rearrange("p (t a) b -> p t (a b)", t=T)
        oss = sb("oss", [P, HT])
        orn = sb("orn", [P, HT])
        osq = cv[:, :, :].rearrange("p a b -> p (a b)").rearrange("p (t d) -> p t d", t=T)
        xnT = sb("x_T", [P, CK, GT])
        qx = sb("qx", [P, CK, GT])
        PT = sb("PT", [P, 2, GT])
        abc = sb("abc", [P, GT])
        Kblk = sb("Kblk", [P, CK, 8, S2])
        kxT = sb("kxT", [P, CK, S2])
        Va = sb("Va", [P, NPAIR + 2, 34])
        ctx = sb("ctx", [P, CK, P])
        padr = sb("padr", [P, S2], I32)
        padc = sb("padc", [S2, 1], I32)
        subi = Y[:, 0:4, :].bitcast(I32).rearrange("p a (b k) -> p (a b) k", k=S2)
        subTi = Y[0:S2, 4:12, :].bitcast(I32).rearrange("p a b -> p (a b)")
        sub01 = sb("sub01", [P, L // P, S2], BF16)
        subT01 = sb("subT01", [S2, L], BF16)
        pr01 = sb("pr01", [P, S2])
        pc01 = sb("pc01", [S2, 1])
        mbf = sb("mbf", [P, L // P, S2], BF16)
        mb = sb("mb", [P, L // P, S2], BF16)
        mT = sb("mT", [S2, GT], BF16)
        aug = sb("aug", [P, GT], BF16)
        nmx = sb("nmx", [P, 2, T, XH])
        nmb = sb("nmb", [P, T, 3 * XH], BF16)
        rden = sb("rden", [P, T, NPAIR, 2])
        xo = sb("xo", [P, D])
        route = sb("route", [P, B * G * T, E])

        plus = (lambda b, per, k: b * per + k)

        def window(M, at, width=96):
            return M.rearrange("p a b -> p (a b)")[:, at:at + width]

        PRIMED = {"kblk_ready": 1, "blocks_cleared": 1, "x2_stored": 16}
        counted = {}

        class Signals:

            def __init__(self, eng, b):
                self.eng, self.b = eng, b

            def wait(self, name, k):
                self.eng.wait_ge(sem(name), plus(self.b, SIGNALS[name], k + PRIMED.get(name, 0)))

            def filled(self, name):
                k = bank_of[name]
                self.eng.wait_ge(filled[k], plus(self.b, fills_per_batch[k], fill_index[name] + 1))
                return banks[k]

            def drained(self, name):
                k = bank_of[name]
                self.eng.wait_ge(drained[k], plus(self.b, fills_per_batch[k], fill_index[name] + 1 + 1))

            def bank_free(self, name):
                k = bank_of[name]
                self.eng.wait_ge(drained[k], plus(self.b, fills_per_batch[k], fill_index[name] + 1))
                return banks[k]

        def full(ins, name):
            ins.then_inc(filled[bank_of[name]], 1)

        def free(ins, name):
            ins.then_inc(drained[bank_of[name]], 1)

        def done(ins, name, n=1):
            counted[name] = counted.get(name, 0) + n
            ins.then_inc(sem(name), n)

        w_loaded = sem("weights_loaded")
        setup_dve = sem("setup_dve")
        setup_pool = sem("setup_pool")
        ffn_loaded = sem("ffn_weights_loaded")
        N_DVE_SETUP, N_POOL_SETUP = 12, 12

        class Steps:

            def __init__(self, eng, name, per_group):
                self.eng, self.sem, self.per = eng, sem(name), per_group

            def at(self, b, g):
                self.b, self.g, self.k = b, g, 0

            def step(self, ins):
                self.k += 1
                ins.then_inc(self.sem, 1)
                return self.k

            def after(self, k):
                self.eng.wait_ge(self.sem, plus(self.b, sum(self.per), sum(self.per[:self.g]) + k))

            def link(self, ins):
                self.after(self.step(ins))

            def end(self):
                assert self.k == self.per[self.g], (self.sem, self.g, self.k)

        block = es.enter_context(nc.Block())

        class Idle:

            def __getitem__(self, name):
                return lambda: None

        idle = Idle()

        def pipeline(eng, main, cross):
            main(0, 0, idle)
            with eng.Fori(0, B - 1) as b:
                main(b, 1, cross(b, 0))
                main(b + 1, 0, cross(b, 1))
            main(B - 1, 1, cross(B - 1, 0))
            for piece in cross(B - 1, 1).values():
                piece()


        ffw = [Bl[:, 0, :, :], Bl[:, 1, :, :], Tf[:, :, :], Rf[:, :, :], UW[:, :, :]]
        ffw = [a.rearrange("p a b -> p (a b)") for a in ffw]

        def expert_flat(e):
            k, i = divmod(e, 2)
            return ffw[k][:, i * 768:(i + 1) * 768]

        def expert(e):
            base = expert_flat(e)
            return (base[:, 0:256].rearrange("p (c n) -> p c n", c=2),
                    base[:, 256:512].rearrange("p (c n) -> p c n", c=2), base[:, 512:768])

        fx = [Y[:, 0:8, :].rearrange("p (c a) b -> p c (a b)", c=CK),
              Y[:, 8:16, :].rearrange("p (c a) b -> p c (a b)", c=CK)]
        facc = [xt[:, 0, :, :], xt[:, 1, :, :]]
        fg = [kvt[:, i, :] for i in range(2)]
        fh = [kvt[:, 2 + i, :] for i in range(2)]
        coef = sb("coef", [P, B * G * T, E])


        @block.sync
        def _(sp):
            sp.dma_start(const[:, :], const_d).then_inc(w_loaded, 16)
            sp.dma_start(param[:, :], param_d).then_inc(w_loaded, 16)
            sp.dma_start(wt[:, :], weight_d).then_inc(w_loaded, 16)
            sp.dma_start(subi, sub.rearrange("(t p) k -> p t k", p=P)).then_inc(w_loaded, 16)
            sp.dma_start(subTi, subT).then_inc(w_loaded, 16)

            def load_rows(b, g):
                done(sp.dma_start(xt[:, g, :, :], x[b, g * GT:(g + 1) * GT, :]
                                  .rearrange("(t p) d -> p t d", p=P)), f"x{g}_loaded", 16)

            def load_context(b):
                done(sp.dma_start(ctx[:, :, :], ctxT[b, :, :, :]), "ctx_loaded", 16)
                done(sp.dma_start(padr[:, :], pad_row[b, :, :]), "ctx_loaded", 16)
                done(sp.dma_start(padc[:, :], pad_col[b, :, :]), "ctx_loaded", 16)

            def store_rows(b, g):
                s = Signals(sp, b)
                s.wait("x2_ready", g + 1)
                done(sp.dma_start(x2_d[b, g, :, :, :], xt[:, g, :, :]), "x2_stored", 16)
                s.drained(f"x2T0.{g}")
                s.drained(f"x2T1.{g}")
                done(sp.dma_start(xnT_d[b, g, :, :, :], xnT[:, :, :]), "x2_stored", 16)
                s.wait("x2_stored", 32 * (g + 1))

            for g in range(G):
                load_rows(0, g)
            load_context(0)
            with sp.Fori(0, B - 1) as b:
                store_rows(b, 0)
                load_rows(b + 1, 0)
                Signals(sp, b).wait("kblk_ready", 1)
                load_context(b + 1)
                store_rows(b, 1)
                load_rows(b + 1, 1)
            s = Signals(sp, B - 1)
            s.drained("oproj1.1")
            s.wait("blocks_cleared", 4)
            for e in range(ES):
                sp.dma_start(expert_flat(e), ffn_d[:, e, :]).then_inc(ffn_loaded, 16)
            store_rows(B - 1, 0)
            store_rows(B - 1, 1)
            with sp.Fori(0, B) as b:
                for g in range(G):
                    sp.wait_ge(sem("y_stored"), b * 32 + 16 * g + 16)
                    sp.dma_start(fx[g], xnT_d[b, g, :, :, :]).then_inc(sem("fx_loaded"), 16)
                    sp.dma_start(facc[g], x2_d[b, g, :, :, :]).then_inc(sem("fx_loaded"), 16)
                    sp.wait_ge(sem("ff_y_used"), b * (G * 9) + g * 9 + 9 + 1)
                    sp.dma_start(out[b, g * GT:(g + 1) * GT, :].rearrange("(t p) d -> p t d", p=P),
                                 facc[g]).then_inc(sem("y_stored"), 16)
            sp.wait_ge(sem("y_stored"), B * G * 16 + 16)

        @block.tensor
        def _(pe):
            mm, tr = pe.matmul, pe.transpose
            ident = cst("ident")
            pe.wait_ge(w_loaded, 16 * 5)
            pe.wait_ge(setup_dve, N_DVE_SETUP)
            pe.wait_ge(setup_pool, N_POOL_SETUP)

            def transpose_rows(s, src, names):
                for c in range(CK):
                    o = s.bank_free(names[c])
                    for t in range(T):
                        last = tr(o[:, t * P:(t + 1) * P], src[:, t, c * P:(c + 1) * P], ident)
                    full(last, names[c])

            def near(M, at, room):
                return M[:, at:at + min(96, room)]

            def cross(b, g):
                s = Signals(pe, b)

                def context():
                    if g:
                        return
                    s.wait("ctx_loaded", 48)
                    n = f"kx.{g}"
                    o = s.bank_free(n)
                    for m in range(CK):
                        for c in range(CK):
                            last = mm(o[:, m * S2:m * S2 + P], wgt("xk", c, D)[:, m * P:(m + 1) * P],
                                      ctx[:, c, :], start=c == 0, stop=c == CK - 1)
                    full(last, n)
                    n = f"vx.{g}"
                    o = s.bank_free(n)
                    for c in range(CK):
                        last = mm(o[:, 0:D], ctx[:, c, :], wgt("xv", c, D), start=c == 0, stop=c == CK - 1)
                    full(last, n)

                def rows():
                    n = f"any.{g}"
                    o = s.bank_free(n)
                    s.wait("mask_ready", g + 1)
                    full(mm(o[:, :], ones_b[0:S2, :], mT[:, :], start=True, stop=True), n)
                    s.wait("x_rows_ready", 2 * g + 1)
                    transpose_rows(s, xn[1], [f"x1T0.{g}", f"x1T1.{g}"])

                def queries():
                    s.drained(f"x1T0.{g}")
                    s.drained(f"x1T1.{g}")
                    for m in range(CK):
                        n = f"qx{m}.{g}"
                        o = s.bank_free(n)
                        for c in range(CK):
                            last = mm(o[:, :], wgt("xq", c, D)[:, m * P:(m + 1) * P], xnT[:, c, :],
                                      start=c == 0, stop=c == CK - 1)
                        full(last, n)

                def masked_scores(t):
                    def piece():
                        if t == 0:
                            s.drained(f"qx0.{g}")
                            s.drained(f"qx1.{g}")
                            s.wait("kblk_ready", 1)
                        for c in range(CK):
                            n = f"sx{t}{c}.{g}"
                            o = s.bank_free(n)
                            ov = o[:, :].rearrange("p (h k) -> p h k", h=8)
                            mm(ov, qx[:, c, t * P:(t + 1) * P], Kblk[:, c, :, :], start=True, stop=False)
                            full(mm(ov, ident_b[:, :], mb[:, g * T + t, :].unsqueeze(1).broadcast_to([P, 8, S2]),
                                    start=False, stop=True), n)
                    return piece

                def maxima():
                    n = f"mxT.{g}"
                    o = s.bank_free(n)
                    s.wait("nmx_ready", g + 1)
                    for t in range(T):
                        last = mm(o[64:112, t * P:(t + 1) * P], nmb[:, t, :], ident_b[:, :], start=True, stop=True)
                    full(last, n)

                def scores(u, j):
                    n = f"sT{u}{j}.{g}"
                    o = s.bank_free(n)
                    if u == 0 and j == 0:
                        s.drained(f"mxT.{g}")
                    uu = slice(u * GT // 2, (u + 1) * GT // 2)
                    for i in range(2):
                        c, k = divmod(2 * j + i, 4)
                        oo = o[:, i * GT // 2:(i + 1) * GT // 2]
                        lhs = Kblk[:, c, 2 * k:2 * k + 2, :].rearrange("p a b -> p (a b)")
                        mm(oo, lhs, qx[:, c, uu], start=True, stop=False)
                        last = mm(oo, aug_lhs[0:112, 2 * j + i, :], aug[0:112, uu], start=False, stop=True)
                    full(last, n)

                def values(u, j):
                    def piece():
                        if j == 0:
                            scores(u, 0)
                        if j < NPAIR // 2 - 1:
                            scores(u, j + 1)
                        s.drained(f"sT{u}{j}.{g}")
                        if u == 0 and j == 0:
                            s.drained("vx.0")
                        for i in range(2):
                            at = (2 * j + i) * 34
                            for k in range(2):
                                n = f"pv{2 * u + k}.{g}"
                                o = s.bank_free(n) if i == j == 0 else banks[bank_of[n]]
                                last = mm(o[:, at:at + 96], PT[:, j % 2, (2 * i + k) * P:(2 * i + k + 1) * P],
                                          window(Va[:, :, :], at), start=True, stop=True)
                                if i == 1 and j == NPAIR // 2 - 1:
                                    full(last, n)
                    return piece

                def routing():
                    s.wait("x_rows_ready", 2 * g + 2)
                    transpose_rows(s, xn[1], [f"x2T0.{g}", f"x2T1.{g}"])
                    s.drained(f"x2T0.{g}")
                    s.drained(f"x2T1.{g}")
                    n = f"route.{g}"
                    o = s.bank_free(n)
                    at = WEIGHT["route"][0]
                    for t in range(T):
                        for c in range(CK):
                            last = mm(o[:, t * E:t * E + 96], xnT[:, c, t * P:(t + 1) * P],
                                      wt[:, at + c * E:at + c * E + 96], start=c == 0, stop=c == CK - 1)
                    full(last, n)

                x = {"context": context, "rows": rows, "queries": queries}
                for t in range(T):
                    x["scores", t] = masked_scores(t)
                x["maxima"] = maxima
                for u in range(2):
                    for j in range(NPAIR // 2):
                        x["values", u, j] = values(u, j)
                x["routing"] = routing
                return x

            def main(b, g, x):
                s = Signals(pe, b)
                s.wait("hs_rows_ready", g + 1)
                transpose_rows(s, xn[0], [f"hsT0.{g}", f"hsT1.{g}"])
                s.drained(f"hsT0.{g}")
                s.drained(f"hsT1.{g}")
                for j, w in enumerate(("k", "k", "q", "q", "v", "v")):
                    n = f"proj{j}.{g}"
                    o = s.bank_free(n)
                    for c in range(CK):
                        last = mm(o[:, :], wgt(w, c, D)[:, (j % 2) * P:(j % 2 + 1) * P], hsT[:, c, :],
                                  start=c == 0, stop=c == CK - 1)
                    full(last, n)
                x["context"]()
                x["rows"]()
                x["queries"]()
                n = f"stat.{g}"
                o = s.bank_free(n)
                s.wait("squares_ready", g + 1)
                for t in range(T):
                    tt = slice(t * P, (t + 1) * P)
                    at = CONST["headsel"][0]
                    for i in range(4):
                        a = 2 * (i % 2) + (1 - i // 2)
                        mm(o[:, t * 12 + 2 * i:t * 12 + 2 * i + 96], sq[:, a, tt], const[:, at:at + 96],
                           start=True, stop=True)
                    at = WEIGHT["beta"][0]
                    for c in range(CK):
                        last = mm(o[:, t * 12 + 8:t * 12 + 104], hsT[:, c, tt],
                                  wt[:, at + c * H:at + c * H + 96], start=c == 0, stop=c == CK - 1)
                full(last, n)
                for t in range(T):
                    n = f"kv{t}.{g}"
                    o = s.bank_free(n)
                    tt = slice(t * P, (t + 1) * P)
                    for c in range(CK):
                        tr(o[:, c * P:(c + 1) * P], kq[:, c, 0, tt], ident)
                    s.wait("act_ready", 6 * g + 6)
                    for c in range(CK):
                        last = tr(o[:, (2 + c) * P:(3 + c) * P],
                                  vT[:, c, HALO + t * P:HALO + (t + 1) * P], ident)
                    full(last, n)
                for t in range(T):
                    for r in range(2):
                        n = f"gram{t}{r}.{g}"
                        o = s.bank_free(n)
                        for i in range(2):
                            rr = slice(DH * r, DH * r + DH)
                            last = mm(o[:, i * 2 * P:(i + 1) * 2 * P], kq[rr, i, 0, t * P:(t + 1) * P],
                                      kq[rr, i, :, t * P:(t + 1) * P], start=True, stop=True)
                        full(last, n)
                lv = 7 * g
                n = f"P1.{g}"
                o = s.bank_free(n)
                s.wait("level_ready", lv + 1)
                at = CONST["eye32"][0]
                for h in range(HT):
                    w_ = min(96, 512 - h * 32)
                    last = mm(o[:, h * 32:h * 32 + w_], Bl[:, 0, h, :], const[:, at:at + w_], start=True, stop=True)
                full(last, n)
                x["scores", 0]()
                for i, size in enumerate(LEVELS[1:5]):
                    n = f"P{size}.{g}"
                    o = s.bank_free(n)
                    s.wait("level_ready", lv + 2 + i)
                    if i == 0:
                        s.drained(f"P1.{g}")
                    else:
                        s.drained(f"D{LEVELS[i]}.{g}")
                    for h in range(HT):
                        w_ = min(96, 512 - h * 32)
                        last = mm(o[:, h * 32:h * 32 + w_], Bl[:, (i + 1) % 2, h, :],
                                  window(Rc[:, :, :], h * 32, w_), start=True, stop=True)
                    full(last, n)
                    s.drained(n)
                    s.wait("blocks_ready", 5 * g + i + 1)
                    s.wait("blocks_cleared", 2 * g)
                    n = f"D{size}.{g}"
                    o = s.bank_free(n)
                    for h in range(HT):
                        w_ = min(96, 512 - h * 32)
                        last = mm(o[:, h * 32:h * 32 + w_], Tf[:, h, :], window(Pc[:, :, :], h * 32, w_),
                                  start=True, stop=True)
                    full(last, n)
                    if i < 3:
                        x["scores", i + 1]()
                x["maxima"]()
                s.wait("blocks_ready", 5 * g + 5)
                halves = [("a", 0), ("b", 8)]
                s.wait("level_ready", lv + 6)

                def quarter(M, h, h_end, a):
                    w_ = min(3, 2 * (h_end - h))
                    return M.rearrange("p h (q c) -> p (h q) c", q=2)[:, 2 * h:2 * h + w_, 32 * a:32 * a + 32]

                for i, (x_, h0) in enumerate(halves):
                    n = f"P32{x_}.{g}"
                    o = s.bank_free(n)
                    for h in range(8):
                        w_ = min(96, 512 - h * 64)
                        last = mm(o[:, h * 64:h * 64 + w_], Bl[:, 1, h0 + h, :],
                                  quarter(Rf[:, :, :], h0 + h, h0 + 8, 1), start=True, stop=True)
                    full(last, n)
                x["values", 0, 0]()
                for i, (x_, h0) in enumerate(halves):
                    s.drained(f"P32{x_}.{g}")
                    n = f"R32{x_}.{g}"
                    o = s.bank_free(n)
                    for h in range(8):
                        w_ = min(96, 512 - h * 64)
                        last = mm(o[:, h * 64:h * 64 + w_], Tf[:, h0 + h, :],
                                  quarter(Pf[:, :, :], h0 + h, h0 + 8, 1), start=True, stop=True)
                    full(last, n)
                x["values", 0, 1]()
                for i, (x_, h0) in enumerate(halves):
                    n = f"T32{x_}.{g}"
                    o = s.bank_free(n)
                    for h in range(8):
                        w_ = min(96, 512 - h * 64)
                        last = mm(o[:, h * 64:h * 64 + w_], Pf[:, h0 + h, :],
                                  quarter(Tf[:, :, :], h0 + h, h0 + 8, 0), start=True, stop=True)
                    full(last, n)
                    x["values", 0, 2 + i]()
                s.wait("level_ready", lv + 7)
                for x_, h0 in halves:
                    s.drained(f"R32{x_}.{g}")
                    n = f"P64{x_}.{g}"
                    o = s.bank_free(n)
                    for h in range(8):
                        w_ = min(96, 512 - h * 64)
                        last = mm(o[:, h * 64:h * 64 + w_], Bl[:, 0, h0 + h, :],
                                  window(Rf[:, :, :], (h0 + h) * P + 64, w_), start=True, stop=True)
                    full(last, n)
                for x_, h0 in halves:
                    s.drained(f"P64{x_}.{g}")
                    s.drained(f"T32{x_}.{g}")
                    n = f"R64{x_}.{g}"
                    o = s.bank_free(n)
                    for h in range(8):
                        w_ = min(96, 512 - h * 64)
                        last = mm(o[:, h * 64:h * 64 + w_], Tf[:, h0 + h, :],
                                  window(Pf[:, :, :], (h0 + h) * P + 64, w_), start=True, stop=True)
                    full(last, n)
                    x["values", 1, 0 if x_ == "a" else 1]()
                s.wait("rows_ready", 8 * g + 8)
                for t in range(T):
                    if t % 2 == 0:
                        s.drained(f"R64{'ab'[t // 2]}.{g}")
                    n = f"uw{t}.{g}"
                    o = s.bank_free(n)
                    for h in range(H):
                        last = mm(o[:, h * P:(h + 1) * P], Rf[:, t * H + h, :], Y[:, t * H + h, :],
                                  start=True, stop=True)
                    full(last, n)
                x["values", 1, 2]()
                for t in range(T):
                    s.drained(f"uw{t}.{g}")
                    n = f"wa{t}.{g}"
                    o = s.bank_free(n)
                    for h in range(H):
                        r, i = h % 2, h // 2
                        w_ = UW[:, t * H + h, 64:128]
                        mm(o[DH * r:DH * r + DH, i * P:(i + 1) * P], w_, attnT[:, t * H + h, :],
                           start=True, stop=True)
                        last = mm(o[DH * r:DH * r + DH, 256 + i * DH:256 + (i + 1) * DH], w_,
                                  kvt[:, t, h * DH:(h + 1) * DH], start=True, stop=True)
                    full(last, n)
                x["values", 1, 3]()
                for t in range(T):
                    s.drained(f"wa{t}.{g}")
                    if t > 0:
                        s.drained(f"state{t - 1}.{g}")
                    first = t == 0 and g == 0
                    n = f"state{t}.{g}"
                    o = s.bank_free(n)
                    for h in range(H):
                        rr, i = slice(DH * (h % 2), DH * (h % 2) + DH), h // 2
                        cc = slice(i * DH, (i + 1) * DH)
                        last = mm(o[rr, cc], kvt[:, t, h * DH:(h + 1) * DH], UW[:, t * H + h, 0:64],
                                  start=True, stop=first)
                        if not first:
                            last = mm(o[rr, cc], MT[rr, t, i, :], S[rr, t % 2, i, :], start=False, stop=True)
                    full(last, n)
                    for r in range(2):
                        n = f"out{t}{r}.{g}"
                        o = s.bank_free(n)
                        rr = slice(DH * r, DH * r + DH)
                        for i in range(2):
                            h = 2 * i + r
                            cc = slice(i * DH, (i + 1) * DH)
                            last = mm(o[:, i * DH:i * DH + P], attnT[:, t * H + h, :], UW[:, t * H + h, :],
                                      start=True, stop=first)
                            if not first:
                                last = mm(o[:, cc], QeT[rr, i, t * P:(t + 1) * P], S[rr, t % 2, i, :],
                                          start=False, stop=True)
                        full(last, n)
                n = f"gm.{g}"
                o = s.bank_free(n)
                s.wait("fir_done", 2 * g + 2)
                for i in range(4):
                    src = (sht, lng)[i // 2]
                    last = mm(o[:, :], cst(("mean_s", "mean_l")[i // 2]), src[:, i % 2, :],
                              start=i == 0, stop=i == 3)
                full(last, n)
                n = f"dmT.{g}"
                o = s.bank_free(n)
                s.wait("delta_ready", 4 * g + 4)
                for t in range(T):
                    last = mm(o[0:DH, t * P:(t + 1) * P], dm[:, t, :], ident, start=True, stop=True)
                full(last, n)
                s.drained(f"gm.{g}")
                s.drained(f"dmT.{g}")
                for m in range(CK):
                    n = f"h1{'ab'[m]}.{g}"
                    o = s.bank_free(n)
                    for i in range(4):
                        rhs = (hsT[:, 0, :], hsT[:, 1, :], gmT[:, :], dmT[:, :])[i]
                        k_ = DH if i == 3 else P
                        last = mm(o[:, :], wgt("fg1", i, D)[0:k_, m * P:(m + 1) * P], rhs,
                                  start=i == 0, stop=i == 3)
                    full(last, n)
                s.drained(f"h1a.{g}")
                s.drained(f"h1b.{g}")
                at = WEIGHT["fg2"][0]
                n = f"logit.{g}"
                o = s.bank_free(n)
                for t in range(T):
                    for c in range(CK):
                        last = mm(o[:, t * 4:t * 4 + 96], h1T[:, c, t * P:(t + 1) * P],
                                  wt[:, at + c * 4:at + c * 4 + 96], start=c == 0, stop=c == CK - 1)
                full(last, n)
                for t in range(T):
                    n = f"sl{t}.{g}"
                    o = s.bank_free(n)
                    for i in range(4):
                        last = tr(o[:, i * P:(i + 1) * P], (sht, lng)[i // 2][:, i % 2, t * P:(t + 1) * P], ident)
                    full(last, n)
                x["routing"]()
                s.wait("on_ready", g + 1)
                transpose_rows(s, om, [f"oT0.{g}", f"oT1.{g}"])
                s.drained(f"oT0.{g}")
                s.drained(f"oT1.{g}")
                for i in range(2):
                    n = f"oproj{i}.{g}"
                    o = s.bank_free(n)
                    for j in range(2):
                        t = 2 * i + j
                        for c in range(CK):
                            last = mm(o[:, j * D:(j + 1) * D], h1T[:, c, t * P:(t + 1) * P], wgt("o", c, D),
                                      start=c == 0, stop=c == CK - 1)
                    full(last, n)

            pipeline(pe, main, cross)
            pe.wait_ge(sem("route_sums"), 1)
            mm(banks[0][:, 0:2 * E], cst("ones"), gw[:, 0, :, :].rearrange("p t k -> p (t k)"),
               start=True, stop=True).then_inc(sem("route_total"), 1)
            pe.wait_ge(ffn_loaded, 16 * ES)
            pe.wait_ge(sem("coef_ready"), 1)
            with pe.Fori(0, B) as b:
                for g in range(G):
                    pe.wait_ge(sem("fx_loaded"), b * 64 + 32 * g + 32)

                    def hidden(e):
                        k = b * (G * ES) + g * ES + e
                        wg_, wu_, _ = expert(e)
                        pe.wait_ge(sem("ff_h_ready"), k if (g or e > 1) else b * (G * ES) + 1)
                        for c in range(CK):
                            last = mm(banks[e % 2][:, :], wg_[:, c, :], fx[g][:, c, :], start=c == 0, stop=c == CK - 1)
                        last.then_inc(sem("ff_gate"), 1)
                        for c in range(CK):
                            last = mm(banks[2 + e % 2][:, :], wu_[:, c, :], fx[g][:, c, :],
                                      start=c == 0, stop=c == CK - 1)
                        last.then_inc(sem("ff_up"), 1)

                    def down(e, srcs, slot):
                        pe.wait_ge(sem("ff_h_ready"), b * (G * ES) + g * ES + e + 2)
                        k = b * (G * 9) + g * 9 + slot
                        pe.wait_ge(sem("ff_y_used"), k if (g or slot > 1) else b * (G * 9) + 1)
                        for i in range(2):
                            o = banks[4 + 2 * ((g * 9 + slot) % 2) + i]
                            for j in range(2):
                                t = 2 * i + j
                                for q_, e_ in enumerate(srcs):
                                    last = mm(o[:, j * D:(j + 1) * D], fh[e_ % 2][:, t * P:(t + 1) * P], expert(e_)[2],
                                              start=q_ == 0, stop=q_ == len(srcs) - 1)
                        last.then_inc(sem("ff_y"), 1)

                    hidden(0)
                    for e in range(1, ES):
                        hidden(e)
                        if e - 1 < E:
                            down(e - 1, [e - 1], e - 1)
                    down(ES - 1, [ES - 2, ES - 1], E)

        @block.scalar
        def _(act):
            act.wait_ge(w_loaded, 16 * 5)
            act.wait_ge(setup_dve, N_DVE_SETUP)
            act.wait_ge(setup_pool, N_POOL_SETUP)
            act.activation(rtemp[:, 1:2], rtemp[:, 0:1], ACT.Exp, scale=-1.0).then_inc(sem("temp_exp"), 1)
            act.wait_ge(sem("temp_exp"), 1)
            act.activation(rtemp[:, 2:3], rtemp[:, 1:2], ACT.Ln, bias=cst("ones")[:, 0:1]).then_inc(sem("temp_ln"), 1)

            def evac(out_, in_, name, func=ACT.Copy, **kw):
                free(act.activation(out_, in_, func, **kw), name)

            def cross(b, g):
                s = Signals(act, b)

                def rows():
                    if g == 0:
                        n = f"kx.{g}"
                        o = s.filled(n)
                        for m in range(CK):
                            last = act.activation(kxT[:, m, :], o[:, m * S2:(m + 1) * S2], ACT.Identity,
                                                  bias=prm("bk", m, 1))
                        free(last, n)
                    for c in range(CK):
                        n = f"x1T{c}.{g}"
                        o = s.filled(n)
                        s.wait("x2_stored", 32 * g)
                        evac(xnT[:, c, :], o[:, :], n)

                def probs(u, j):
                    def piece():
                        n = f"sT{u}{j}.{g}"
                        o = s.filled(n)
                        evac(PT[:, j % 2, :], o[:, :], n, ACT.Exp)
                    return piece

                def routing():
                    for c in range(CK):
                        n = f"x2T{c}.{g}"
                        o = s.filled(n)
                        evac(xnT[:, c, :], o[:, :], n)

                x = {"rows": rows}
                for u in range(2):
                    for j in range(NPAIR // 2):
                        x["probs", u, j] = probs(u, j)
                x["routing"] = routing
                return x

            def main(b, g, x):
                s = Signals(act, b)
                for c in range(CK):
                    n = f"hsT{c}.{g}"
                    o = s.filled(n)
                    evac(hsT[:, c, :], o[:, :], n)
                for j in range(6):
                    n = f"proj{j}.{g}"
                    o = s.filled(n)
                    if j == 0:
                        s.wait("hs_rstd_ready", g + 1)
                    evac(pre[:, j, CONV - 1:], o[:, :], n)
                x["rows"]()
                for j in range(6):
                    s.wait("conv_ready", 6 * g + j + 1)
                    dst = kq[:, j % 2, j // 2, :] if j < 4 else vT[:, j % 2, HALO:]
                    done(act.activation(dst, cv[:, j % 2, :], ACT.Silu), "act_ready")
                n = f"stat.{g}"
                o = s.filled(n)
                ov = o[:, 0:T * 12].rearrange("p (t k) -> p t k", t=T)
                act.activation(st[:, :, 0:8], ov[:, :, 0:8], ACT.Copy)
                evac(st[:, :, 8:12], ov[:, :, 8:12], n, ACT.Tanh, scale=0.5)
                for t in range(T):
                    n = f"kv{t}.{g}"
                    o = s.filled(n)
                    evac(kvt[:, t, :], o[:, :], n)

                def spread(dst, src, n):
                    for r in range(4):
                        rr = slice(32 * r, 32 * r + 32)
                        last = act.activation(dst[rr, :, rr], src[rr, :, :], ACT.Copy)
                    done(last, n)

                for i, size in enumerate(LEVELS[1:5]):
                    s.wait("compact_ready", 5 * g + i + 1)
                    spread(Tf, Tc, "blocks_ready")
                    n = f"P{size}.{g}"
                    o = s.filled(n)
                    evac(Pc[:, :, :], o[:, :].rearrange("p (h k) -> p h k", k=32), n)
                s.drained(f"D16.{g}")
                for r in range(4):
                    rr = slice(32 * r, 32 * r + 32)
                    act.activation(Rf[rr, :, rr], Rc[rr, :, :], ACT.Copy)
                s.wait("compact_ready", 5 * g + 5)
                spread(Tf, Tc, "blocks_ready")
                view = lambda M, h0: M[:, h0:h0 + 8, :].rearrange("p h (a c) -> p h a c", a=2)
                for x_, h0 in (("a", 0), ("b", 8)):
                    n = f"P32{x_}.{g}"
                    o = s.filled(n)
                    evac(view(Pf, h0)[:, :, :, 32:64],
                         o[:, :].rearrange("p (h a c) -> p h a c", h=8, a=2), n)
                for j in range(NPAIR // 2):
                    x["probs", 0, j]()
                for x_, h0 in (("a", 0), ("b", 8)):
                    n = f"P64{x_}.{g}"
                    o = s.filled(n)
                    s.filled(f"T32{x_}.{g}")
                    evac(Pf[:, h0:h0 + 8, 64:128], o[:, :].rearrange("p (h c) -> p h c", h=8), n)
                for j in range(2):
                    x["probs", 1, j]()
                for t in range(T):
                    n = f"uw{t}.{g}"
                    o = s.filled(n)
                    if t == 0:
                        s.filled(f"R64a.{g}")
                        s.filled(f"R64b.{g}")
                    evac(UW[:, t * H:(t + 1) * H, :], o[:, :].rearrange("p (h c) -> p h c", h=H), n)
                for j in range(2, 4):
                    x["probs", 1, j]()
                for t in range(T):
                    n = f"state{t}.{g}"
                    o = s.filled(n)
                    if t > 0:
                        s.filled(f"out{t - 1}1.{g}")
                    evac(S[:, (t + 1) % 2, :, :], o[:, 0:P].rearrange("p (i c) -> p i c", i=2), n)
                n = f"gm.{g}"
                o = s.filled(n)
                evac(gmT[:, :], o[:, :], n)
                n = f"dmT.{g}"
                o = s.filled(n)
                evac(dmT[:, :], o[0:DH, :], n, scale=1.0 / H)
                for m in range(CK):
                    n = f"h1{'ab'[m]}.{g}"
                    o = s.filled(n)
                    evac(h1T[:, m, :], o[:, :], n, ACT.Gelu, bias=prm("fg_b1", m, 1))
                s.drained(f"logit.{g}")
                s.wait("gate_ready", 2 * g + 1)
                done(act.activation(gw[:, 1, :, :], gw[:, 0, :, :], ACT.Exp), "exp_ready")
                x["routing"]()
                for c in range(CK):
                    n = f"oT{c}.{g}"
                    o = s.filled(n)
                    evac(h1T[:, c, :], o[:, :], n)

            pipeline(act, main, cross)
            act.wait_ge(drained[bank_of["route.1"]], B * fills_per_batch[bank_of["route.1"]] + 1)
            act.activation(coef[:, :, :], route[:, :, :], ACT.Sigmoid).then_inc(sem("route_scores"), 1)
            with act.Fori(0, B) as b:
                for g in range(G):
                    for e in range(ES):
                        k = b * (G * ES) + g * ES + e
                        act.wait_ge(sem("ff_gate"), k + 1)
                        act.wait_ge(sem("ff_h_ready"), k if (g or e > 1) else b * (G * ES) + 1)
                        act.activation(fg[e % 2], banks[e % 2][:, :], ACT.Silu).then_inc(sem("ff_silu"), 1)

        @block.gpsimd
        def _(pool):
            n_setup = [0]

            def once(ins):
                n_setup[0] += 1
                ins.then_inc(setup_pool, 1)
                pool.wait_ge(setup_pool, n_setup[0])

            once(pool.memset(minus_half[:, :], -0.5))
            once(pool.memset(eps[:, 0, :], 1e-5))
            once(pool.memset(eps[:, 1, :], 1e-12))
            once(pool.memset(Tf[:, :, :], 0.0))
            once(pool.memset(Rf[:, :, :], 0.0))
            once(pool.memset(pre[:, :, :], 0.0))
            once(pool.memset(vT[:, :, :], 0.0))
            once(pool.memset(Va[:, :, :], 0.0))
            once(pool.memset(UW[:, :, :], 0.0))
            once(pool.memset(Va[0:64, :, 32:33], 1.0))
            once(pool.memset(Va[64:128, :, 33:34], 1.0))
            once(pool.memset(aug[:, :], 0.0))
            assert n_setup[0] == N_POOL_SETUP
            for k in range(8):
                pool.sem_inc(drained[k], 1)
            for n in ("ff_h_ready", "ff_y", "ff_y_used"):
                pool.sem_inc(sem(n), 1)
            for n in ("kblk_ready", "blocks_cleared", "x2_stored"):
                pool.sem_inc(sem(n), PRIMED[n])
            pool.sem_inc(sem("y_stored"), 16)
            pool.wait_ge(setup_dve, N_DVE_SETUP)
            own, own_x = Steps(pool, "pool_step", (2, 2)), Steps(pool, "pool_cross_step", (2, 2))

            def norm_scale(s, chain, i, tag, k):
                s.wait(f"{tag}_stats_ready", k)
                chain.link(pool.tensor_tensor(rstd[i][:, :], mv[i][:, :, 1], eps[:, 0, 0:T], ALU.add))
                done(pool.tensor_tensor(rstd[i][:, :], rstd[i][:, :], minus_half[:, 0:T], ALU.pow),
                     f"{tag}_rstd_ready")

            def cross(b, g):
                s = Signals(pool, b)
                own_x.at(b, g)

                def norm2():
                    norm_scale(s, own_x, 1, "x", 2 * g + 1)

                def norm3():
                    norm_scale(s, own_x, 1, "x", 2 * g + 2)
                    own_x.end()

                return {"norm2": norm2, "norm3": norm3}

            def main(b, g, x):
                s = Signals(pool, b)
                own.at(b, g)
                norm_scale(s, own, 0, "hs", g + 1)
                x["norm2"]()
                s.wait("act_ready", 6 * g + 4)
                done(pool.tensor_tensor(sq, kq[:, :, :, :].rearrange("p a b c -> p (a b) c"),
                                        kq[:, :, :, :].rearrange("p a b c -> p (a b) c"), ALU.mult),
                     "squares_ready")
                s.drained(f"stat.{g}")
                own.link(pool.tensor_tensor(rn[:, :, :], st[:, :, 0:8],
                                        eps[:, 1, 0:8].unsqueeze(1).broadcast_to([P, T, 8]), ALU.add))
                done(pool.tensor_tensor(rn[:, :, :], rn[:, :, :],
                                        minus_half[:, 0:8].unsqueeze(1).broadcast_to([P, T, 8]), ALU.pow),
                     "rnorm_ready")
                for i, size in enumerate(LEVELS):
                    s.wait("rows_ready", 8 * g + 4)
                    if i >= 2:
                        s.filled(f"P{LEVELS[i - 2]}{'b' if LEVELS[i - 2] > 16 else ''}.{g}")
                    done(pool.tensor_tensor(Bl[:, i % 2, :, :], A[:, :, :],
                                            cst(f"level{size}").unsqueeze(1).broadcast_to([P, HT, P]),
                                            ALU.mult), "level_ready")
                s.drained(f"uw0.{g}")
                for a in range(2):
                    rr, cc = slice(64 * a + 32, 64 * a + 64), slice(64 * a, 64 * a + 32)
                    zero = cst("upper", rr)[:, cc].unsqueeze(1).broadcast_to([32, HT, 32])
                    done(pool.tensor_tensor(Tf[rr, :, cc], zero, zero, ALU.mult), "blocks_cleared")
                    s.wait("blocks_cleared", 2 * g + a + 1)
                x["norm3"]()
                s.wait("mix_ready", g + 1)
                done(pool.tensor_tensor(osq, om[:, :, :], om[:, :, :], ALU.mult), "osq_ready")
                s.wait("oms_ready", g + 1)
                done(pool.tensor_tensor(orn[:, :], oss[:, :], minus_half[:, 0:HT], ALU.pow), "orms_ready")
                own.end()

            pipeline(pool, main, cross)

        @block.vector
        def _(dve):
            V = dve
            dve.wait_ge(w_loaded, 16 * 5)
            n_setup = [0]

            def once(ins):
                n_setup[0] += 1
                ins.then_inc(setup_dve, 1)
                dve.wait_ge(setup_dve, n_setup[0])

            once(V.tensor_copy(ident_b[:, :], cst("ident")))
            once(V.tensor_copy(ones_b[:, :], cst("ones")))
            once(V.tensor_copy(aug_lhs[0:S2, :, :].rearrange("p j (a k) -> p (j a) k", a=2),
                               cst("eye64", slice(0, S2)).unsqueeze(1).broadcast_to([S2, XH, S2])))
            once(V.memset(aug_lhs[64:128, :, :], 0.0))
            once(V.tensor_copy(aug_lhs[64:112, :, :].rearrange("p j (a k) -> p (j a) k", a=2),
                               cst("eye64", slice(64, 112))[:, 0:XH].unsqueeze(2).broadcast_to([48, XH, S2])))
            for part in (1, 2):
                once(V.tensor_tensor(aug_lhs[64:112, :, :].rearrange("p j (a k) -> p (j a) k", a=2),
                                     aug_lhs[64:112, :, :].rearrange("p j (a k) -> p (j a) k", a=2),
                                     cst("eye64", slice(64, 112))[:, part * XH:(part + 1) * XH].unsqueeze(2)
                                     .broadcast_to([48, XH, S2]), ALU.add))
            once(V.scalar_tensor_tensor(rtemp[:, 0:1], prm("temp"), -1.0, prm("temp"), ALU.mult, ALU.max))
            for c in range(CK):
                n0 = WEIGHT["o"][0] + c * D
                once(V.tensor_scalar(wt[:, n0:n0 + D], wt[:, n0:n0 + D], prm("onorm"), None, ALU.mult))
            once(V.tensor_scalar(sub01[:, :, :], subi, 0.0, None, ALU.not_equal))
            once(V.tensor_scalar(subT01[:, :], subTi, 0.0, None, ALU.not_equal))
            assert n_setup[0] == N_DVE_SETUP, n_setup
            head, own, own_x = Steps(dve, "dve_head_step", (2,)), Steps(dve, "dve_step", DVE_MAIN), \
                Steps(dve, "dve_cross_step", DVE_CROSS)
            head.at(0, 0)
            dve.wait_ge(sem("temp_ln"), 1)
            head.link(V.scalar_tensor_tensor(rtemp[:, 3:4], prm("temp"), 0.0, rtemp[:, 2:3], ALU.max, ALU.add))
            head.link(V.tensor_scalar(rtemp[:, 4:5], rtemp[:, 3:4], 1e-4, None, ALU.add))
            V.reciprocal(rtemp[:, 5:6], rtemp[:, 4:5]).then_inc(sem("temp_ready"), 1)
            dve.wait_ge(sem("temp_ready"), 1)

            def norm_stats(chain, i, rows, tag):
                for t in range(T):
                    last = chain.step(V.bn_stats(stats[i][:, t, :], rows[:, t, :]))
                chain.after(last)
                V.memset(spare[:, :], 0.0)
                for t in range(T):
                    last = V.bn_aggr(mv[i][:, t, :], stats[i][:, t, :])
                done(last, f"{tag}_stats_ready")

            def norm_rows(s, i, rows, tag, k):
                s.wait(f"{tag}_rstd_ready", k)
                for t in range(T):
                    last = V.tensor_scalar(xn[i][:, t, :], rows[:, t, :], mv[i][:, t, 0:1], rstd[i][:, t:t + 1],
                                           ALU.subtract, ALU.mult)
                done(last, f"{tag}_rows_ready")

            def cross(b, g):
                s = Signals(dve, b)
                step, after, link = own_x.step, own_x.after, own_x.link
                own_x.at(b, g)
                rows = xt[:, g, :, :]

                def masks():
                    if g == 0:
                        s.wait("ctx_loaded", 48)
                        step(V.tensor_scalar(pr01[:, :], padr[:, :], 0.0, None, ALU.not_equal))
                        link(V.tensor_scalar(pc01[:, :], padc[:, :], 0.0, None, ALU.not_equal))
                        link(V.tensor_tensor(mbf[:, :, :], sub01[:, :, :],
                                             pr01[:, :].unsqueeze(1).broadcast_to([P, L // P, S2]), ALU.mult))
                        step(V.tensor_scalar(mb[:, :, :], mbf[:, :, :], -1.0, -NEG, ALU.add, ALU.mult))
                    link(V.tensor_scalar(mT[:, :], subT01[:, g * GT:(g + 1) * GT], pc01[:, 0:1], None, ALU.mult))
                    done(V.tensor_scalar(aug[0:S2, :], mT[:, :], -1.0, -NEG, ALU.add, ALU.mult), "mask_ready")
                    s.drained(f"oproj0.{g}")
                    s.drained(f"oproj1.{g}")
                    norm_stats(own_x, 1, rows, "x")

                def rows2():
                    norm_rows(s, 1, rows, "x", 2 * g + 1)

                def anykey():
                    n = f"any.{g}"
                    o = s.filled(n)
                    free(V.tensor_scalar(abc[:, :], o[:, :], 1.0, XD ** -0.5, ALU.min, ALU.mult), n)

                def queries():
                    s.drained(f"any.{g}")
                    for m in range(CK):
                        n = f"qx{m}.{g}"
                        o = s.filled(n)
                        free(V.scalar_tensor_tensor(qx[:, m, :], o[:, :], prm("bq", m, 1), abc[:, :],
                                                    ALU.add, ALU.mult), n)

                def context():
                    if g:
                        return
                    n = f"vx.{g}"
                    o = s.filled(n)
                    for r in range(2):
                        rr = slice(64 * r, 64 * r + 64)
                        vv = o[rr, 0:D].rearrange("p (j r c) -> p j r c", r=2, c=XD)[:, :, r, :]
                        bb = prm("bv")[rr, :].rearrange("p (j r c) -> p j r c", r=2, c=XD)[:, :, r, :]
                        last = V.tensor_tensor(Va[rr, 0:NPAIR, XD * r:XD * (r + 1)], vv, bb, ALU.add)
                    free(last, n)
                    s.drained(f"kx.{g}")
                    for c in range(CK):
                        last = V.tensor_tensor(Kblk[:, c, :, :], kxT[:, c, :].unsqueeze(1).broadcast_to([P, 8, S2]),
                                               cst("head16").unsqueeze(2).broadcast_to([P, 8, S2]), ALU.mult)
                    done(last, "kblk_ready")

                def maxima(t):
                    def piece():
                        for c in range(CK):
                            n = f"sx{t}{c}.{g}"
                            o = s.filled(n)
                            free(V.tensor_reduce(nmx[:, 0, t, 8 * c:8 * c + 8],
                                                 o[:, :].rearrange("p (h k) -> p h k", h=8),
                                                 AX.X, ALU.max, negate=True), n)
                    return piece

                def parts():
                    s.drained(f"sx30.{g}")
                    s.drained(f"sx31.{g}")
                    link(V.tensor_copy(nmb[:, :, 0:16], nmx[:, 0, :, :]))
                    link(V.tensor_tensor(nmx[:, 1, :, :], nmx[:, 0, :, :], nmb[:, :, 0:16], ALU.subtract))
                    link(V.tensor_copy(nmb[:, :, 16:32], nmx[:, 1, :, :]))
                    link(V.tensor_tensor(nmx[:, 0, :, :], nmx[:, 1, :, :], nmb[:, :, 16:32], ALU.subtract))
                    done(V.tensor_copy(nmb[:, :, 32:48], nmx[:, 0, :, :]), "nmx_ready")
                    n = f"mxT.{g}"
                    o = s.filled(n)
                    free(V.tensor_copy(aug[64:112, :], o[64:112, :]), n)

                def values(u):
                    def piece():
                        for t in (2 * u, 2 * u + 1):
                            n = f"pv{t}.{g}"
                            o = s.filled(n)
                            ov = o[:, 0:NPAIR * 34].rearrange("p (j c) -> p j c", c=34)
                            link(V.reciprocal(rden[:, t, :, :], ov[:, :, 32:34]))
                            free(V.tensor_tensor(xo[:, :].rearrange("p (j r c) -> p j r c", r=2, c=XD),
                                                 ov[:, :, 0:32].rearrange("p j (r c) -> p j r c", r=2),
                                                 rden[:, t, :, :].unsqueeze(3).broadcast_to([P, NPAIR, 2, XD]),
                                                 ALU.mult), n)
                            s.drained(n)
                            ins = V.tensor_tensor(rows[:, t, :], rows[:, t, :], xo[:, :], ALU.add)
                            if t < T - 1:
                                link(ins)
                            else:
                                done(ins, "x2_ready")
                        if u:
                            s.wait("x2_ready", g + 1)
                            norm_stats(own_x, 1, rows, "x")
                    return piece

                def rows3():
                    norm_rows(s, 1, rows, "x", 2 * g + 2)

                def routing():
                    n = f"route.{g}"
                    o = s.filled(n)
                    rv = route[:, :, :].rearrange("p (b t) e -> p b t e", b=B)
                    free(V.tensor_tensor(rv[:, b, g * T:(g + 1) * T, :],
                                         o[:, 0:T * E].rearrange("p (t e) -> p t e", t=T),
                                         prm("lb").unsqueeze(1).broadcast_to([P, T, E]), ALU.add), n)
                    own_x.end()

                x = {"masks": masks, "rows2": rows2, "context": context, "anykey": anykey, "queries": queries}
                for t in range(T):
                    x["maxima", t] = maxima(t)
                x.update({"parts": parts, ("values", 0): values(0), ("values", 1): values(1),
                          "rows3": rows3, "routing": routing})
                return x

            def main(b, g, x):
                s = Signals(dve, b)
                step, after, link = own.step, own.after, own.link
                own.at(b, g)
                rows = xt[:, g, :, :]
                fir_k = {}

                def fir(g, lo, hi):
                    for j in range(lo, hi):
                        for c in range(CK):
                            w_ = param[:, PARAM["fir_l"][0] + c * FL + j:PARAM["fir_l"][0] + c * FL + j + 1]
                            src = vT[:, c, j:j + GT]
                            if j == 0:
                                k = step(V.tensor_scalar(lng[:, c, :], src, w_, None, ALU.mult))
                            else:
                                after(fir_k[c])
                                ins = V.scalar_tensor_tensor(lng[:, c, :], src, w_, lng[:, c, :], ALU.mult, ALU.add)
                                k = step(ins)
                            fir_k[c] = k

                def fir_short(g):
                    for j in range(FS):
                        for c in range(CK):
                            w_ = param[:, PARAM["fir_s"][0] + c * FS + j:PARAM["fir_s"][0] + c * FS + j + 1]
                            src = vT[:, c, FL - FS + j:FL - FS + j + GT]
                            if j == 0:
                                fir_k["s", c] = step(V.tensor_scalar(sht[:, c, :], src, w_, None, ALU.mult))
                            else:
                                after(fir_k["s", c])
                                ins = V.scalar_tensor_tensor(sht[:, c, :], src, w_, sht[:, c, :], ALU.mult, ALU.add)
                                if j < FS - 1:
                                    fir_k["s", c] = step(ins)
                                else:
                                    done(ins, "fir_done")

                s.wait(f"x{g}_loaded", 16)
                norm_stats(own, 0, rows, "hs")
                x["masks"]()
                norm_rows(s, 0, rows, "hs", g + 1)
                x["rows2"]()
                for j in range(6):
                    s.drained(f"proj{j}.{g}")
                    if j >= 2:
                        s.wait("act_ready", 6 * g + j - 1)
                    cw = lambda i: param[:, PARAM["conv"][0] + j * CONV + i:PARAM["conv"][0] + j * CONV + i + 1]
                    link(V.tensor_scalar(cv[:, j % 2, :], pre[:, j, 0:GT], cw(0), None, ALU.mult))
                    for i in range(1, CONV):
                        ins = V.scalar_tensor_tensor(cv[:, j % 2, :], pre[:, j, i:i + GT], cw(i),
                                                     cv[:, j % 2, :], ALU.mult, ALU.add)
                        if i < CONV - 1:
                            link(ins)
                    done(ins, "conv_ready")
                    if j == 0:
                        x["context"]()
                    if j == 1:
                        x["anykey"]()
                    if j == 3:
                        x["queries"]()
                s.wait("act_ready", 6 * g + 6)
                fir(g, 0, 4)
                s.drained(f"stat.{g}")
                link(V.tensor_scalar(beta[:, :, :], st[:, :, 8:12], 1.0, 0.5, ALU.add, ALU.mult))
                s.wait("rnorm_ready", g + 1)
                link(V.tensor_tensor(rb[:, :, :], beta[:, :, :], rn[:, :, 4:8], ALU.mult))
                link(V.tensor_tensor(sc[:, :, :], rb[:, :, :], rn[:, :, 4:8], ALU.mult))
                for t in range(T):
                    for r in range(2):
                        n = f"gram{t}{r}.{g}"
                        o = s.filled(n)
                        ov = o[:, :].rearrange("p (i a c) -> p i a c", i=2, a=2)
                        for i in range(2):
                            h = t * H + 2 * i + r
                            V.scalar_tensor_tensor(A[:, h, :], ov[:, i, 0, :], sc[:, t, 2 * i + r:2 * i + r + 1],
                                                   cst("lower"), ALU.mult, ALU.mult)
                        free(V.tensor_tensor(attnT[:, t * H + r:(t + 1) * H:2, :], ov[:, :, 1, :],
                                             cst("upper").unsqueeze(1).broadcast_to([P, 2, P]), ALU.mult), n)
                for t in range(T):
                    s.drained(f"kv{t}.{g}")
                    hh = slice(t * H, (t + 1) * H)
                    ins = V.tensor_tensor(Y[:, hh, 0:64], kvt[:, t, 256:512].rearrange("p (h c) -> p h c", h=H),
                                          rb[:, t, :].unsqueeze(2).broadcast_to([P, H, DH]), ALU.mult)
                    done(ins, "rows_ready")
                    ins = V.tensor_tensor(Y[:, hh, 64:128], kvt[:, t, 0:256].rearrange("p (h c) -> p h c", h=H),
                                          sc[:, t, :].unsqueeze(2).broadcast_to([P, H, DH]), ALU.mult)
                    done(ins, "rows_ready")
                n = f"P1.{g}"
                o = s.filled(n)
                free(V.tensor_tensor(Rc[:, :, :], cst("eye32").unsqueeze(1).broadcast_to([P, HT, 32]),
                                     o[:, :].rearrange("p (h k) -> p h k", k=32), ALU.subtract), n)
                s.drained(n)
                done(V.transpose(Tc[:, :, :].rearrange("p h k -> p (h k)"),
                                 Rc[:, :, :].rearrange("p h k -> p (h k)")), "compact_ready")
                x["maxima", 0]()
                for i, size in enumerate(LEVELS[1:5]):
                    fir(g, 4 + 4 * i, 8 + 4 * i)
                    n = f"D{size}.{g}"
                    o = s.filled(n)
                    free(V.tensor_tensor(Rc[:, :, :], Rc[:, :, :],
                                         o[:, :].rearrange("p (h k) -> p h k", k=32), ALU.subtract), n)
                    s.drained(n)
                    s.wait("blocks_ready", 5 * g + i + 1)
                    done(V.transpose(Tc[:, :, :].rearrange("p h k -> p (h k)"),
                                     Rc[:, :, :].rearrange("p h k -> p (h k)")), "compact_ready")
                    if i < 3:
                        x["maxima", i + 1]()
                x["parts"]()
                fir(g, 20, 24)
                view = lambda M, h0: M[:, h0:h0 + 8, :].rearrange("p h (a c) -> p h a c", a=2)
                for x_, h0 in (("a", 0), ("b", 8)):
                    n = f"R32{x_}.{g}"
                    o = s.filled(n)
                    for a in range(2):
                        rr = slice(64 * a, 64 * a + 32)
                        last = V.tensor_scalar(Rf[rr, h0:h0 + 8, 64 * a + 32:64 * a + 64],
                                               o[rr, :].rearrange("p (h a c) -> p h a c", h=8, a=2)[:, :, a, :],
                                               -1.0, None, ALU.mult)
                    free(last, n)
                for x_, h0 in (("a", 0), ("b", 8)):
                    n = f"T32{x_}.{g}"
                    o = s.filled(n)
                    for a in range(2):
                        rr = slice(64 * a + 32, 64 * a + 64)
                        last = V.tensor_scalar(Tf[rr, h0:h0 + 8, 64 * a:64 * a + 32],
                                               o[rr, :].rearrange("p (h a c) -> p h a c", h=8, a=2)[:, :, a, :],
                                               -1.0, None, ALU.mult)
                    free(last, n)
                x["values", 0]()
                fir(g, 24, 28)
                for x_, h0 in (("a", 0), ("b", 8)):
                    n = f"R64{x_}.{g}"
                    o = s.filled(n)
                    free(V.tensor_scalar(Rf[0:64, h0:h0 + 8, 64:128], o[0:64, :].rearrange("p (h c) -> p h c", h=8),
                                         -1.0, None, ALU.mult), n)
                fir(g, 28, FL)
                fir_short(g)
                for t in range(T):
                    n = f"wa{t}.{g}"
                    o = s.filled(n)
                    V.tensor_tensor(QeT[:, :, t * P:(t + 1) * P], kq[:, :, 1, t * P:(t + 1) * P],
                                    o[:, 0:256].rearrange("p (i c) -> p i c", i=2), ALU.subtract)
                    free(V.tensor_tensor(MT[:, t, :, :], cst("eye64").unsqueeze(1).broadcast_to([P, 2, DH]),
                                         o[:, 256:384].rearrange("p (i c) -> p i c", i=2), ALU.subtract), n)
                x["values", 1]()
                for t in range(T):
                    for r in range(2):
                        n = f"out{t}{r}.{g}"
                        o = s.filled(n)
                        free(V.tensor_tensor(delta[:, t, :].rearrange("p (i r c) -> p i r c", i=2, r=2)[:, :, r, :],
                                             o[:, 0:P].rearrange("p (i c) -> p i c", i=2),
                                             rn[:, t, r:4:2].unsqueeze(2).broadcast_to([P, 2, DH]), ALU.mult), n)
                    s.drained(f"out{t}0.{g}")
                    s.drained(f"out{t}1.{g}")
                    done(V.tensor_reduce(dm[:, t, :], delta[:, t, :].rearrange("p (h c) -> p c h", h=H),
                                         AX.X, ALU.add), "delta_ready")
                n = f"logit.{g}"
                o = s.filled(n)
                free(V.tensor_tensor(gw[:, 2, :, :], o[:, 0:T * 4].rearrange("p (t k) -> p t k", t=T),
                                     prm("fg_b2").unsqueeze(1).broadcast_to([P, T, 4]), ALU.add), n)
                s.drained(n)
                link(V.tensor_scalar(gw[:, 3, :, :], gw[:, 2, :, :], rtemp[:, 5:6], None, ALU.mult))
                link(V.tensor_reduce(gs[:, 0, :], gw[:, 3, :, :], AX.X, ALU.max))
                done(V.tensor_tensor(gw[:, 0, :, :], gw[:, 3, :, :],
                                     gs[:, 0, :].unsqueeze(2).broadcast_to([P, T, 4]), ALU.subtract), "gate_ready")
                x["rows3"]()
                s.wait("exp_ready", g + 1)
                link(V.tensor_reduce(gs[:, 1, :], gw[:, 1, :, :], AX.X, ALU.add))
                link(V.reciprocal(gs[:, 2, :], gs[:, 1, :]))
                link(V.tensor_tensor(gw[:, 4, :, :], gw[:, 1, :, :],
                                     gs[:, 2, :].unsqueeze(2).broadcast_to([P, T, 4]), ALU.mult))
                link(V.tensor_scalar(gs[:, 3, :], gw[:, 4, :, 3], MIN_LOCAL, None, ALU.mult))
                step(V.tensor_copy(gw[:, 5, :, 2:4], gw[:, 4, :, 2:4]))
                link(V.tensor_tensor(gw[:, 5, :, 0:2], gw[:, 4, :, 0:2],
                                     gs[:, 3, :].unsqueeze(2).broadcast_to([P, T, 2]), ALU.max))
                link(V.tensor_reduce(gs[:, 1, :], gw[:, 5, :, :], AX.X, ALU.add))
                link(V.reciprocal(gs[:, 2, :], gs[:, 1, :]))
                done(V.tensor_tensor(gw[:, 6, :, :], gw[:, 5, :, :],
                                     gs[:, 2, :].unsqueeze(2).broadcast_to([P, T, 4]), ALU.mult), "gate_ready")
                s.wait("gate_ready", 2 * g + 2)
                ks = []
                for t in range(T):
                    n = f"sl{t}.{g}"
                    o = s.filled(n)
                    ks.append(step(V.tensor_scalar(om[:, t, :], o[:, 0:256], gw[:, 6, t, 0:1], None, ALU.mult)))
                for t in range(T):
                    n = f"sl{t}.{g}"
                    after(ks[t])
                    o = banks[bank_of[n]]
                    free(V.scalar_tensor_tensor(om[:, t, :], o[:, 256:512], gw[:, 6, t, 1:2], om[:, t, :],
                                                ALU.mult, ALU.add), n)
                for t in range(T):
                    s.drained(f"sl{t}.{g}")
                    ks[t] = step(V.scalar_tensor_tensor(om[:, t, :], delta[:, t, :], gw[:, 6, t, 2:3],
                                                        om[:, t, :], ALU.mult, ALU.add))
                for t in range(T):
                    after(ks[t])
                    last = V.scalar_tensor_tensor(om[:, t, :], kvt[:, t, 256:512], gw[:, 6, t, 3:4],
                                                  om[:, t, :], ALU.mult, ALU.add)
                done(last, "mix_ready")
                x["routing"]()
                s.wait("osq_ready", g + 1)
                link(V.tensor_reduce(gw[:, 7, :, :].rearrange("p a b -> p (a b)"),
                                     osq.rearrange("p t (h c) -> p (t h) c", h=H), AX.X, ALU.add))
                done(V.tensor_scalar(oss[:, :], gw[:, 7, :, :].rearrange("p a b -> p (a b)"), 1.0 / DH, 1e-5,
                                     ALU.mult, ALU.add), "oms_ready")
                s.wait("orms_ready", g + 1)
                omv = om[:, :, :].rearrange("p t (h c) -> p (t h) c", h=H)
                done(V.tensor_tensor(omv, omv, orn[:, :].unsqueeze(2).broadcast_to([P, HT, DH]), ALU.mult),
                     "on_ready")
                for i in range(2):
                    n = f"oproj{i}.{g}"
                    o = s.filled(n)
                    dst = rows[:, 2 * i:2 * i + 2, :]
                    free(V.tensor_tensor(dst, dst, o[:, :].rearrange("p (t d) -> p t d", t=2), ALU.add), n)
                if g == 0:
                    link(V.tensor_copy(pre[:, :, 0:CONV - 1], pre[:, :, GT:GT + CONV - 1]))
                    link(V.tensor_copy(vT[:, :, 0:HALO], vT[:, :, GT:GT + HALO]))
                else:
                    link(V.memset(pre[:, :, 0:CONV - 1], 0.0))
                    link(V.memset(vT[:, :, 0:HALO], 0.0))
                own.end()

            pipeline(dve, main, cross)
            NT = B * G * T
            route_chain = Steps(dve, "route_step", (12,))
            route_chain.at(0, 0)
            tlink = route_chain.link

            dve.wait_ge(drained[bank_of["route.1"]], B * fills_per_batch[bank_of["route.1"]] + 1)
            dve.wait_ge(sem("route_scores"), 1)
            cmp = kq[:, :, :, :].rearrange("p a b c -> p (a b c)").rearrange("p (t e f) -> p t e f", t=NT, e=E)
            eqv = attnT[:, :, :].rearrange("p a b -> p (a b)").rearrange("p (t e f) -> p t e f", t=NT, e=E)
            ce = coef[:, :, :].unsqueeze(3).broadcast_to([P, NT, E, E])
            cf = coef[:, :, :].unsqueeze(2).broadcast_to([P, NT, E, E])
            tlink(V.tensor_tensor(cmp, cf, ce, ALU.is_gt))
            tlink(V.tensor_tensor(eqv, cf, ce, ALU.is_equal))
            tlink(V.tensor_tensor(eqv.rearrange("p t e f -> p t (e f)"), eqv.rearrange("p t e f -> p t (e f)"),
                                  cst("before").unsqueeze(1).broadcast_to([P, NT, E * E]), ALU.mult))
            tlink(V.tensor_tensor(cmp, cmp, eqv, ALU.add))
            rank = xo[:, :].rearrange("p (t e) -> p t e", t=NT)
            sel = delta[:, 0, :].rearrange("p (t e) -> p t e", t=NT)
            selw = delta[:, 1, :].rearrange("p (t e) -> p t e", t=NT)
            den = delta[:, 2, 0:NT]
            tlink(V.tensor_reduce(rank, cmp, AX.X, ALU.add))
            tlink(V.tensor_scalar(sel, rank, 2.0, None, ALU.is_lt))
            tlink(V.tensor_tensor(selw, sel, coef[:, :, :], ALU.mult))
            tlink(V.tensor_reduce(den, selw, AX.X, ALU.add))
            tlink(V.tensor_scalar(delta[:, 2, NT:2 * NT], den, 1e-8, None, ALU.add))
            tlink(V.reciprocal(delta[:, 2, 2 * NT:3 * NT], delta[:, 2, NT:2 * NT]))
            tlink(V.tensor_tensor(selw, selw, delta[:, 2, 2 * NT:3 * NT].unsqueeze(2).broadcast_to([P, NT, E]),
                                  ALU.mult))
            sums = gw[:, 0, :, :].rearrange("p t k -> p (t k)")
            tlink(V.tensor_reduce(sums[:, 0:E], selw.rearrange("p t e -> p e t"), AX.X, ALU.add))
            V.tensor_reduce(sums[:, E:2 * E], sel.rearrange("p t e -> p e t"), AX.X, ALU.add)\
                .then_inc(sem("route_sums"), 1)
            dve.wait_ge(sem("route_total"), 1)
            tot = gw[:, 1, :, :].rearrange("p t k -> p (t k)")
            tlink(V.tensor_scalar(tot[:, 0:E], banks[0][:, E:2 * E], 1.0, None, ALU.max))
            tlink(V.reciprocal(tot[:, E:2 * E], tot[:, 0:E]))
            wm = gw[:, 2, :, :].rearrange("p t k -> p (t k)")
            tlink(V.tensor_tensor(wm[:, 0:E], banks[0][:, 0:E], tot[:, E:2 * E], ALU.mult))
            V.tensor_tensor(coef[:, :, :], sel, wm[:, 0:E].unsqueeze(1).broadcast_to([P, NT, E]), ALU.mult)\
                .then_inc(sem("coef_ready"), 1)
            dve.wait_ge(sem("coef_ready"), 1)
            with dve.Fori(0, B) as b:
                cv_ = coef[:, :, :].rearrange("p (b t) e -> p b t e", b=B)
                for g in range(G):
                    acc = facc[g]
                    dve.wait_ge(sem("fx_loaded"), b * 64 + 32 * g + 32)

                    def product(e):
                        k = b * (G * ES) + g * ES + e
                        dve.wait_ge(sem("ff_silu"), k + 1)
                        dve.wait_ge(sem("ff_up"), k + 1)
                        kd = b * (G * 9) + g * 9
                        dve.wait_ge(sem("ff_y"), kd + (e if e >= 2 else 1))
                        V.tensor_tensor(fh[e % 2], banks[2 + e % 2][:, :], fg[e % 2], ALU.mult)\
                            .then_inc(sem("ff_h_ready"), 1)

                    def gather(slot):
                        k = b * (G * 9) + g * 9 + slot
                        dve.wait_ge(sem("ff_y"), k + 2)
                        if slot:
                            dve.wait_ge(sem("ff_y_used"), k + 1)
                        for i in range(2):
                            o = banks[4 + 2 * ((g * 9 + slot) % 2) + i]
                            if slot == E:
                                last = V.tensor_tensor(acc[:, 2 * i:2 * i + 2, :], acc[:, 2 * i:2 * i + 2, :],
                                                       o[:, :].rearrange("p (t d) -> p t d", t=2), ALU.add)
                            else:
                                for j in range(2):
                                    t = 2 * i + j
                                    last = V.scalar_tensor_tensor(acc[:, t, :], o[:, j * D:(j + 1) * D],
                                                                  cv_[:, b, g * T + t, slot:slot + 1], acc[:, t, :],
                                                                  ALU.mult, ALU.add)
                        last.then_inc(sem("ff_y_used"), 1)

                    product(0)
                    for e in range(1, ES):
                        product(e)
                        if e - 1 < E:
                            gather(e - 1)
                    gather(E)

        wrong = {n: (SIGNALS.get(n), c) for n, c in counted.items() if 2 * SIGNALS.get(n, 0) != c}
        assert not wrong, wrong




def constants():
    c = np.zeros((P, NCONST), np.float32)
    p, q = np.arange(P)[:, None], np.arange(P)[None, :]

    def put(name, v):
        a, z = CONST[name]
        c[:, a:z] = v

    put("ident", p == q)
    put("lower", q < p)
    put("upper", p <= q)
    for s in LEVELS:
        put(f"level{s}", (p // (2 * s) == q // (2 * s)) & (p // s % 2 == 1) & (q // s % 2 == 0))
    put("eye64", p % DH == q[:, :DH])
    put("headsel", p // DH == q[:, :2])
    put("mean_s", (p % DH == q) / H)
    put("mean_l", (p % DH == q - DH) / H)
    put("ones", 1.0)
    put("head16", p // XD == q[:, :8])
    put("eye32", p % 32 == q[:, :32])
    e, f = np.arange(E)[:, None], np.arange(E)[None, :]
    put("before", (f < e).reshape(1, -1))
    return c


def kernel(**inputs):
    import concourse.bacc as _bacc
    from concourse import mybir as _mybir
    from concourse.bass_utils import run_bass_kernel_spmd as _run

    a = {n: np.asarray(v) for n, v in inputs.items()}
    f = np.float32

    def rows(w):
        wt = np.ascontiguousarray(w.T)
        n = wt.shape[0] // P
        return wt.reshape(n, P, -1).transpose(1, 0, 2).reshape(P, -1)

    def cols(v):
        v = v.reshape(CK, P, -1)
        return v.transpose(1, 0, 2).reshape(P, -1)

    def spread(v):
        return np.broadcast_to(v.reshape(1, -1), (P, v.size))

    pre = "L0_attn_"
    conv = np.concatenate([cols(a[pre + n + "_conv_w"]) for n in ("k", "q", "v")], axis=1)
    param = np.concatenate([
        conv, cols(a[pre + "fir_short_w"].reshape(D, FS)), cols(a[pre + "fir_long_w"].reshape(D, FL)),
        cols(a[pre + "fg_b1"]), cols(a["L0_xattn_bq"]), cols(a["L0_xattn_bk"]), spread(a["L0_xattn_bv"]),
        spread(a[pre + "fg_b2"]), spread(a["L0_ffn_lb_bias"]), spread(a[pre + "logit_temp"]),
        np.concatenate([a[pre + "o_norm_w"]] * 2).reshape(P, 1)], axis=1)
    w1 = a[pre + "fg_w1"]
    w1p = np.concatenate([w1, np.zeros((D, DH), f)], axis=1)
    weight = np.concatenate([
        rows(a[pre + "k_proj_w"]), rows(a[pre + "q_proj_w"]), rows(a[pre + "v_proj_w"]), rows(a[pre + "b_proj_w"]),
        rows(w1p), rows(a[pre + "fg_w2"]), rows(a[pre + "o_proj_w"]), rows(a["L0_ffn_gate_w"]),
        rows(a["L0_xattn_Wq"]), rows(a["L0_xattn_Wk"]), rows(a["L0_xattn_Wv"])], axis=1)
    ff = "L0_ffn_"
    gates = list(a[ff + "expert_gate_w"]) + list(a[ff + "shared_gate_w"].reshape(2, EI, D))
    ups = list(a[ff + "expert_up_w"]) + list(a[ff + "shared_up_w"].reshape(2, EI, D))
    sd = a[ff + "shared_down_w"]
    downs = list(a[ff + "expert_down_w"]) + [sd[:, :EI], sd[:, EI:]]
    ffn = np.stack([np.concatenate([rows(g), rows(u), rows(d)], axis=1) for g, u, d in zip(gates, ups, downs)], axis=1)
    ctx = a["ctx_1024"].transpose(0, 2, 1).reshape(B, CK, P, S2).transpose(0, 2, 1, 3)
    ctx = np.concatenate([ctx, ctx], axis=3)
    pad = a["mask_Bx1x1xS2_ik0"].reshape(B, S2)
    sub = a["mask_1x1xSxS2_ik0"].reshape(L, S2)
    feeds = {
        "x": a["x"], "ctxT": ctx, "pad_row": np.broadcast_to(pad[:, None, :], (B, P, S2)),
        "pad_col": pad.reshape(B, S2, 1), "sub": sub, "subT": sub.T, "const": constants(),
        "param": param, "weight": weight, "ffn": ffn,
    }
    nc = _bacc.Bacc("TRN2", target_bir_lowering=False, num_devices=1)
    arrays, aps = {}, []
    for n, v in feeds.items():
        v = np.ascontiguousarray(v)
        arrays[n + "_in"] = v
        aps.append(nc.dram_tensor(n + "_in", v.shape, _mybir.dt.from_np(v.dtype), kind="ExternalInput").ap())
    out = nc.dram_tensor("y", (B, L, D), _mybir.dt.float32, kind="ExternalOutput").ap()
    x2 = nc.dram_tensor("x2", (B, G, P, T, D), _mybir.dt.float32, kind="Internal").ap()
    xnT = nc.dram_tensor("xnT", (B, G, P, CK, GT), _mybir.dt.float32, kind="Internal").ap()
    decoder(nc, *aps, out, x2, xnT)
    r = _run(nc, [arrays], core_ids=[0])
    return r.results[0]["y"]
```

```python
from contextlib import ExitStack

import numpy as np

import concourse.bass as bass
from concourse import mybir

ALU = mybir.AluOpType
ACT = mybir.ActivationFunctionType
AX = mybir.AxisListType
F32 = mybir.dt.float32
BF16 = mybir.dt.bfloat16
I32 = mybir.dt.int32

P = 128
B, L, D = 4, 1024, 256
G = 2
GT = L // G
T = GT // P
H, DH = 4, 64
HT = T * H
CK = D // P
CONV, FS, FL = 4, 3, 31
HALO = FL - 1
TAPS = 20
N_TAPS = CK * (FL - TAPS)
XH, XD, S2 = 16, 16, 64
NPAIR = XH // 2
E, EI = 8, 128
ES = 10
NEG = -1.0e9
MIN_LOCAL = 0.05
LEVELS = (1, 2, 4, 8, 16, 32, 64)


def columns(spec):
    at, out = 0, {}
    for name, width in spec:
        out[name] = (at, at + width)
        at += width
    return out, at


CONST, NCONST = columns([("ident", P), ("lower", P), ("upper", P)] + [(f"level{s}", P) for s in LEVELS]
                        + [("eye64", DH), ("headsel", 2), ("mean_s", P), ("mean_l", P), ("ones", P),
                           ("head16", 8), ("eye32", 32), ("before", E * E), ("past", 32)])
PARAM, NPARAM = columns([("conv", 6 * CONV), ("fir_s", CK * FS), ("fir_l", CK * FL), ("fg_b1", CK),
                         ("bq", CK), ("bk", CK), ("bv", D), ("fg_b2", 4), ("lb", E), ("temp", 1), ("onorm", 1)])
WEIGHT, NWEIGHT = columns([("k", CK * D), ("q", CK * D), ("v", CK * D), ("beta", CK * H), ("fg1", 4 * D),
                           ("fg2", CK * 4), ("o", CK * D), ("route", CK * E), ("xq", CK * D), ("xk", CK * D),
                           ("xv", CK * D)])


DVE_MAIN, DVE_CROSS, DVE_PREP = (63, 63), (24, 20), (24, 24)
MAIN_BANKS, PREP_BANKS, CROSS_BANKS = (0, 1, 2), (3, 7), (4, 5, 6)


def psum_plan():
    plan = []

    def ring(names, banks):
        for i, n in enumerate(names):
            plan.append((n, banks[i % len(banks)]))

    for g in range(G):
        names = ["hsT0", "hsT1"] + [f"proj{j}" for j in range(6)] + ["stat"]
        ring([f"{n}.{g}" for n in names], PREP_BANKS)
        ring([f"kv{t}.{g}" for t in range(T)], MAIN_BANKS)
        ring([f"gram{t}{i}.{g}" for t in range(T) for i in range(2)], MAIN_BANKS)
        names = ["P1"]
        for s in LEVELS[1:5]:
            names += [f"P{s}", f"D{s}"]
        names += ["P32a", "P32b", "R32a", "R32b", "T32a", "T32b", "P64a", "P64b", "R64a", "R64b"]
        names += [f"uw{t}" for t in range(T)] + [f"wa{t}" for t in range(T)] + ["gm"]
        for t in range(T):
            names += [f"state{t}", f"out{t}"]
        ring([f"{n}.{g}" for n in ("h1a", "h1b")], PREP_BANKS)
        names += ["dmT", "logit"] + [f"sl{t}" for t in range(T)]
        names += ["oT0", "oT1", "oproj0", "oproj1"]
        ring([f"{n}.{g}" for n in names], MAIN_BANKS)
        names = ["kx", "vx"] if g == 0 else []
        names += ["any", "x1T0", "x1T1", "qx0", "qx1"]
        names += [f"sx{t}{c}" for t in range(T) for c in range(CK)]
        names += ["mxT"]
        ring([f"{n}.{g}" for n in names], CROSS_BANKS)
        for u in range(2):
            ring([f"sT{u}{j}.{g}" for j in range(NPAIR // 2)], CROSS_BANKS[0:1])
            ring([f"pv{2 * u + i}.{g}" for i in range(2)], CROSS_BANKS[1:3])
        ring([f"{n}.{g}" for n in ("x2T0", "x2T1", "route")], CROSS_BANKS)
    bank = dict(plan)
    seen = [0] * 8
    index = {}
    for n, k in plan:
        index[n] = seen[k]
        seen[k] += 1
    return bank, index, seen


SIGNALS = {
    "x0_loaded": 16, "x1_loaded": 16, "hs_stats_ready": 2, "hs_rstd_ready": 2, "hs_rows_ready": 2,
    "conv_ready": 12, "act_ready": 12, "keys_ready": 4, "squares_ready": 8, "rnorm_ready": 4,
    "fir_begun": 4, "tap_ready": 2 * N_TAPS, "tap_added": 2 * N_TAPS, "fir_done": 4, "level1_ready": 8, "level_ready": 12, "rows_ready": 16, "scales_ready": 2, "compact_ready": 10,
    "blocks_ready": 10, "inverse_ready": 2, "blocks_cleared": 4, "delta_ready": 8, "exp_ready": 2, "gate_ready": 4, "mix_ready": 2,
    "osq_ready": 2, "oms_ready": 2, "orms_ready": 2, "on_ready": 2,
    "ctx_loaded": 16 * 3, "x_stats_ready": 4, "x_rstd_ready": 4, "x_rows_ready": 4,
    "mask_ready": 2, "kblk_ready": 1, "nmx_ready": 2, "x2_ready": 2, "x2_stored": 32, "xnT_stored": 32,
}


def decoder(nc, x, ctxT, pad_row, pad_col, sub, subT, const_d, param_d, weight_d, ffn_d, out, x2_d, xnT_d):
    bank_of, fill_index, fills_per_batch = psum_plan()
    es = ExitStack()
    with es:
        def sb(name, shape, dt=F32):
            return es.enter_context(nc.sbuf_tensor(name, shape, dt))

        sems = {}

        def sem(name):
            if name not in sems:
                sems[name] = es.enter_context(nc.semaphore(name))
            return sems[name]

        banks = [es.enter_context(nc.psum_tensor(f"bank{i}", [P, 512], F32)) for i in range(8)]
        filled = [sem(f"bank{i}_filled") for i in range(8)]
        drained = [sem(f"bank{i}_drained") for i in range(8)]

        const = sb("const", [P, NCONST])
        param = sb("param", [P, NPARAM])
        wt = sb("wt", [P, NWEIGHT])

        def cst(n, rows=slice(0, P)):
            return const[rows, CONST[n][0]:CONST[n][1]]

        def prm(n, i=0, w=None):
            a = PARAM[n][0] + i
            return param[:, a:(a + w) if w else PARAM[n][1]]

        def wgt(n, c, width):
            a = WEIGHT[n][0] + c * width
            return wt[:, a:a + width]

        ident_b = sb("ident_b", [P, P], BF16)
        ones_b = sb("ones_b", [P, P], BF16)
        aug_lhs = sb("aug_lhs", [P, NPAIR, P], BF16)
        minus_half = sb("minus_half", [P, 16])
        eps = sb("eps", [P, 2, 8])
        rtemp = sb("rtemp", [P, 8])

        xt = sb("xt", [P, G, T, D])
        spare = sb("spare", [P, 1])
        xn, stats, mv, rstd = ([sb(f"{n}_{i}", [P, T] + w) for i in ("hs", "x")]
                               for n, w in (("xn", [D]), ("stats", [6]), ("mv", [2]), ("rstd", [])))
        hsT = sb("hsT", [P, CK, GT])
        pre = sb("pre", [P, 6, CONV - 1 + GT])
        cv = sb("cv", [P, 2, GT])
        kq = sb("kq", [P, 2, 2, GT])
        vT = sb("vT", [P, CK, HALO + GT])
        lng = sb("lng", [P, CK, GT])
        sht = sb("sht", [P, CK, GT])
        st = sb("st", [P, T, 12])
        rn = sb("rn", [P, T, 8])
        beta = sb("beta", [P, T, H])
        rb = sb("rb", [P, T, H])
        sc = sb("sc", [P, T, H])
        kvt = sb("kvt", [P, T, 512])
        Y = sb("Y", [P, HT, P])
        A = sb("A", [P, HT, P])
        attnT = sb("attnT", [P, HT, P])
        Bl = sb("Bl", [P, 2, HT, P])
        sq = Bl[:, 1, :, :].rearrange("p (a c) d -> p a (c d)", a=4)
        Tf = sb("Tf", [P, HT, P])
        Rf = sb("Rf", [P, HT, P])
        Rc = sb("Rc", [P, HT, 32])
        Tc = sb("Tc", [P, HT, 32])
        Pc = sb("Pc", [P, HT, 32])
        UW = sb("UW", [P, HT, P])
        Pf = UW
        kz = UW[:, :, :].rearrange("p (r i a) b -> p r i (a b)", r=2, i=2)
        QeT = kq[:, :, 1, :]
        MT = sb("MT", [P, T, 2, P])
        S = sb("S", [P, 2, 2, P])
        delta = Bl[:, 0, 0:8, :].rearrange("p (t a) b -> p t (a b)", t=T)
        taps = A[:, :, :].rearrange("p (s a) b -> p s (a b)", s=4)
        gmT = A[:, 0:4, :].rearrange("p a b -> p (a b)")
        dm = sb("dm", [P, T, DH])
        dmT = A[:, 4:8, :].rearrange("p a b -> p (a b)")
        h1T = A[:, 8:16, :].rearrange("p (c a) b -> p c (a b)", c=CK)
        gw = sb("gw", [P, 8, T, 4])
        gs = sb("gs", [P, 4, T])
        om = attnT[:, 0:8, :].rearrange("p (t a) b -> p t (a b)", t=T)
        oss = sb("oss", [P, HT])
        orn = sb("orn", [P, HT])
        osq = Y[:, 0:8, :].rearrange("p (t a) b -> p t (a b)", t=T)
        xnT = sb("x_T", [P, CK, GT])
        qx = sb("qx", [P, CK, GT])
        PT = sb("PT", [P, 2, GT])
        abc = sb("abc", [P, GT])
        Kblk = sb("Kblk", [P, CK, 8, S2])
        kxT = sb("kxT", [P, CK, S2])
        Va = sb("Va", [P, NPAIR + 3, 34])
        ctx = sb("ctx", [P, CK, P])
        padr = sb("padr", [P, S2], I32)
        padc = sb("padc", [S2, 1], I32)
        subi = Y[:, 0:4, :].bitcast(I32).rearrange("p a (b k) -> p (a b) k", k=S2)
        subTi = Y[0:S2, 4:12, :].bitcast(I32).rearrange("p a b -> p (a b)")
        sub01 = sb("sub01", [P, L // P, S2], BF16)
        subT01 = sb("subT01", [S2, L], BF16)
        pr01 = sb("pr01", [P, S2])
        pc01 = sb("pc01", [S2, 1])
        mbf = sb("mbf", [P, L // P, S2], BF16)
        mb = sb("mb", [P, L // P, S2], BF16)
        mT = sb("mT", [S2, GT], BF16)
        aug = sb("aug", [P, GT], BF16)
        nmx = sb("nmx", [P, 2, T, XH])
        nmb = sb("nmb", [P, T, 3 * XH], BF16)
        rden = sb("rden", [P, T, NPAIR, 2])
        xo = sb("xo", [P, D])
        route = sb("route", [P, B * G * T, E])

        plus = (lambda b, per, k: b * per + k)

        def window(M, at, width=P):
            return M.rearrange("p a b -> p (a b)")[:, at:at + width]

        PRIMED = {"blocks_cleared": 1, "xnT_stored": 16}
        counted = {}

        class Signals:

            def __init__(self, eng, b):
                self.eng, self.b = eng, b

            def wait(self, name, k):
                self.eng.wait_ge(sem(name), plus(self.b, SIGNALS[name], k + PRIMED.get(name, 0)))

            def filled(self, name):
                k = bank_of[name]
                self.eng.wait_ge(filled[k], plus(self.b, fills_per_batch[k], fill_index[name] + 1))
                return banks[k]

            def drained(self, name):
                k = bank_of[name]
                self.eng.wait_ge(drained[k], plus(self.b, fills_per_batch[k], fill_index[name] + 1 + 1))

            def bank_free(self, name):
                k = bank_of[name]
                self.eng.wait_ge(drained[k], plus(self.b, fills_per_batch[k], fill_index[name] + 1))
                return banks[k]

        def full(ins, name):
            ins.then_inc(filled[bank_of[name]], 1)

        def free(ins, name):
            ins.then_inc(drained[bank_of[name]], 1)

        def done(ins, name, n=1):
            counted[name] = counted.get(name, 0) + n
            ins.then_inc(sem(name), n)

        tables_loaded = sem("tables_loaded")
        w_loaded = sem("weights_loaded")
        setup_dve = sem("setup_dve")
        setup_pool = sem("setup_pool")
        ffn_loaded = sem("ffn_weights_loaded")
        N_DVE_SETUP, N_POOL_SETUP = 12, 14

        class Steps:

            def __init__(self, eng, name, per_group):
                self.eng, self.sem, self.per = eng, sem(name), per_group

            def at(self, b, g):
                self.b, self.g, self.k = b, g, 0

            def step(self, ins):
                self.k += 1
                ins.then_inc(self.sem, 1)
                return self.k

            def after(self, k):
                self.eng.wait_ge(self.sem, plus(self.b, sum(self.per), sum(self.per[:self.g]) + k))

            def link(self, ins):
                self.after(self.step(ins))

            def end(self):
                assert self.k == self.per[self.g], (self.sem, self.g, self.k)

        block = es.enter_context(nc.Block())

        class Idle:

            def __getitem__(self, name):
                return lambda: None

        idle = Idle()

        def pipeline(eng, prep, main, cross):
            for piece in prep(0, 0).values():
                piece()
            main(0, 0, idle, prep(0, 1))
            with eng.Fori(0, B - 1) as b:
                main(b, 1, cross(b, 0), prep(b + 1, 0))
                main(b + 1, 0, cross(b, 1), prep(b + 1, 1))
            main(B - 1, 1, cross(B - 1, 0), idle)
            for piece in cross(B - 1, 1).values():
                piece()

        ffw = [Bl[:, 0, :, :], Bl[:, 1, :, :], Tf[:, :, :], Rf[:, :, :], UW[:, :, :]]
        ffw = [a.rearrange("p a b -> p (a b)") for a in ffw]

        def expert_flat(e):
            k, i = divmod(e, 2)
            return ffw[k][:, i * 768:(i + 1) * 768]

        def expert(e):
            base = expert_flat(e)
            return (base[:, 0:256].rearrange("p (c n) -> p c n", c=2),
                    base[:, 256:512].rearrange("p (c n) -> p c n", c=2), base[:, 512:768])

        fx = [Y[:, 0:8, :].rearrange("p (c a) b -> p c (a b)", c=CK),
              Y[:, 8:16, :].rearrange("p (c a) b -> p c (a b)", c=CK)]
        facc = [xt[:, 0, :, :], xt[:, 1, :, :]]
        fg = [kvt[:, i, :] for i in range(2)]
        fh = [kvt[:, 2 + i, :] for i in range(2)]
        coef = sb("coef", [P, B * G * T, E])


        @block.sync
        def _(sp):
            sp.dma_start(const[:, :], const_d).then_inc(tables_loaded, 16)
            sp.dma_start(param[:, :], param_d).then_inc(tables_loaded, 16)
            sp.dma_start(wt[:, :], weight_d).then_inc(w_loaded, 16)
            sp.dma_start(subi, sub.rearrange("(t p) k -> p t k", p=P)).then_inc(w_loaded, 16)
            sp.dma_start(subTi, subT).then_inc(w_loaded, 16)

            def load_rows(b, g):
                done(sp.dma_start(xt[:, g, :, :], x[b, g * GT:(g + 1) * GT, :]
                                  .rearrange("(t p) d -> p t d", p=P)), f"x{g}_loaded", 16)

            def load_context(b):
                done(sp.dma_start(ctx[:, :, :], ctxT[b, :, :, :]), "ctx_loaded", 16)
                done(sp.dma_start(padr[:, :], pad_row[b, :, :]), "ctx_loaded", 16)
                done(sp.dma_start(padc[:, :], pad_col[b, :, :]), "ctx_loaded", 16)

            def passed():
                sp.sem_inc(sem("sp_passed"), 1)

            def store_rows(b, g, load):
                s = Signals(sp, b)
                s.wait("x2_ready", g + 1)
                done(sp.dma_start(x2_d[b, g, :, :, :], xt[:, g, :, :]), "x2_stored", 16)
                if load:
                    s.wait("x2_stored", 16 * (g + 1))
                    passed()
                    s.wait("x_rows_ready", 2 * g + 2)
                    passed()
                    load_rows(b + 1, g)
                s.drained(f"x2T0.{g}")
                passed()
                s.drained(f"x2T1.{g}")
                passed()
                done(sp.dma_start(xnT_d[b, g, :, :, :], xnT[:, :, :]), "xnT_stored", 16)

            for g in range(G):
                load_rows(0, g)
            load_context(0)
            with sp.Fori(0, B - 1) as b:
                store_rows(b, 0, True)
                Signals(sp, b).wait("kblk_ready", 1)
                passed()
                load_context(b + 1)
                store_rows(b, 1, True)
            s = Signals(sp, B - 1)
            s.drained("oproj1.1")
            s.wait("blocks_cleared", 4)
            for e in range(ES):
                sp.dma_start(expert_flat(e), ffn_d[:, e, :]).then_inc(ffn_loaded, 16)
            store_rows(B - 1, 0, False)
            store_rows(B - 1, 1, False)
            for name in ("x2_stored", "xnT_stored"):
                s.wait(name, SIGNALS[name])

            def load_ffn(b, g):
                sp.dma_start(fx[g], xnT_d[b, g, :, :, :]).then_inc(sem(f"fx{g}_loaded"), 16)
                sp.dma_start(facc[g], x2_d[b, g, :, :, :]).then_inc(sem(f"fx{g}_loaded"), 16)

            def store_result(b, g):
                sp.wait_ge(sem("ff_y_used"), b * (G * 9) + g * 9 + 9 + 1)
                passed()
                sp.dma_start(out[b, g * GT:(g + 1) * GT, :].rearrange("(t p) d -> p t d", p=P),
                             facc[g]).then_inc(sem("y_stored"), 16)

            for g in range(G):
                load_ffn(0, g)
            with sp.Fori(0, B - 1) as b:
                for g in range(G):
                    store_result(b, g)
                    sp.wait_ge(sem("y_stored"), b * 32 + 16 * g + 16)
                    passed()
                    load_ffn(b + 1, g)
            for g in range(G):
                store_result(B - 1, g)
            sp.wait_ge(sem("y_stored"), B * G * 16)

        @block.tensor
        def _(pe):
            mm, tr = pe.matmul, pe.transpose
            ident = cst("ident")
            pe.wait_ge(tables_loaded, 16 * 2)
            pe.wait_ge(w_loaded, 16 * 3)
            pe.wait_ge(setup_dve, N_DVE_SETUP)
            pe.wait_ge(setup_pool, N_POOL_SETUP)

            def transpose_rows(s, src, names):
                for c in range(CK):
                    o = s.bank_free(names[c])
                    for t in range(T):
                        last = tr(o[:, t * P:(t + 1) * P], src[:, t, c * P:(c + 1) * P], ident)
                    full(last, names[c])

            def cross(b, g):
                s = Signals(pe, b)

                def context():
                    if g:
                        return
                    s.wait("ctx_loaded", 48)
                    n = f"kx.{g}"
                    o = s.bank_free(n)
                    for m in range(CK):
                        for c in range(CK):
                            last = mm(o[:, m * S2:m * S2 + P], wgt("xk", c, D)[:, m * P:(m + 1) * P],
                                      ctx[:, c, :], start=c == 0, stop=c == CK - 1)
                    full(last, n)
                    n = f"vx.{g}"
                    o = s.bank_free(n)
                    for c in range(CK):
                        last = mm(o[:, 0:D], ctx[:, c, :], wgt("xv", c, D), start=c == 0, stop=c == CK - 1)
                    full(last, n)

                def rows():
                    n = f"any.{g}"
                    o = s.bank_free(n)
                    s.wait("mask_ready", g + 1)
                    full(mm(o[:, :], ones_b[0:S2, :], mT[:, :], start=True, stop=True), n)
                    s.wait("x_rows_ready", 2 * g + 1)
                    transpose_rows(s, xn[1], [f"x1T0.{g}", f"x1T1.{g}"])

                def queries():
                    s.drained(f"x1T0.{g}")
                    s.drained(f"x1T1.{g}")
                    for m in range(CK):
                        n = f"qx{m}.{g}"
                        o = s.bank_free(n)
                        for c in range(CK):
                            last = mm(o[:, :], wgt("xq", c, D)[:, m * P:(m + 1) * P], xnT[:, c, :],
                                      start=c == 0, stop=c == CK - 1)
                        full(last, n)

                def masked_scores(t):
                    def piece():
                        if t == 0:
                            s.drained(f"qx0.{g}")
                            s.drained(f"qx1.{g}")
                            s.wait("kblk_ready", 1)
                        for c in range(CK):
                            n = f"sx{t}{c}.{g}"
                            o = s.bank_free(n)
                            ov = o[:, :].rearrange("p (h k) -> p h k", h=8)
                            mm(ov, qx[:, c, t * P:(t + 1) * P], Kblk[:, c, :, :], start=True, stop=False)
                            full(mm(ov, ident_b[:, :], mb[:, g * T + t, :].unsqueeze(1).broadcast_to([P, 8, S2]),
                                    start=False, stop=True), n)
                    return piece

                def maxima():
                    n = f"mxT.{g}"
                    o = s.bank_free(n)
                    s.wait("nmx_ready", g + 1)
                    for t in range(T):
                        last = mm(o[64:112, t * P:(t + 1) * P], nmb[:, t, :], ident_b[:, :], start=True, stop=True)
                    full(last, n)

                def scores(u, j):
                    n = f"sT{u}{j}.{g}"
                    o = s.bank_free(n)
                    if u == 0 and j == 0:
                        s.drained(f"mxT.{g}")
                    uu = slice(u * GT // 2, (u + 1) * GT // 2)
                    for i in range(2):
                        c, k = divmod(2 * j + i, 4)
                        oo = o[:, i * GT // 2:(i + 1) * GT // 2]
                        lhs = Kblk[:, c, 2 * k:2 * k + 2, :].rearrange("p a b -> p (a b)")
                        mm(oo, lhs, qx[:, c, uu], start=True, stop=False)
                        last = mm(oo, aug_lhs[0:112, 2 * j + i, :], aug[0:112, uu], start=False, stop=True)
                    full(last, n)

                def first(u):
                    return lambda: scores(u, 0)

                def values(u, j):
                    def piece():
                        if j < NPAIR // 2 - 1:
                            scores(u, j + 1)
                        s.drained(f"sT{u}{j}.{g}")
                        for i in range(2):
                            at = (2 * j + i) * 34
                            for k in range(2):
                                n = f"pv{2 * u + k}.{g}"
                                o = s.bank_free(n) if i == j == 0 else banks[bank_of[n]]
                                last = mm(o[:, at:at + P], PT[:, j % 2, (2 * i + k) * P:(2 * i + k + 1) * P],
                                          window(Va[:, :, :], at), start=True, stop=True)
                                if i == 1 and j == NPAIR // 2 - 1:
                                    full(last, n)
                    return piece

                def routing():
                    s.wait("x_rows_ready", 2 * g + 2)
                    transpose_rows(s, xn[1], [f"x2T0.{g}", f"x2T1.{g}"])
                    s.drained(f"x2T0.{g}")
                    s.drained(f"x2T1.{g}")
                    n = f"route.{g}"
                    o = s.bank_free(n)
                    at = WEIGHT["route"][0]
                    for t in range(T):
                        for c in range(CK):
                            last = mm(o[:, t * E:t * E + P], xnT[:, c, t * P:(t + 1) * P],
                                      wt[:, at + c * E:at + c * E + P], start=c == 0, stop=c == CK - 1)
                    full(last, n)

                x = {"context": context, "rows": rows, "queries": queries}
                for t in range(T):
                    x["scores", t] = masked_scores(t)
                x["maxima"] = maxima
                for u in range(2):
                    x["first", u] = first(u)
                    for j in range(NPAIR // 2):
                        x["values", u, j] = values(u, j)
                x["routing"] = routing
                return x

            def prep(b, g):
                s = Signals(pe, b)

                def rows():
                    s.wait("hs_rows_ready", g + 1)
                    transpose_rows(s, xn[0], [f"hsT0.{g}", f"hsT1.{g}"])

                def project(j):
                    def piece():
                        if j == 0:
                            s.drained(f"hsT0.{g}")
                            s.drained(f"hsT1.{g}")
                        w = "kqv"[j // 2]
                        n = f"proj{j}.{g}"
                        o = s.bank_free(n)
                        for c in range(CK):
                            last = mm(o[:, :], wgt(w, c, D)[:, (j % 2) * P:(j % 2 + 1) * P], hsT[:, c, :],
                                      start=c == 0, stop=c == CK - 1)
                        full(last, n)
                    return piece

                def beta_logits():
                    n = f"stat.{g}"
                    o = s.bank_free(n)
                    at = WEIGHT["beta"][0]
                    for t in range(T):
                        for c in range(CK):
                            mm(o[:, D + t * H:D + t * H + P], hsT[:, c, t * P:(t + 1) * P],
                               wt[:, at + c * H:at + c * H + P], start=c == 0, stop=c == CK - 1)

                def stat():
                    n = f"stat.{g}"
                    o = banks[bank_of[n]]
                    at = CONST["headsel"][0]
                    s.wait("squares_ready", 4 * g + 4)
                    for t in range(T):
                        for i in range(4):
                            a = 2 * (i % 2) + (1 - i // 2)
                            last = mm(o[:, t * 8 + 2 * i:t * 8 + 2 * i + P], sq[:, a, t * P:(t + 1) * P],
                                      const[:, at:at + P], start=True, stop=True)
                    full(last, n)

                p = {"rows": rows}
                for j in range(6):
                    p["project", j] = project(j)
                p["beta"] = beta_logits
                p["stat"] = stat
                return p

            def main(b, g, x, p):
                s = Signals(pe, b)
                for t in range(T):
                    n = f"kv{t}.{g}"
                    o = s.bank_free(n)
                    tt = slice(t * P, (t + 1) * P)
                    for c in range(CK):
                        tr(o[:, c * P:(c + 1) * P], kq[:, c, 0, tt], ident)
                    s.wait("act_ready", 6 * g + 6)
                    for c in range(CK):
                        last = tr(o[:, (2 + c) * P:(3 + c) * P],
                                  vT[:, c, HALO + t * P:HALO + (t + 1) * P], ident)
                    full(last, n)
                s.wait("keys_ready", 2 * g + 2)
                for t in range(T):
                    for r in range(2):
                        n = f"gram{t}{r}.{g}"
                        o = s.bank_free(n)
                        for i in range(2):
                            last = mm(o[:, i * 2 * P:(i + 1) * 2 * P], kz[:, r, i, t * P:(t + 1) * P],
                                      kq[:, i, :, t * P:(t + 1) * P], start=True, stop=True)
                        full(last, n)
                lv = 6 * g - 1
                n = f"P1.{g}"
                o = s.bank_free(n)
                at = CONST["eye32"][0]
                for h in range(HT):
                    if h % H == 0:
                        s.wait("level1_ready", T * g + h // H + 1)
                    w_ = min(P, 512 - h * 32)
                    last = mm(o[:, h * 32:h * 32 + w_], Bl[:, 0, h, :], const[:, at:at + w_], start=True, stop=True)
                full(last, n)
                x["context"]()
                x["rows"]()
                for i, size in enumerate(LEVELS[1:5]):
                    n = f"P{size}.{g}"
                    o = s.bank_free(n)
                    s.wait("level_ready", lv + 2 + i)
                    if i == 0:
                        s.drained(f"P1.{g}")
                    else:
                        s.drained(f"D{LEVELS[i]}.{g}")
                    for h in range(HT):
                        w_ = min(P, 512 - h * 32)
                        last = mm(o[:, h * 32:h * 32 + w_], Bl[:, (i + 1) % 2, h, :],
                                  window(Rc[:, :, :], h * 32, w_), start=True, stop=True)
                    full(last, n)
                    if i == 0:
                        x["queries"]()
                    s.drained(n)
                    s.wait("blocks_ready", 5 * g + i + 1)
                    s.wait("blocks_cleared", 2 * g)
                    n = f"D{size}.{g}"
                    o = s.bank_free(n)
                    for h in range(HT):
                        w_ = min(P, 512 - h * 32)
                        last = mm(o[:, h * 32:h * 32 + w_], Tf[:, h, :], window(Pc[:, :, :], h * 32, w_),
                                  start=True, stop=True)
                    full(last, n)
                    if i:
                        x["scores", i - 1]()
                s.wait("blocks_ready", 5 * g + 5)
                s.wait("inverse_ready", g + 1)
                halves = [("a", 0), ("b", 8)]
                s.wait("level_ready", lv + 6)

                def quarter(M, h, h_end, a):
                    w_ = min(4, 2 * (h_end - h))
                    return M.rearrange("p h (q c) -> p (h q) c", q=2)[:, 2 * h:2 * h + w_, 32 * a:32 * a + 32]

                for i, (x_, h0) in enumerate(halves):
                    n = f"P32{x_}.{g}"
                    o = s.bank_free(n)
                    for h in range(8):
                        w_ = min(P, 512 - h * 64)
                        last = mm(o[:, h * 64:h * 64 + w_], Bl[:, 1, h0 + h, :],
                                  quarter(Rf[:, :, :], h0 + h, h0 + 8, 1), start=True, stop=True)
                    full(last, n)
                x["scores", 3]()
                for i, (x_, h0) in enumerate(halves):
                    s.drained(f"P32{x_}.{g}")
                    n = f"R32{x_}.{g}"
                    o = s.bank_free(n)
                    for h in range(8):
                        w_ = min(P, 512 - h * 64)
                        last = mm(o[:, h * 64:h * 64 + w_], Tf[:, h0 + h, :],
                                  quarter(Pf[:, :, :], h0 + h, h0 + 8, 1), start=True, stop=True)
                    full(last, n)
                x["maxima"]()
                x["first", 0]()
                for i, (x_, h0) in enumerate(halves):
                    n = f"T32{x_}.{g}"
                    o = s.bank_free(n)
                    for h in range(8):
                        w_ = min(P, 512 - h * 64)
                        last = mm(o[:, h * 64:h * 64 + w_], Pf[:, h0 + h, :],
                                  quarter(Tf[:, :, :], h0 + h, h0 + 8, 0), start=True, stop=True)
                    full(last, n)
                    x["values", 0, i]()
                s.wait("level_ready", lv + 7)
                for x_, h0 in halves:
                    s.drained(f"R32{x_}.{g}")
                    n = f"P64{x_}.{g}"
                    o = s.bank_free(n)
                    for h in range(8):
                        w_ = min(P, 512 - h * 64)
                        last = mm(o[:, h * 64:h * 64 + w_], Bl[:, 0, h0 + h, :],
                                  window(Rf[:, :, :], (h0 + h) * P + 64, w_), start=True, stop=True)
                    full(last, n)
                    x["values", 0, 2 if x_ == "a" else 3]()
                x["first", 1]()
                for x_, h0 in halves:
                    s.drained(f"P64{x_}.{g}")
                    s.drained(f"T32{x_}.{g}")
                    n = f"R64{x_}.{g}"
                    o = s.bank_free(n)
                    for h in range(8):
                        w_ = min(P, 512 - h * 64)
                        last = mm(o[:, h * 64:h * 64 + w_], Tf[:, h0 + h, :],
                                  window(Pf[:, :, :], (h0 + h) * P + 64, w_), start=True, stop=True)
                    full(last, n)
                    x["values", 1, 0 if x_ == "a" else 1]()
                s.wait("rows_ready", 8 * g + 8)
                for t in range(T):
                    if t % 2 == 0:
                        s.drained(f"R64{'ab'[t // 2]}.{g}")
                    n = f"uw{t}.{g}"
                    o = s.bank_free(n)
                    for h in range(H):
                        last = mm(o[:, h * P:(h + 1) * P], Rf[:, t * H + h, :], Y[:, t * H + h, :],
                                  start=True, stop=True)
                    full(last, n)
                x["values", 1, 2]()
                for t in range(T):
                    s.drained(f"uw{t}.{g}")
                    n = f"wa{t}.{g}"
                    o = s.bank_free(n)
                    for h in range(H):
                        r, i = h % 2, h // 2
                        w_ = UW[:, t * H + h, 64:128]
                        mm(o[DH * r:DH * r + DH, i * P:(i + 1) * P], w_, attnT[:, t * H + h, :],
                           start=True, stop=True)
                        last = mm(o[DH * r:DH * r + DH, 256 + i * DH:256 + (i + 1) * DH], w_,
                                  kvt[:, t, h * DH:(h + 1) * DH], start=True, stop=True)
                    full(last, n)
                x["values", 1, 3]()
                n = f"gm.{g}"
                o = s.bank_free(n)
                s.wait("fir_done", 2 * g + 2)
                s.wait("tap_added", N_TAPS * (g + 1))
                for i in range(4):
                    src = (sht, lng)[i // 2]
                    last = mm(o[:, :], cst(("mean_s", "mean_l")[i // 2]), src[:, i % 2, :],
                              start=i == 0, stop=i == 3)
                full(last, n)

                def gate_hidden(m, i):
                    n = f"h1{'ab'[m]}.{g}"
                    o = s.bank_free(n) if i == 0 else banks[bank_of[n]]
                    if m == 0 and i == 2:
                        s.drained(f"gm.{g}")
                    rhs = (hsT[:, 0, :], hsT[:, 1, :], gmT[:, :], dmT[:, :])[i]
                    last = mm(o[:, :], wgt("fg1", i, D)[:, m * P:(m + 1) * P], rhs, start=i == 0, stop=i == 3)
                    if i == 3:
                        full(last, n)

                gate_hidden(0, 0)
                for t in range(T):
                    s.drained(f"wa{t}.{g}")
                    if t > 0:
                        s.drained(f"state{t - 1}.{g}")
                    first = t == 0 and g == 0
                    n = f"state{t}.{g}"
                    o = s.bank_free(n)
                    for i in range(2):
                        cc = slice(i * P, (i + 1) * P)
                        last = mm(o[:, cc], kvt[:, t, cc], UW[:, t * H + 2 * i:t * H + 2 * i + 2, 0:64],
                                  start=True, stop=first)
                        if not first:
                            last = mm(o[:, cc], MT[:, t, i, :], S[:, t % 2, i, :], start=False, stop=True)
                    full(last, n)
                    if t < 2:
                        gate_hidden(t, 1)
                    n = f"out{t}.{g}"
                    o = s.bank_free(n)
                    for i in range(2):
                        if not first:
                            mm(o[:, i * P:(i + 1) * P], QeT[:, i, t * P:(t + 1) * P], S[:, t % 2, i, :],
                               start=True, stop=False)
                        for r in range(2):
                            h = 2 * i + r
                            last = mm(o[:, h * DH:(h + 1) * DH], attnT[:, t * H + h, :], UW[:, t * H + h, 0:DH],
                                      start=first, stop=first or r == 1)
                    full(last, n)
                    if t == 0:
                        gate_hidden(0, 2)
                        gate_hidden(1, 0)
                    if t == 1:
                        gate_hidden(1, 2)
                n = f"dmT.{g}"
                o = s.bank_free(n)
                s.wait("delta_ready", 4 * g + 4)
                for t in range(T):
                    last = mm(o[0:DH, t * P:(t + 1) * P], dm[:, t, :], ident, start=True, stop=True)
                full(last, n)
                s.drained(f"dmT.{g}")
                for m in range(CK):
                    gate_hidden(m, 3)
                p["rows"]()
                s.drained(f"h1a.{g}")
                s.drained(f"h1b.{g}")
                at = WEIGHT["fg2"][0]
                n = f"logit.{g}"
                o = s.bank_free(n)
                for t in range(T):
                    for c in range(CK):
                        last = mm(o[:, t * 4:t * 4 + P], h1T[:, c, t * P:(t + 1) * P],
                                  wt[:, at + c * 4:at + c * 4 + P], start=c == 0, stop=c == CK - 1)
                full(last, n)
                p["project", 0]()
                p["project", 1]()
                for t in range(T):
                    if t == T - 1:
                        p["project", 2]()
                        p["project", 3]()
                    n = f"sl{t}.{g}"
                    o = s.bank_free(n)
                    for i in range(4):
                        last = tr(o[:, i * P:(i + 1) * P], (sht, lng)[i // 2][:, i % 2, t * P:(t + 1) * P], ident)
                    full(last, n)
                x["routing"]()
                for j in range(4, 6):
                    p["project", j]()
                p["beta"]()
                s.wait("on_ready", g + 1)
                transpose_rows(s, om, [f"oT0.{g}", f"oT1.{g}"])
                s.drained(f"oT0.{g}")
                s.drained(f"oT1.{g}")
                for i in range(2):
                    n = f"oproj{i}.{g}"
                    o = s.bank_free(n)
                    for j in range(2):
                        t = 2 * i + j
                        for c in range(CK):
                            last = mm(o[:, j * D:(j + 1) * D], h1T[:, c, t * P:(t + 1) * P], wgt("o", c, D),
                                      start=c == 0, stop=c == CK - 1)
                    full(last, n)
                p["stat"]()

            pipeline(pe, prep, main, cross)
            pe.wait_ge(sem("route_sums"), 1)
            mm(banks[0][:, 0:2 * E], cst("ones"), gw[:, 0, :, :].rearrange("p t k -> p (t k)"),
               start=True, stop=True).then_inc(sem("route_total"), 1)
            pe.wait_ge(ffn_loaded, 16 * ES)
            pe.wait_ge(sem("coef_ready"), 1)
            with pe.Fori(0, B) as b:
                for g in range(G):
                    pe.wait_ge(sem(f"fx{g}_loaded"), b * 32 + 32)

                    def hidden(e):
                        k = b * (G * ES) + g * ES + e
                        wg_, wu_, _ = expert(e)
                        pe.wait_ge(sem("ff_h_ready"), k if (g or e > 1) else b * (G * ES) + 1)
                        for c in range(CK):
                            last = mm(banks[e % 2][:, :], wg_[:, c, :], fx[g][:, c, :], start=c == 0, stop=c == CK - 1)
                        last.then_inc(sem("ff_gate"), 1)
                        for c in range(CK):
                            last = mm(banks[2 + e % 2][:, :], wu_[:, c, :], fx[g][:, c, :],
                                      start=c == 0, stop=c == CK - 1)
                        last.then_inc(sem("ff_up"), 1)

                    def down(e, srcs, slot):
                        pe.wait_ge(sem("ff_h_ready"), b * (G * ES) + g * ES + e + 2)
                        k = b * (G * 9) + g * 9 + slot
                        pe.wait_ge(sem("ff_y_used"), k if (g or slot > 1) else b * (G * 9) + 1)
                        for i in range(2):
                            o = banks[4 + 2 * ((g * 9 + slot) % 2) + i]
                            for j in range(2):
                                t = 2 * i + j
                                for q_, e_ in enumerate(srcs):
                                    last = mm(o[:, j * D:(j + 1) * D], fh[e_ % 2][:, t * P:(t + 1) * P], expert(e_)[2],
                                              start=q_ == 0, stop=q_ == len(srcs) - 1)
                        last.then_inc(sem("ff_y"), 1)

                    hidden(0)
                    for e in range(1, ES):
                        hidden(e)
                        if e - 1 < E:
                            down(e - 1, [e - 1], e - 1)
                    down(ES - 1, [ES - 2, ES - 1], E)

        @block.scalar
        def _(act):
            act.wait_ge(tables_loaded, 16 * 2)
            act.wait_ge(w_loaded, 16 * 3)
            act.wait_ge(setup_dve, N_DVE_SETUP)
            act.wait_ge(setup_pool, N_POOL_SETUP)
            act.activation(rtemp[:, 1:2], rtemp[:, 0:1], ACT.Exp, scale=-1.0).then_inc(sem("temp_exp"), 1)
            act.wait_ge(sem("temp_exp"), 1)
            act.activation(rtemp[:, 2:3], rtemp[:, 1:2], ACT.Ln, bias=cst("ones")[:, 0:1]).then_inc(sem("temp_ln"), 1)

            def evac(out_, in_, name, func=ACT.Copy, **kw):
                free(act.activation(out_, in_, func, **kw), name)

            def cross(b, g):
                s = Signals(act, b)

                def rows():
                    if g == 0:
                        n = f"kx.{g}"
                        o = s.filled(n)
                        for m in range(CK):
                            last = act.activation(kxT[:, m, :], o[:, m * S2:(m + 1) * S2], ACT.Identity,
                                                  bias=prm("bk", m, 1))
                        free(last, n)
                    for c in range(CK):
                        n = f"x1T{c}.{g}"
                        o = s.filled(n)
                        s.wait("xnT_stored", 16 * g)
                        evac(xnT[:, c, :], o[:, :], n)

                def probs(u, j):
                    def piece():
                        n = f"sT{u}{j}.{g}"
                        o = s.filled(n)
                        evac(PT[:, j % 2, :], o[:, :], n, ACT.Exp)
                    return piece

                def routing():
                    for c in range(CK):
                        n = f"x2T{c}.{g}"
                        o = s.filled(n)
                        evac(xnT[:, c, :], o[:, :], n)

                x = {"rows": rows}
                for u in range(2):
                    for j in range(NPAIR // 2):
                        x["probs", u, j] = probs(u, j)
                x["routing"] = routing
                return x

            def prep(b, g):
                s = Signals(act, b)

                def rows():
                    for c in range(CK):
                        n = f"hsT{c}.{g}"
                        o = s.filled(n)
                        evac(hsT[:, c, :], o[:, :], n)

                def project(j):
                    def piece():
                        n = f"proj{j}.{g}"
                        o = s.filled(n)
                        if j == 0:
                            s.wait("hs_rstd_ready", g + 1)
                        evac(pre[:, j, CONV - 1:], o[:, :], n)
                    return piece

                def silu(j):
                    def piece():
                        s.wait("conv_ready", 6 * g + j + 1)
                        dst = kq[:, j % 2, j // 2, :] if j < 4 else vT[:, j % 2, HALO:]
                        done(act.activation(dst, cv[:, j % 2, :], ACT.Silu), "act_ready")
                        if j == 2:
                            s.wait("act_ready", 6 * g + 2)
                            for r in range(2):
                                done(act.activation(kz[:, r, :, :], kq[:, :, 0, :], ACT.Copy,
                                                    scale=cst("headsel")[:, r:r + 1]), "keys_ready")
                    return piece

                def stat():
                    n = f"stat.{g}"
                    o = s.filled(n)
                    act.activation(st[:, :, 0:8], o[:, 0:T * 8].rearrange("p (t k) -> p t k", t=T), ACT.Copy)
                    evac(st[:, :, 8:12], o[:, D:D + T * H].rearrange("p (t k) -> p t k", t=T), n, ACT.Tanh, scale=0.5)

                p = {"rows": rows}
                for j in range(6):
                    p["project", j] = project(j)
                for j in range(5):
                    p["silu", j] = silu(j)
                p["stat"] = stat
                p["silu", 5] = silu(5)
                return p

            def main(b, g, x, p):
                s = Signals(act, b)
                for t in range(T):
                    n = f"kv{t}.{g}"
                    o = s.filled(n)
                    evac(kvt[:, t, :], o[:, :], n)
                x["rows"]()

                def products(lo, hi):
                    for i in range(lo, hi):
                        j, c = TAPS + i // CK, i % CK
                        if i >= 4:
                            s.wait("tap_added", N_TAPS * g + i - 3)
                        at = PARAM["fir_l"][0] + c * FL + j
                        done(act.activation(taps[:, i % 4, :], vT[:, c, j:j + GT], ACT.Copy,
                                            scale=param[:, at:at + 1]), "tap_ready")

                def spread(dst, src, n):
                    for r in range(4):
                        rr = slice(32 * r, 32 * r + 32)
                        last = act.activation(dst[rr, :, rr], src[rr, :, :], ACT.Copy)
                    done(last, n)

                for i, size in enumerate(LEVELS[1:5]):
                    s.wait("compact_ready", 5 * g + i + 1)
                    spread(Tf, Tc, "blocks_ready")
                    n = f"P{size}.{g}"
                    o = s.filled(n)
                    evac(Pc[:, :, :], o[:, :].rearrange("p (h k) -> p h k", k=32), n)
                s.drained(f"D16.{g}")
                spread(Rf, Rc, "blocks_ready")
                view = lambda M, h0: M[:, h0:h0 + 8, :].rearrange("p h (a c) -> p h a c", a=2)
                for x_, h0 in (("a", 0), ("b", 8)):
                    n = f"P32{x_}.{g}"
                    o = s.filled(n)
                    evac(view(Pf, h0)[:, :, :, 32:64],
                         o[:, :].rearrange("p (h a c) -> p h a c", h=8, a=2), n)
                s.wait("level_ready", 6 * g + 6)
                products(0, 4)
                for j in range(3):
                    x["probs", 0, j]()
                    products(4 + 2 * j, 6 + 2 * j)
                for x_, h0 in (("a", 0), ("b", 8)):
                    n = f"P64{x_}.{g}"
                    if x_ == "b":
                        products(10, 12)
                        x["probs", 0, 3]()
                    o = s.filled(n)
                    s.filled(f"T32{x_}.{g}")
                    evac(Pf[:, h0:h0 + 8, 64:128], o[:, :].rearrange("p (h c) -> p h c", h=8), n)
                products(12, 14)
                for j in range(3):
                    x["probs", 1, j]()
                    products(14 + 2 * j, 16 + 2 * j)
                for t in range(T):
                    n = f"uw{t}.{g}"
                    o = s.filled(n)
                    if t == 0:
                        s.filled(f"R64a.{g}")
                        s.filled(f"R64b.{g}")
                    evac(UW[:, t * H:(t + 1) * H, :], o[:, :].rearrange("p (h c) -> p h c", h=H), n)
                products(20, N_TAPS)
                x["probs", 1, 3]()
                n = f"gm.{g}"
                o = s.filled(n)
                evac(gmT[:, :], o[:, :], n)
                for t in range(T):
                    n = f"state{t}.{g}"
                    o = s.filled(n)
                    if t > 0:
                        s.filled(f"out{t - 1}.{g}")
                    for r in range(2):
                        rr = slice(DH * r, DH * r + DH)
                        last = act.activation(S[rr, (t + 1) % 2, :, rr],
                                              o[rr, 0:2 * P].rearrange("p (i c) -> p i c", i=2)[:, :, rr], ACT.Copy)
                    free(last, n)
                n = f"dmT.{g}"
                o = s.filled(n)
                evac(dmT[0:DH, :], o[0:DH, :], n, scale=1.0 / H)
                for m in range(CK):
                    n = f"h1{'ab'[m]}.{g}"
                    o = s.filled(n)
                    evac(h1T[:, m, :], o[:, :], n, ACT.Gelu, bias=prm("fg_b1", m, 1))
                p["rows"]()
                s.drained(f"logit.{g}")
                s.wait("gate_ready", 2 * g + 1)
                done(act.activation(gw[:, 1, :, :], gw[:, 0, :, :], ACT.Exp), "exp_ready")
                for j in range(4):
                    p["project", j]()
                x["routing"]()
                p["project", 4]()
                s.wait("mix_ready", g + 1)
                done(act.activation(osq, om, ACT.Square), "osq_ready")
                p["project", 5]()
                for j in range(3):
                    p["silu", j]()
                for c in range(CK):
                    n = f"oT{c}.{g}"
                    o = s.filled(n)
                    evac(h1T[:, c, :], o[:, :], n)
                for j in range(3, 5):
                    p["silu", j]()
                p["stat"]()
                p["silu", 5]()

            pipeline(act, prep, main, cross)
            act.wait_ge(drained[bank_of["route.1"]], B * fills_per_batch[bank_of["route.1"]] + 1)
            act.activation(coef[:, :, :], route[:, :, :], ACT.Sigmoid).then_inc(sem("route_scores"), 1)
            with act.Fori(0, B) as b:
                for g in range(G):
                    for e in range(ES):
                        k = b * (G * ES) + g * ES + e
                        act.wait_ge(sem("ff_gate"), k + 1)
                        act.wait_ge(sem("ff_h_ready"), k if (g or e > 1) else b * (G * ES) + 1)
                        act.activation(fg[e % 2], banks[e % 2][:, :], ACT.Silu).then_inc(sem("ff_silu"), 1)

        @block.gpsimd
        def _(pool):
            n_setup = [0]

            def once(ins):
                n_setup[0] += 1
                ins.then_inc(setup_pool, 1)
                pool.wait_ge(setup_pool, n_setup[0])

            once(pool.memset(minus_half[:, :], -0.5))
            once(pool.memset(eps[:, 0, :], 1e-5))
            once(pool.memset(eps[:, 1, :], 1e-12))
            once(pool.memset(Tf[:, :, :], 0.0))
            once(pool.memset(Rf[:, :, :], 0.0))
            once(pool.memset(pre[:, :, :], 0.0))
            once(pool.memset(vT[:, :, :], 0.0))
            once(pool.memset(Va[:, :, :], 0.0))
            once(pool.memset(UW[:, :, :], 0.0))
            once(pool.memset(Va[0:64, :, 32:33], 1.0))
            once(pool.memset(Va[64:128, :, 33:34], 1.0))
            once(pool.memset(aug[:, :], 0.0))
            once(pool.memset(MT[:, :, :, :], 0.0))
            once(pool.memset(S[:, :, :, :], 0.0))
            assert n_setup[0] == N_POOL_SETUP
            for k in range(8):
                pool.sem_inc(drained[k], 1)
            for n in ("ff_h_ready", "ff_y", "ff_y_used"):
                pool.sem_inc(sem(n), 1)
            for n in PRIMED:
                pool.sem_inc(sem(n), PRIMED[n])
            pool.wait_ge(setup_dve, N_DVE_SETUP)
            own_p, own_x = Steps(pool, "pool_prep_step", (2, 2)), Steps(pool, "pool_cross_step", (2, 2))

            def norm_scale(s, chain, i, tag, k):
                s.wait(f"{tag}_stats_ready", k)
                chain.link(pool.tensor_tensor(rstd[i][:, :], mv[i][:, :, 1], eps[:, 0, 0:T], ALU.add))
                done(pool.tensor_tensor(rstd[i][:, :], rstd[i][:, :], minus_half[:, 0:T], ALU.pow),
                     f"{tag}_rstd_ready")

            def cross(b, g):
                s = Signals(pool, b)
                own_x.at(b, g)

                def norm2():
                    norm_scale(s, own_x, 1, "x", 2 * g + 1)

                def norm3():
                    norm_scale(s, own_x, 1, "x", 2 * g + 2)
                    own_x.end()

                return {"norm2": norm2, "norm3": norm3}

            def prep(b, g):
                s = Signals(pool, b)
                own_p.at(b, g)

                def norm1():
                    norm_scale(s, own_p, 0, "hs", g + 1)

                def squares():
                    for j in range(4):
                        s.wait("act_ready", 6 * g + j + 1)
                        done(pool.tensor_tensor(sq[:, 2 * (j % 2) + j // 2, :], kq[:, j % 2, j // 2, :],
                                                kq[:, j % 2, j // 2, :], ALU.mult), "squares_ready")

                def rnorm():
                    s.drained(f"stat.{g}")
                    own_p.link(pool.tensor_tensor(rn[:, :, :], st[:, :, 0:8],
                                                  eps[:, 1, 0:8].unsqueeze(1).broadcast_to([P, T, 8]), ALU.add))
                    done(pool.tensor_tensor(rn[:, :, 4:8], rn[:, :, 4:8],
                                            minus_half[:, 0:4].unsqueeze(1).broadcast_to([P, T, 4]), ALU.pow),
                         "rnorm_ready")
                    own_p.end()

                return {"norm1": norm1, "squares": squares, "rnorm": rnorm}

            def main(b, g, x, p):
                s = Signals(pool, b)
                x["norm2"]()
                for t in range(T):
                    for r in range(2):
                        s.drained(f"gram{t}{r}.{g}")
                    done(pool.tensor_tensor(Bl[:, 0, t * H:(t + 1) * H, :], A[:, t * H:(t + 1) * H, :],
                                            cst("level1").unsqueeze(1).broadcast_to([P, H, P]), ALU.mult),
                         "level1_ready")
                for i, size in enumerate(LEVELS[1:], 1):
                    if i == 2:
                        done(pool.tensor_tensor(rn[:, :, 0:4], rn[:, :, 0:4],
                                                minus_half[:, 0:4].unsqueeze(1).broadcast_to([P, T, 4]), ALU.pow),
                             "rnorm_ready")
                    if i >= 2:
                        s.filled(f"P{LEVELS[i - 2]}{'b' if LEVELS[i - 2] > 16 else ''}.{g}")
                    done(pool.tensor_tensor(Bl[:, i % 2, :, :], A[:, :, :],
                                            cst(f"level{size}").unsqueeze(1).broadcast_to([P, HT, P]),
                                            ALU.mult), "level_ready")
                s.wait("scales_ready", g + 1)
                for t in range(T):
                    s.drained(f"kv{t}.{g}")
                    hh = slice(t * H, (t + 1) * H)
                    ins = pool.tensor_tensor(Y[:, hh, 0:64], kvt[:, t, 256:512].rearrange("p (h c) -> p h c", h=H),
                                          rb[:, t, :].unsqueeze(2).broadcast_to([P, H, DH]), ALU.mult)
                    done(ins, "rows_ready")
                    ins = pool.tensor_tensor(Y[:, hh, 64:128], kvt[:, t, 0:256].rearrange("p (h c) -> p h c", h=H),
                                          sc[:, t, :].unsqueeze(2).broadcast_to([P, H, DH]), ALU.mult)
                    done(ins, "rows_ready")
                s.wait("fir_begun", 2 * g + 2)
                for i in range(N_TAPS):
                    s.wait("tap_ready", N_TAPS * g + i + 1)
                    if i >= CK:
                        s.wait("tap_added", N_TAPS * g + i - 1)
                    done(pool.tensor_tensor(lng[:, i % CK, :], lng[:, i % CK, :], taps[:, i % 4, :], ALU.add),
                         "tap_added")
                s.wait("tap_added", N_TAPS * (g + 1))
                s.drained(f"uw0.{g}")
                for a in range(2):
                    rr, cc = slice(64 * a + 32, 64 * a + 64), slice(64 * a, 64 * a + 32)
                    zero = cst("upper", rr)[:, cc].unsqueeze(1).broadcast_to([32, HT, 32])
                    done(pool.tensor_tensor(Tf[rr, :, cc], zero, zero, ALU.mult), "blocks_cleared")
                    s.wait("blocks_cleared", 2 * g + a + 1)
                x["norm3"]()
                p["norm1"]()
                s.wait("oms_ready", g + 1)
                done(pool.tensor_tensor(orn[:, :], oss[:, :], minus_half[:, 0:HT], ALU.pow), "orms_ready")
                p["squares"]()
                p["rnorm"]()

            pipeline(pool, prep, main, cross)

        @block.vector
        def _(dve):
            V = dve
            dve.wait_ge(tables_loaded, 16 * 2)
            n_setup = [0]

            def once(ins):
                n_setup[0] += 1
                ins.then_inc(setup_dve, 1)
                dve.wait_ge(setup_dve, n_setup[0])

            once(V.tensor_copy(ident_b[:, :], cst("ident")))
            once(V.tensor_copy(ones_b[:, :], cst("ones")))
            once(V.tensor_copy(aug_lhs[0:S2, :, :].rearrange("p j (a k) -> p (j a) k", a=2),
                               cst("eye64", slice(0, S2)).unsqueeze(1).broadcast_to([S2, XH, S2])))
            once(V.memset(aug_lhs[64:128, :, :], 0.0))
            once(V.tensor_copy(aug_lhs[64:112, :, :].rearrange("p j (a k) -> p (j a) k", a=2),
                               cst("eye64", slice(64, 112))[:, 0:XH].unsqueeze(2).broadcast_to([48, XH, S2])))
            for part in (1, 2):
                once(V.tensor_tensor(aug_lhs[64:112, :, :].rearrange("p j (a k) -> p (j a) k", a=2),
                                     aug_lhs[64:112, :, :].rearrange("p j (a k) -> p (j a) k", a=2),
                                     cst("eye64", slice(64, 112))[:, part * XH:(part + 1) * XH].unsqueeze(2)
                                     .broadcast_to([48, XH, S2]), ALU.add))
            once(V.scalar_tensor_tensor(rtemp[:, 0:1], prm("temp"), -1.0, prm("temp"), ALU.mult, ALU.max))
            dve.wait_ge(w_loaded, 16 * 3)
            for c in range(CK):
                n0 = WEIGHT["o"][0] + c * D
                once(V.tensor_scalar(wt[:, n0:n0 + D], wt[:, n0:n0 + D], prm("onorm"), None, ALU.mult))
            once(V.tensor_scalar(sub01[:, :, :], subi, 0.0, None, ALU.not_equal))
            once(V.tensor_scalar(subT01[:, :], subTi, 0.0, None, ALU.not_equal))
            assert n_setup[0] == N_DVE_SETUP, n_setup
            head, own, own_x = Steps(dve, "dve_head_step", (2,)), Steps(dve, "dve_step", DVE_MAIN), \
                Steps(dve, "dve_cross_step", DVE_CROSS)
            own_p = Steps(dve, "dve_prep_step", DVE_PREP)
            head.at(0, 0)
            dve.wait_ge(sem("temp_ln"), 1)
            head.link(V.scalar_tensor_tensor(rtemp[:, 3:4], prm("temp"), 0.0, rtemp[:, 2:3], ALU.max, ALU.add))
            head.link(V.tensor_scalar(rtemp[:, 4:5], rtemp[:, 3:4], 1e-4, None, ALU.add))
            V.reciprocal(rtemp[:, 5:6], rtemp[:, 4:5]).then_inc(sem("temp_ready"), 1)
            dve.wait_ge(sem("temp_ready"), 1)

            def norm_stats(chain, i, rows, tag):
                for t in range(T):
                    last = chain.step(V.bn_stats(stats[i][:, t, :], rows[:, t, :]))
                chain.after(last)
                V.memset(spare[:, :], 0.0)
                for t in range(T):
                    last = V.bn_aggr(mv[i][:, t, :], stats[i][:, t, :])
                done(last, f"{tag}_stats_ready")

            def norm_rows(s, i, rows, tag, k):
                s.wait(f"{tag}_rstd_ready", k)
                for t in range(T):
                    last = V.tensor_scalar(xn[i][:, t, :], rows[:, t, :], mv[i][:, t, 0:1], rstd[i][:, t:t + 1],
                                           ALU.subtract, ALU.mult)
                done(last, f"{tag}_rows_ready")

            def cross(b, g):
                s = Signals(dve, b)
                step, after, link = own_x.step, own_x.after, own_x.link
                own_x.at(b, g)
                rows = xt[:, g, :, :]

                def masks():
                    if g == 0:
                        s.wait("ctx_loaded", 48)
                        step(V.tensor_scalar(pr01[:, :], padr[:, :], 0.0, None, ALU.not_equal))
                        link(V.tensor_scalar(pc01[:, :], padc[:, :], 0.0, None, ALU.not_equal))
                        link(V.tensor_tensor(mbf[:, :, :], sub01[:, :, :],
                                             pr01[:, :].unsqueeze(1).broadcast_to([P, L // P, S2]), ALU.mult))
                        step(V.tensor_scalar(mb[:, :, :], mbf[:, :, :], -1.0, -NEG, ALU.add, ALU.mult))
                    link(V.tensor_scalar(mT[:, :], subT01[:, g * GT:(g + 1) * GT], pc01[:, 0:1], None, ALU.mult))
                    done(V.tensor_scalar(aug[0:S2, :], mT[:, :], -1.0, -NEG, ALU.add, ALU.mult), "mask_ready")
                    s.drained(f"oproj0.{g}")
                    s.drained(f"oproj1.{g}")
                    norm_stats(own_x, 1, rows, "x")

                def rows2():
                    norm_rows(s, 1, rows, "x", 2 * g + 1)

                def anykey():
                    n = f"any.{g}"
                    o = s.filled(n)
                    free(V.tensor_scalar(abc[:, :], o[:, :], 1.0, XD ** -0.5, ALU.min, ALU.mult), n)

                def queries():
                    s.drained(f"any.{g}")
                    for m in range(CK):
                        n = f"qx{m}.{g}"
                        o = s.filled(n)
                        free(V.scalar_tensor_tensor(qx[:, m, :], o[:, :], prm("bq", m, 1), abc[:, :],
                                                    ALU.add, ALU.mult), n)

                def context():
                    if g:
                        return
                    n = f"vx.{g}"
                    o = s.filled(n)
                    for r in range(2):
                        rr = slice(64 * r, 64 * r + 64)
                        vv = o[rr, 0:D].rearrange("p (j r c) -> p j r c", r=2, c=XD)[:, :, r, :]
                        bb = prm("bv")[rr, :].rearrange("p (j r c) -> p j r c", r=2, c=XD)[:, :, r, :]
                        last = V.tensor_tensor(Va[rr, 0:NPAIR, XD * r:XD * (r + 1)], vv, bb, ALU.add)
                    free(last, n)
                    s.drained(f"kx.{g}")
                    for c in range(CK):
                        last = V.tensor_tensor(Kblk[:, c, :, :], kxT[:, c, :].unsqueeze(1).broadcast_to([P, 8, S2]),
                                               cst("head16").unsqueeze(2).broadcast_to([P, 8, S2]), ALU.mult)
                    done(last, "kblk_ready")

                def maxima(t):
                    def piece():
                        for c in range(CK):
                            n = f"sx{t}{c}.{g}"
                            o = s.filled(n)
                            free(V.tensor_reduce(nmx[:, 0, t, 8 * c:8 * c + 8],
                                                 o[:, :].rearrange("p (h k) -> p h k", h=8),
                                                 AX.X, ALU.max, negate=True), n)
                    return piece

                def parts():
                    s.drained(f"sx30.{g}")
                    s.drained(f"sx31.{g}")
                    link(V.tensor_copy(nmb[:, :, 0:16], nmx[:, 0, :, :]))
                    link(V.tensor_tensor(nmx[:, 1, :, :], nmx[:, 0, :, :], nmb[:, :, 0:16], ALU.subtract))
                    link(V.tensor_copy(nmb[:, :, 16:32], nmx[:, 1, :, :]))
                    link(V.tensor_tensor(nmx[:, 0, :, :], nmx[:, 1, :, :], nmb[:, :, 16:32], ALU.subtract))
                    done(V.tensor_copy(nmb[:, :, 32:48], nmx[:, 0, :, :]), "nmx_ready")
                    n = f"mxT.{g}"
                    o = s.filled(n)
                    free(V.tensor_copy(aug[64:112, :], o[64:112, :]), n)

                def values(u):
                    def piece():
                        for t in (2 * u, 2 * u + 1):
                            n = f"pv{t}.{g}"
                            o = s.filled(n)
                            ov = o[:, 0:NPAIR * 34].rearrange("p (j c) -> p j c", c=34)
                            link(V.reciprocal(rden[:, t, :, :], ov[:, :, 32:34]))
                            free(V.tensor_tensor(xo[:, :].rearrange("p (j r c) -> p j r c", r=2, c=XD),
                                                 ov[:, :, 0:32].rearrange("p j (r c) -> p j r c", r=2),
                                                 rden[:, t, :, :].unsqueeze(3).broadcast_to([P, NPAIR, 2, XD]),
                                                 ALU.mult), n)
                            s.drained(n)
                            ins = V.tensor_tensor(rows[:, t, :], rows[:, t, :], xo[:, :], ALU.add)
                            if t < T - 1:
                                link(ins)
                            else:
                                done(ins, "x2_ready")
                        if u:
                            s.wait("x2_ready", g + 1)
                            norm_stats(own_x, 1, rows, "x")
                    return piece

                def rows3():
                    norm_rows(s, 1, rows, "x", 2 * g + 2)

                def routing():
                    n = f"route.{g}"
                    o = s.filled(n)
                    rv = route[:, :, :].rearrange("p (b t) e -> p b t e", b=B)
                    free(V.tensor_tensor(rv[:, b, g * T:(g + 1) * T, :],
                                         o[:, 0:T * E].rearrange("p (t e) -> p t e", t=T),
                                         prm("lb").unsqueeze(1).broadcast_to([P, T, E]), ALU.add), n)
                    own_x.end()

                x = {"masks": masks, "rows2": rows2, "context": context, "anykey": anykey, "queries": queries}
                for t in range(T):
                    x["maxima", t] = maxima(t)
                x.update({"parts": parts, ("values", 0): values(0), ("values", 1): values(1),
                          "rows3": rows3, "routing": routing})
                return x

            def prep(b, g):
                s = Signals(dve, b)
                step, after, link = own_p.step, own_p.after, own_p.link
                own_p.at(b, g)
                rows = xt[:, g, :, :]

                def first():
                    if g:
                        link(V.tensor_copy(pre[:, :, 0:CONV - 1], pre[:, :, GT:GT + CONV - 1]))
                        link(V.tensor_copy(vT[:, :, 0:HALO], vT[:, :, GT:GT + HALO]))
                    else:
                        link(V.memset(pre[:, :, 0:CONV - 1], 0.0))
                        link(V.memset(vT[:, :, 0:HALO], 0.0))
                    s.wait(f"x{g}_loaded", 16)
                    norm_stats(own_p, 0, rows, "hs")

                def rows1():
                    norm_rows(s, 0, rows, "hs", g + 1)

                def conv(j):
                    def piece():
                        s.drained(f"proj{j}.{g}")
                        if j >= 2:
                            s.wait("act_ready", 6 * g + j - 1)
                        cw = lambda i: param[:, PARAM["conv"][0] + j * CONV + i:PARAM["conv"][0] + j * CONV + i + 1]
                        link(V.tensor_scalar(cv[:, j % 2, :], pre[:, j, 0:GT], cw(0), None, ALU.mult))
                        for i in range(1, CONV):
                            ins = V.scalar_tensor_tensor(cv[:, j % 2, :], pre[:, j, i:i + GT], cw(i),
                                                         cv[:, j % 2, :], ALU.mult, ALU.add)
                            if i < CONV - 1:
                                link(ins)
                        done(ins, "conv_ready")
                        if j == 5:
                            own_p.end()
                    return piece

                p = {"stats": first, "rows": rows1}
                for j in range(6):
                    p["conv", j] = conv(j)
                return p

            def main(b, g, x, p):
                s = Signals(dve, b)
                step, after, link = own.step, own.after, own.link
                own.at(b, g)
                rows = xt[:, g, :, :]
                fir_k = {}

                def fir(g, lo, hi):
                    for j in range(lo, hi):
                        for c in range(CK):
                            w_ = param[:, PARAM["fir_l"][0] + c * FL + j:PARAM["fir_l"][0] + c * FL + j + 1]
                            src = vT[:, c, j:j + GT]
                            if j == 0:
                                k = step(V.tensor_scalar(lng[:, c, :], src, w_, None, ALU.mult))
                            else:
                                after(fir_k[c])
                                ins = V.scalar_tensor_tensor(lng[:, c, :], src, w_, lng[:, c, :], ALU.mult, ALU.add)
                                if j == TAPS - 1:
                                    done(ins, "fir_begun")
                                    continue
                                k = step(ins)
                            fir_k[c] = k

                def fir_short(g):
                    for j in range(FS):
                        for c in range(CK):
                            w_ = param[:, PARAM["fir_s"][0] + c * FS + j:PARAM["fir_s"][0] + c * FS + j + 1]
                            src = vT[:, c, FL - FS + j:FL - FS + j + GT]
                            if j == 0:
                                fir_k["s", c] = step(V.tensor_scalar(sht[:, c, :], src, w_, None, ALU.mult))
                            else:
                                after(fir_k["s", c])
                                ins = V.scalar_tensor_tensor(sht[:, c, :], src, w_, sht[:, c, :], ALU.mult, ALU.add)
                                if j < FS - 1:
                                    fir_k["s", c] = step(ins)
                                else:
                                    done(ins, "fir_done")

                x["masks"]()
                s.wait("act_ready", 6 * g + 6)
                s.drained(f"stat.{g}")
                link(V.tensor_scalar(beta[:, :, :], st[:, :, 8:12], 1.0, 0.5, ALU.add, ALU.mult))
                s.wait("rnorm_ready", 2 * g + 1)
                link(V.tensor_tensor(rb[:, :, :], beta[:, :, :], rn[:, :, 4:8], ALU.mult))
                done(V.tensor_tensor(sc[:, :, :], rb[:, :, :], rn[:, :, 4:8], ALU.mult), "scales_ready")
                s.wait("scales_ready", g + 1)
                for t in range(T):
                    for r in range(2):
                        n = f"gram{t}{r}.{g}"
                        o = s.filled(n)
                        ov = o[:, :].rearrange("p (i a c) -> p i a c", i=2, a=2)
                        for i in range(2):
                            h = t * H + 2 * i + r
                            V.scalar_tensor_tensor(A[:, h, :], ov[:, i, 0, :], sc[:, t, 2 * i + r:2 * i + r + 1],
                                                   cst("lower"), ALU.mult, ALU.mult)
                        free(V.tensor_tensor(attnT[:, t * H + r:(t + 1) * H:2, :], ov[:, :, 1, :],
                                             cst("upper").unsqueeze(1).broadcast_to([P, 2, P]), ALU.mult), n)
                x["rows2"]()
                fir(g, 0, 1)
                n = f"P1.{g}"
                o = s.filled(n)
                free(V.tensor_tensor(Rc[:, :, :], cst("eye32").unsqueeze(1).broadcast_to([P, HT, 32]),
                                     o[:, :].rearrange("p (h k) -> p h k", k=32), ALU.subtract), n)
                s.drained(n)
                done(V.transpose(Tc[:, :, :].rearrange("p h k -> p (h k)"),
                                 Rc[:, :, :].rearrange("p h k -> p (h k)")), "compact_ready")
                fir(g, 1, 3)
                x["context"]()
                x["anykey"]()
                for i, size in enumerate(LEVELS[1:5]):
                    if i == 0:
                        fir(g, 3, 6)
                        x["queries"]()
                    else:
                        fir(g, (2, 6, 11, 16)[i], (0, 11, 16, TAPS)[i])
                    n = f"D{size}.{g}"
                    o = s.filled(n)
                    free(V.tensor_tensor(Rc[:, :, :], Rc[:, :, :],
                                         o[:, :].rearrange("p (h k) -> p h k", k=32), ALU.subtract), n)
                    s.drained(n)
                    s.wait("blocks_ready", 5 * g + i + 1)
                    done(V.transpose(Tc[:, :, :].rearrange("p h k -> p (h k)"),
                                     Rc[:, :, :].rearrange("p h k -> p (h k)")), "compact_ready")
                    if i == 3:
                        s.wait("compact_ready", 5 * g + 5)
                        for r in range(4):
                            rr = slice(32 * r, 32 * r + 32)
                            last = V.tensor_copy(Tf[rr, :, rr], Tc[rr, :, :])
                        done(last, "inverse_ready")
                    if i:
                        x["maxima", i - 1]()
                x["maxima", 3]()
                x["parts"]()
                view = lambda M, h0: M[:, h0:h0 + 8, :].rearrange("p h (a c) -> p h a c", a=2)
                for x_, h0 in (("a", 0), ("b", 8)):
                    n = f"R32{x_}.{g}"
                    o = s.filled(n)
                    for a in range(2):
                        rr = slice(64 * a, 64 * a + 32)
                        last = V.tensor_scalar(Rf[rr, h0:h0 + 8, 64 * a + 32:64 * a + 64],
                                               o[rr, :].rearrange("p (h a c) -> p h a c", h=8, a=2)[:, :, a, :],
                                               -1.0, None, ALU.mult)
                    free(last, n)
                for x_, h0 in (("a", 0), ("b", 8)):
                    n = f"T32{x_}.{g}"
                    o = s.filled(n)
                    for a in range(2):
                        rr = slice(64 * a + 32, 64 * a + 64)
                        last = V.tensor_scalar(Tf[rr, h0:h0 + 8, 64 * a:64 * a + 32],
                                               o[rr, :].rearrange("p (h a c) -> p h a c", h=8, a=2)[:, :, a, :],
                                               -1.0, None, ALU.mult)
                    free(last, n)
                for x_, h0 in (("a", 0), ("b", 8)):
                    n = f"R64{x_}.{g}"
                    o = s.filled(n)
                    free(V.tensor_scalar(Rf[0:64, h0:h0 + 8, 64:128], o[0:64, :].rearrange("p (h c) -> p h c", h=8),
                                         -1.0, None, ALU.mult), n)
                    if x_ == "a":
                        x["values", 0]()
                fir_short(g)
                for t in range(T):
                    n = f"wa{t}.{g}"
                    o = s.filled(n)
                    V.tensor_tensor(QeT[:, :, t * P:(t + 1) * P], kq[:, :, 1, t * P:(t + 1) * P],
                                    o[:, 0:256].rearrange("p (i c) -> p i c", i=2), ALU.subtract)
                    for r in range(2):
                        rr = slice(DH * r, DH * r + DH)
                        last = V.tensor_tensor(MT[rr, t, :, rr],
                                               cst("eye64", rr).unsqueeze(1).broadcast_to([DH, 2, DH]),
                                               o[rr, 256:384].rearrange("p (i c) -> p i c", i=2), ALU.subtract)
                    free(last, n)
                x["values", 1]()
                s.wait("rnorm_ready", 2 * g + 2)
                for t in range(T):
                    n = f"out{t}.{g}"
                    o = s.filled(n)
                    free(V.tensor_tensor(delta[:, t, :].rearrange("p (h c) -> p h c", h=H),
                                         o[:, 0:D].rearrange("p (h c) -> p h c", h=H),
                                         rn[:, t, 0:4].unsqueeze(2).broadcast_to([P, H, DH]), ALU.mult), n)
                    s.drained(n)
                    done(V.tensor_reduce(dm[:, t, :], delta[:, t, :].rearrange("p (h c) -> p c h", h=H),
                                         AX.X, ALU.add), "delta_ready")
                    if t == 0:
                        x["rows3"]()
                p["stats"]()
                p["rows"]()
                n = f"logit.{g}"
                o = s.filled(n)
                free(V.tensor_tensor(gw[:, 2, :, :], o[:, 0:T * 4].rearrange("p (t k) -> p t k", t=T),
                                     prm("fg_b2").unsqueeze(1).broadcast_to([P, T, 4]), ALU.add), n)
                s.drained(n)
                link(V.tensor_scalar(gw[:, 3, :, :], gw[:, 2, :, :], rtemp[:, 5:6], None, ALU.mult))
                link(V.tensor_reduce(gs[:, 0, :], gw[:, 3, :, :], AX.X, ALU.max))
                done(V.tensor_tensor(gw[:, 0, :, :], gw[:, 3, :, :],
                                     gs[:, 0, :].unsqueeze(2).broadcast_to([P, T, 4]), ALU.subtract), "gate_ready")
                p["conv", 0]()
                s.wait("exp_ready", g + 1)
                link(V.tensor_reduce(gs[:, 1, :], gw[:, 1, :, :], AX.X, ALU.add))
                link(V.reciprocal(gs[:, 2, :], gs[:, 1, :]))
                link(V.tensor_tensor(gw[:, 4, :, :], gw[:, 1, :, :],
                                     gs[:, 2, :].unsqueeze(2).broadcast_to([P, T, 4]), ALU.mult))
                link(V.tensor_scalar(gs[:, 3, :], gw[:, 4, :, 3], MIN_LOCAL, None, ALU.mult))
                step(V.tensor_copy(gw[:, 5, :, 2:4], gw[:, 4, :, 2:4]))
                link(V.tensor_tensor(gw[:, 5, :, 0:2], gw[:, 4, :, 0:2],
                                     gs[:, 3, :].unsqueeze(2).broadcast_to([P, T, 2]), ALU.max))
                link(V.tensor_reduce(gs[:, 1, :], gw[:, 5, :, :], AX.X, ALU.add))
                link(V.reciprocal(gs[:, 2, :], gs[:, 1, :]))
                done(V.tensor_tensor(gw[:, 6, :, :], gw[:, 5, :, :],
                                     gs[:, 2, :].unsqueeze(2).broadcast_to([P, T, 4]), ALU.mult), "gate_ready")
                s.wait("gate_ready", 2 * g + 2)
                for t0 in range(0, T, 2):
                    tt = (t0, t0 + 1)
                    ks = {}
                    for t in tt:
                        o = s.filled(f"sl{t}.{g}")
                        ks[t] = step(V.tensor_scalar(om[:, t, :], o[:, 0:256], gw[:, 6, t, 0:1], None, ALU.mult))
                    for t in tt:
                        after(ks[t])
                        n = f"sl{t}.{g}"
                        free(V.scalar_tensor_tensor(om[:, t, :], banks[bank_of[n]][:, 256:512], gw[:, 6, t, 1:2],
                                                    om[:, t, :], ALU.mult, ALU.add), n)
                    for t in tt:
                        s.drained(f"sl{t}.{g}")
                        ks[t] = step(V.scalar_tensor_tensor(om[:, t, :], delta[:, t, :], gw[:, 6, t, 2:3],
                                                            om[:, t, :], ALU.mult, ALU.add))
                    for t in tt:
                        after(ks[t])
                        last = V.scalar_tensor_tensor(om[:, t, :], kvt[:, t, 256:512], gw[:, 6, t, 3:4],
                                                      om[:, t, :], ALU.mult, ALU.add)
                done(last, "mix_ready")
                p["conv", 1]()
                x["routing"]()
                s.wait("osq_ready", g + 1)
                link(V.tensor_reduce(gw[:, 7, :, :].rearrange("p a b -> p (a b)"),
                                     osq.rearrange("p t (h c) -> p (t h) c", h=H), AX.X, ALU.add))
                done(V.tensor_scalar(oss[:, :], gw[:, 7, :, :].rearrange("p a b -> p (a b)"), 1.0 / DH, 1e-5,
                                     ALU.mult, ALU.add), "oms_ready")
                p["conv", 2]()
                s.wait("orms_ready", g + 1)
                omv = om[:, :, :].rearrange("p t (h c) -> p (t h) c", h=H)
                done(V.tensor_tensor(omv, omv, orn[:, :].unsqueeze(2).broadcast_to([P, HT, DH]), ALU.mult),
                     "on_ready")
                p["conv", 3]()
                p["conv", 4]()
                p["conv", 5]()
                for i in range(2):
                    n = f"oproj{i}.{g}"
                    o = s.filled(n)
                    dst = rows[:, 2 * i:2 * i + 2, :]
                    free(V.tensor_tensor(dst, dst, o[:, :].rearrange("p (t d) -> p t d", t=2), ALU.add), n)
                own.end()

            pipeline(dve, prep, main, cross)
            NT = B * G * T
            route_chain = Steps(dve, "route_step", (12,))
            route_chain.at(0, 0)
            tlink = route_chain.link

            dve.wait_ge(drained[bank_of["route.1"]], B * fills_per_batch[bank_of["route.1"]] + 1)
            dve.wait_ge(sem("route_scores"), 1)
            cmp = kq[:, :, :, :].rearrange("p a b c -> p (a b c)").rearrange("p (t e f) -> p t e f", t=NT, e=E)
            eqv = attnT[:, :, :].rearrange("p a b -> p (a b)").rearrange("p (t e f) -> p t e f", t=NT, e=E)
            ce = coef[:, :, :].unsqueeze(3).broadcast_to([P, NT, E, E])
            cf = coef[:, :, :].unsqueeze(2).broadcast_to([P, NT, E, E])
            tlink(V.tensor_tensor(cmp, cf, ce, ALU.is_gt))
            tlink(V.tensor_tensor(eqv, cf, ce, ALU.is_equal))
            tlink(V.tensor_tensor(eqv.rearrange("p t e f -> p t (e f)"), eqv.rearrange("p t e f -> p t (e f)"),
                                  cst("before").unsqueeze(1).broadcast_to([P, NT, E * E]), ALU.mult))
            tlink(V.tensor_tensor(cmp, cmp, eqv, ALU.add))
            rank = xo[:, :].rearrange("p (t e) -> p t e", t=NT)
            sel = hsT[:, 0, 0:NT * E].rearrange("p (t e) -> p t e", t=NT)
            selw = hsT[:, 1, 0:NT * E].rearrange("p (t e) -> p t e", t=NT)
            den = hsT[:, 0, NT * E:NT * E + NT]
            tlink(V.tensor_reduce(rank, cmp, AX.X, ALU.add))
            tlink(V.tensor_scalar(sel, rank, 2.0, None, ALU.is_lt))
            tlink(V.tensor_tensor(selw, sel, coef[:, :, :], ALU.mult))
            tlink(V.tensor_reduce(den, selw, AX.X, ALU.add))
            tlink(V.tensor_scalar(hsT[:, 1, NT * E:NT * E + NT], den, 1e-8, None, ALU.add))
            tlink(V.reciprocal(hsT[:, 0, NT * E + NT:NT * E + 2 * NT], hsT[:, 1, NT * E:NT * E + NT]))
            tlink(V.tensor_tensor(selw, selw, hsT[:, 0, NT * E + NT:NT * E + 2 * NT].unsqueeze(2).broadcast_to([P, NT, E]),
                                  ALU.mult))
            sums = gw[:, 0, :, :].rearrange("p t k -> p (t k)")
            tlink(V.tensor_reduce(sums[:, 0:E], selw.rearrange("p t e -> p e t"), AX.X, ALU.add))
            V.tensor_reduce(sums[:, E:2 * E], sel.rearrange("p t e -> p e t"), AX.X, ALU.add)\
                .then_inc(sem("route_sums"), 1)
            dve.wait_ge(sem("route_total"), 1)
            tot = gw[:, 1, :, :].rearrange("p t k -> p (t k)")
            tlink(V.tensor_scalar(tot[:, 0:E], banks[0][:, E:2 * E], 1.0, None, ALU.max))
            tlink(V.reciprocal(tot[:, E:2 * E], tot[:, 0:E]))
            wm = gw[:, 2, :, :].rearrange("p t k -> p (t k)")
            tlink(V.tensor_tensor(wm[:, 0:E], banks[0][:, 0:E], tot[:, E:2 * E], ALU.mult))
            V.tensor_tensor(coef[:, :, :], sel, wm[:, 0:E].unsqueeze(1).broadcast_to([P, NT, E]), ALU.mult)\
                .then_inc(sem("coef_ready"), 1)
            dve.wait_ge(sem("coef_ready"), 1)
            with dve.Fori(0, B) as b:
                cv_ = coef[:, :, :].rearrange("p (b t) e -> p b t e", b=B)
                for g in range(G):
                    acc = facc[g]
                    dve.wait_ge(sem(f"fx{g}_loaded"), b * 32 + 32)

                    def product(e):
                        k = b * (G * ES) + g * ES + e
                        dve.wait_ge(sem("ff_silu"), k + 1)
                        dve.wait_ge(sem("ff_up"), k + 1)
                        kd = b * (G * 9) + g * 9
                        dve.wait_ge(sem("ff_y"), kd + (e if e >= 2 else 1))
                        V.tensor_tensor(fh[e % 2], banks[2 + e % 2][:, :], fg[e % 2], ALU.mult)\
                            .then_inc(sem("ff_h_ready"), 1)

                    def gather(slot):
                        k = b * (G * 9) + g * 9 + slot
                        dve.wait_ge(sem("ff_y"), k + 2)
                        if slot:
                            dve.wait_ge(sem("ff_y_used"), k + 1)
                        for i in range(2):
                            o = banks[4 + 2 * ((g * 9 + slot) % 2) + i]
                            if slot == E:
                                last = V.tensor_tensor(acc[:, 2 * i:2 * i + 2, :], acc[:, 2 * i:2 * i + 2, :],
                                                       o[:, :].rearrange("p (t d) -> p t d", t=2), ALU.add)
                            else:
                                for j in range(2):
                                    t = 2 * i + j
                                    last = V.scalar_tensor_tensor(acc[:, t, :], o[:, j * D:(j + 1) * D],
                                                                  cv_[:, b, g * T + t, slot:slot + 1], acc[:, t, :],
                                                                  ALU.mult, ALU.add)
                        last.then_inc(sem("ff_y_used"), 1)

                    product(0)
                    for e in range(1, ES):
                        product(e)
                        if e - 1 < E:
                            gather(e - 1)
                    gather(E)

        wrong = {n: (SIGNALS.get(n), c) for n, c in counted.items() if 2 * SIGNALS.get(n, 0) != c}
        assert not wrong, wrong




def constants():
    c = np.zeros((P, NCONST), np.float32)
    p, q = np.arange(P)[:, None], np.arange(P)[None, :]

    def put(name, v):
        a, z = CONST[name]
        c[:, a:z] = v

    put("ident", p == q)
    put("lower", q < p)
    put("upper", p <= q)
    for s in LEVELS:
        put(f"level{s}", (p // (2 * s) == q // (2 * s)) & (p // s % 2 == 1) & (q // s % 2 == 0))
    put("eye64", p % DH == q[:, :DH])
    put("headsel", p // DH == q[:, :2])
    put("mean_s", (p % DH == q) / H)
    put("mean_l", (p % DH == q - DH) / H)
    put("ones", 1.0)
    put("head16", p // XD == q[:, :8])
    put("eye32", p % 32 == q[:, :32])
    e, f = np.arange(E)[:, None], np.arange(E)[None, :]
    put("before", (f < e).reshape(1, -1))
    return c


def kernel(**inputs):
    import concourse.bacc as _bacc
    from concourse import mybir as _mybir
    from concourse.bass_utils import run_bass_kernel_spmd as _run

    a = {n: np.asarray(v) for n, v in inputs.items()}
    f = np.float32

    def rows(w):
        wt = np.ascontiguousarray(w.T)
        n = wt.shape[0] // P
        return wt.reshape(n, P, -1).transpose(1, 0, 2).reshape(P, -1)

    def cols(v):
        v = v.reshape(CK, P, -1)
        return v.transpose(1, 0, 2).reshape(P, -1)

    def spread(v):
        return np.broadcast_to(v.reshape(1, -1), (P, v.size))

    pre = "L0_attn_"
    conv = np.concatenate([cols(a[pre + n + "_conv_w"]) for n in ("k", "q", "v")], axis=1)
    param = np.concatenate([
        conv, cols(a[pre + "fir_short_w"].reshape(D, FS)), cols(a[pre + "fir_long_w"].reshape(D, FL)),
        cols(a[pre + "fg_b1"]), cols(a["L0_xattn_bq"]), cols(a["L0_xattn_bk"]), spread(a["L0_xattn_bv"]),
        spread(a[pre + "fg_b2"]), spread(a["L0_ffn_lb_bias"]), spread(a[pre + "logit_temp"]),
        np.concatenate([a[pre + "o_norm_w"]] * 2).reshape(P, 1)], axis=1)
    w1 = a[pre + "fg_w1"]
    w1p = np.concatenate([w1, np.zeros((D, DH), f)], axis=1)
    weight = np.concatenate([
        rows(a[pre + "k_proj_w"]), rows(a[pre + "q_proj_w"]), rows(a[pre + "v_proj_w"]), rows(a[pre + "b_proj_w"]),
        rows(w1p), rows(a[pre + "fg_w2"]), rows(a[pre + "o_proj_w"]), rows(a["L0_ffn_gate_w"]),
        rows(a["L0_xattn_Wq"]), rows(a["L0_xattn_Wk"]), rows(a["L0_xattn_Wv"])], axis=1)
    ff = "L0_ffn_"
    gates = list(a[ff + "expert_gate_w"]) + list(a[ff + "shared_gate_w"].reshape(2, EI, D))
    ups = list(a[ff + "expert_up_w"]) + list(a[ff + "shared_up_w"].reshape(2, EI, D))
    sd = a[ff + "shared_down_w"]
    downs = list(a[ff + "expert_down_w"]) + [sd[:, :EI], sd[:, EI:]]
    ffn = np.stack([np.concatenate([rows(g), rows(u), rows(d)], axis=1) for g, u, d in zip(gates, ups, downs)], axis=1)
    ctx = a["ctx_1024"].transpose(0, 2, 1).reshape(B, CK, P, S2).transpose(0, 2, 1, 3)
    ctx = np.concatenate([ctx, ctx], axis=3)
    pad = a["mask_Bx1x1xS2_ik0"].reshape(B, S2)
    sub = a["mask_1x1xSxS2_ik0"].reshape(L, S2)
    feeds = {
        "x": a["x"], "ctxT": ctx, "pad_row": np.broadcast_to(pad[:, None, :], (B, P, S2)),
        "pad_col": pad.reshape(B, S2, 1), "sub": sub, "subT": sub.T, "const": constants(),
        "param": param, "weight": weight, "ffn": ffn,
    }
    nc = _bacc.Bacc("TRN2", target_bir_lowering=False, num_devices=1)
    arrays, aps = {}, []
    for n, v in feeds.items():
        v = np.ascontiguousarray(v)
        arrays[n + "_in"] = v
        aps.append(nc.dram_tensor(n + "_in", v.shape, _mybir.dt.from_np(v.dtype), kind="ExternalInput").ap())
    out = nc.dram_tensor("y", (B, L, D), _mybir.dt.float32, kind="ExternalOutput").ap()
    x2 = nc.dram_tensor("x2", (B, G, P, T, D), _mybir.dt.float32, kind="Internal").ap()
    xnT = nc.dram_tensor("xnT", (B, G, P, CK, GT), _mybir.dt.float32, kind="Internal").ap()
    decoder(nc, *aps, out, x2, xnT)
    r = _run(nc, [arrays], core_ids=[0])
    return r.results[0]["y"]
```
